# Optimizing a Trainium2 kernel written in Bass

```python
import numpy as np
import jax
import jax.numpy as jnp

def _softmax(x, axis=-1):
    return jax.nn.softmax(x, axis=axis)
def _gelu(x):
    return jax.nn.gelu(x, approximate=True)
def _silu(x):
    return jax.nn.silu(x)
def _sigmoid(x):
    return jax.nn.sigmoid(x)
def _layernorm(x, axis=-1, eps=1e-5):
    m = jnp.mean(x, axis=axis, keepdims=True)
    v = jnp.var(x, axis=axis, keepdims=True)
    return (x - m) / jnp.sqrt(v + eps)
def _scatter_add(tgt, idx, src, axis=0):
    return tgt.at[idx].add(src)
def _segment_sum(src, seg, n):
    return jax.ops.segment_sum(src, seg, n)

kernel_name = 'mk_adj_ffn_d2_adj_256_ead099'

def setup_inputs(seed: int = 0):
    np.random.seed(seed)
    _w = jnp.asarray
    def _rec_inputs():
        import jax
        import jax.numpy as jnp
        _gk = jax.random.key(seed)
        x = -0.0005207 + 1.001 * jax.random.normal(jax.random.fold_in(_gk, 1), (3327, 256), jnp.float32)
        _a = jax.random.bernoulli(jax.random.fold_in(_gk, 2), 0.00120228, (3327, 3327))
        _a = jnp.logical_or(_a, jnp.swapaxes(_a, -1, -2))
        _a = jnp.logical_or(_a, jnp.eye(3327, dtype=bool))
        adj = _a.astype(jnp.int32)
        return x, adj
    x, adj = _rec_inputs()
    def _L0_gnn_setup():
        import jax, jax.numpy as jnp
        import numpy as np
        N_NODES = 8192
        IN_F = 256
        OUT_F = 256
        ALPHA = 0.2
        key = jax.random.key(seed)
        k1, k2, k3, k4 = jax.random.split(key, 4)
        X = jax.random.normal(k1, (N_NODES, IN_F), dtype=jnp.float32)
        A = jax.random.randint(k2, (N_NODES, N_NODES), 0, 2, dtype=jnp.int32)
        W = jax.random.normal(k3, (OUT_F, IN_F), dtype=jnp.float32) * (1.0 / np.sqrt(IN_F))
        r = jax.random.normal(k4, (2 * OUT_F, 1), dtype=jnp.float32)
        return {'X': X, 'A': A, 'W': W, 'r': r}
    _L0_gnn_all = _L0_gnn_setup()
    _L0_gnn_in = {k: v for k, v in _L0_gnn_all.items() if k in ('W', 'r', )}
    del _L0_gnn_all

    def _L0_ffn_setup():
        import jax, jax.numpy as jnp
        import numpy as np
        B, T, D, H, E = (16, 4096, 256, 512, 8)
        key = jax.random.key(seed)
        ks = jax.random.split(key, 5)
        x = jax.random.normal(ks[0], (B, T, D), dtype=jnp.float32)
        gate_w = jax.random.normal(ks[1], (D, E), dtype=jnp.float32) * 0.02
        gate_b = jnp.zeros((E,), dtype=jnp.float32)
        W1 = jax.random.normal(ks[2], (E, D, H), dtype=jnp.float32) * 0.02
        b1 = jnp.zeros((E, H), dtype=jnp.float32)
        W2 = jax.random.normal(ks[3], (E, H, D), dtype=jnp.float32) * 0.02
        b2 = jnp.zeros((E, D), dtype=jnp.float32)
        return {'x': x, 'gate_w': gate_w, 'gate_b': gate_b, 'W1': W1, 'b1': b1, 'W2': W2, 'b2': b2}
    _L0_ffn_all = _L0_ffn_setup()
    _L0_ffn_in = {k: v for k, v in _L0_ffn_all.items() if k in ('gate_w', 'gate_b', 'W1', 'b1', 'W2', 'b2', )}
    del _L0_ffn_all

    def _L1_gnn_setup():
        import jax, jax.numpy as jnp
        import numpy as np
        N, IN_F, H, D = (4096, 256, 4, 64)
        NEG_SLOPE = 0.2
        key = jax.random.key(seed)
        ks = jax.random.split(key, 8)
        s_w = 1.0 / np.sqrt(H * D)
        s_u = 1.0
        return {'inputs': jax.random.normal(ks[0], (N, IN_F), jnp.float32), 'adj_mat': jax.random.randint(ks[1], (N, N), 0, 2, jnp.int32), 'weight': jax.random.normal(ks[2], (IN_F, H * D), jnp.float32) * s_w, 'weight_u': jax.random.normal(ks[3], (H, D, 1), jnp.float32) * s_u, 'weight_v': jax.random.normal(ks[4], (H, D, 1), jnp.float32) * s_u, 'bias': jax.random.normal(ks[5], (1, H * D), jnp.float32) * s_w, 'proj_w': jax.random.normal(ks[6], (H * D, IN_F), jnp.float32) * (1.0 / np.sqrt(IN_F)), 'proj_b': jax.random.normal(ks[7], (H * D,), jnp.float32) * (1.0 / np.sqrt(IN_F))}
    _L1_gnn_all = _L1_gnn_setup()
    _L1_gnn_in = {k: v for k, v in _L1_gnn_all.items() if k in ('weight', 'weight_u', 'weight_v', 'bias', 'proj_w', 'proj_b', )}
    del _L1_gnn_all

    def _L1_ffn_setup():
        import jax, jax.numpy as jnp
        import numpy as np
        TOP_K = 2
        LN_EPS = 1e-05
        key = jax.random.key(seed)
        ks = jax.random.split(key, 8)
        B, S, D, E, H = (16, 1024, 256, 8, 1024)
        x = jax.random.normal(ks[0], (B, S, D), dtype=jnp.float32)
        Wr = jax.random.normal(ks[1], (D, E), dtype=jnp.float32) * 0.1
        br = jnp.zeros((E,), dtype=jnp.float32)
        ln_g = jnp.ones((E, D), dtype=jnp.float32)
        ln_b = jnp.zeros((E, D), dtype=jnp.float32)
        W1 = jax.random.normal(ks[2], (E, D, H), dtype=jnp.float32) * (1.0 / np.sqrt(D))
        b1 = jnp.zeros((E, H), dtype=jnp.float32)
        W2 = jax.random.normal(ks[3], (E, H, D), dtype=jnp.float32) * (1.0 / np.sqrt(H))
        b2 = jnp.zeros((E, D), dtype=jnp.float32)
        return {'x': x, 'Wr': Wr, 'br': br, 'ln_g': ln_g, 'ln_b': ln_b, 'W1': W1, 'b1': b1, 'W2': W2, 'b2': b2}
    _L1_ffn_all = _L1_ffn_setup()
    _L1_ffn_in = {k: v for k, v in _L1_ffn_all.items() if k in ('Wr', 'br', 'ln_g', 'ln_b', 'W1', 'b1', 'W2', 'b2', )}
    del _L1_ffn_all

    return {
        "x": x,
        "adj": adj,
        "L0_gnn_W": _L0_gnn_in["W"],
        "L0_gnn_r": _L0_gnn_in["r"],
        "L0_ffn_gate_w": _L0_ffn_in["gate_w"],
        "L0_ffn_gate_b": _L0_ffn_in["gate_b"],
        "L0_ffn_W1": _L0_ffn_in["W1"],
        "L0_ffn_b1": _L0_ffn_in["b1"],
        "L0_ffn_W2": _L0_ffn_in["W2"],
        "L0_ffn_b2": _L0_ffn_in["b2"],
        "L1_gnn_weight": _L1_gnn_in["weight"],
        "L1_gnn_weight_u": _L1_gnn_in["weight_u"],
        "L1_gnn_weight_v": _L1_gnn_in["weight_v"],
        "L1_gnn_bias": _L1_gnn_in["bias"],
        "L1_gnn_proj_w": _L1_gnn_in["proj_w"],
        "L1_gnn_proj_b": _L1_gnn_in["proj_b"],
        "L1_ffn_Wr": _L1_ffn_in["Wr"],
        "L1_ffn_br": _L1_ffn_in["br"],
        "L1_ffn_ln_g": _L1_ffn_in["ln_g"],
        "L1_ffn_ln_b": _L1_ffn_in["ln_b"],
        "L1_ffn_W1": _L1_ffn_in["W1"],
        "L1_ffn_b1": _L1_ffn_in["b1"],
        "L1_ffn_W2": _L1_ffn_in["W2"],
        "L1_ffn_b2": _L1_ffn_in["b2"],
    }

def reference(x, adj, L0_gnn_W, L0_gnn_r, L0_ffn_gate_w, L0_ffn_gate_b, L0_ffn_W1, L0_ffn_b1, L0_ffn_W2, L0_ffn_b2, L1_gnn_weight, L1_gnn_weight_u, L1_gnn_weight_v, L1_gnn_bias, L1_gnn_proj_w, L1_gnn_proj_b, L1_ffn_Wr, L1_ffn_br, L1_ffn_ln_g, L1_ffn_ln_b, L1_ffn_W1, L1_ffn_b1, L1_ffn_W2, L1_ffn_b2):
    import jax
    import jax.numpy as jnp
    def _L0_gnn_ref(X, A, W, r):
        import jax, jax.numpy as jnp
        import numpy as np
        N_NODES = 8192
        IN_F = 256
        OUT_F = 256
        ALPHA = 0.2
        Wh = X @ W.T
        F_out = Wh.shape[-1]
        r_src = r[:F_out, 0]
        r_dst = r[F_out:, 0]
        s_i = Wh @ r_src
        s_j = Wh @ r_dst
        e = s_i[:, None] + s_j[None, :]
        e = jnp.where(e >= 0, e, ALPHA * e)
        e = jnp.where(A == 0, -jnp.inf, e)
        attention = jax.nn.softmax(e, axis=1)
        output = attention @ Wh
        return jax.nn.gelu(output, approximate=False)

    def _L0_ffn_ref(x, gate_w, gate_b, W1, b1, W2, b2):
        import jax, jax.numpy as jnp
        import numpy as np
        B, T, D, H, E = (16, 4096, 256, 512, 8)
        Bb, Tt, Dd = x.shape
        Ee = gate_w.shape[1]
        xf = x.reshape(-1, Dd)
        N = xf.shape[0]
        logits = xf @ gate_w + gate_b
        probs = jax.nn.softmax(logits, axis=-1)
        top2_vals, top2_idx = jax.lax.top_k(probs, 2)
        cw = jnp.zeros((N, Ee), dtype=xf.dtype).at[jnp.arange(N)[:, None], top2_idx].add(top2_vals)

        def step(acc, params):
            w1, bb1, w2, bb2, we = params
            h = jax.nn.gelu(xf @ w1 + bb1, approximate=False)
            y = h @ w2 + bb2
            return (acc + we[:, None] * y, None)
        out, _ = jax.lax.scan(step, jnp.zeros_like(xf), (W1, b1, W2, b2, cw.T))
        return out.reshape(Bb, Tt, Dd)

    def _L1_gnn_ref(inputs, adj_mat, weight, weight_u, weight_v, bias, proj_w, proj_b):
        import jax, jax.numpy as jnp
        import numpy as np
        N, IN_F, H, D = (4096, 256, 4, 64)
        NEG_SLOPE = 0.2
        support = (inputs @ weight).reshape(-1, H, D).transpose(1, 0, 2)
        f1 = jnp.einsum('hnd,hd->hn', support, weight_u[..., 0])[:, None, :]
        f2 = jnp.einsum('hnd,hd->hn', support, weight_v[..., 0])[:, :, None]
        scores = jax.nn.leaky_relu(f1 + f2, NEG_SLOPE)
        masked = scores * adj_mat.astype(scores.dtype)
        mask = masked != 0
        neg_inf = jnp.asarray(-jnp.inf, masked.dtype)
        m = jnp.max(jnp.where(mask, masked, neg_inf), axis=2, keepdims=True)
        m = jnp.where(jnp.isfinite(m), m, jnp.zeros_like(m))
        e = jnp.where(mask, jnp.exp(masked - m), jnp.zeros_like(masked))
        denom = e.sum(axis=2, keepdims=True)
        attn = jnp.where(denom > 0, e / jnp.where(denom > 0, denom, 1.0), jnp.zeros_like(e))
        out = jnp.einsum('hnm,hmd->hnd', attn, support)
        out = out.transpose(1, 0, 2).reshape(-1, H * D)
        out = out + bias
        out = out + inputs @ proj_w.T + proj_b
        return out

    def _L1_ffn_ref(x, Wr, br, ln_g, ln_b, W1, b1, W2, b2):
        import jax, jax.numpy as jnp
        import numpy as np
        TOP_K = 2
        LN_EPS = 1e-05
        B, S, D = x.shape
        N = B * S
        xt = x.reshape(N, D)
        logits = xt @ Wr + br
        probs = jax.nn.softmax(logits, axis=-1)
        top_p, top_idx = jax.lax.top_k(probs, TOP_K)
        weights = top_p / top_p.sum(axis=-1, keepdims=True)
        mu = xt.mean(axis=-1, keepdims=True)
        var = ((xt - mu) ** 2).mean(axis=-1, keepdims=True)
        xn = (xt - mu) * jax.lax.rsqrt(var + LN_EPS)
        xe = xn[None, :, :] * ln_g[:, None, :] + ln_b[:, None, :]
        h = jax.nn.gelu(jnp.einsum('end,edh->enh', xe, W1) + b1[:, None, :], approximate=False)
        y = jnp.einsum('enh,ehd->end', h, W2) + b2[:, None, :]
        y_tok = jnp.transpose(y, (1, 0, 2))
        sel = jnp.take_along_axis(y_tok, top_idx[:, :, None], axis=1)
        out = (weights[:, :, None] * sel).sum(axis=1)
        return out.reshape(B, S, D)

    x = x + _L0_gnn_ref(_layernorm(x, axis=-1), adj, L0_gnn_W, L0_gnn_r)
    x = x + _L0_ffn_ref((_layernorm(x, axis=-1))[None], L0_ffn_gate_w, L0_ffn_gate_b, L0_ffn_W1, L0_ffn_b1, L0_ffn_W2, L0_ffn_b2)[0]
    x = x + _L1_gnn_ref(_layernorm(x, axis=-1), adj, L1_gnn_weight, L1_gnn_weight_u, L1_gnn_weight_v, L1_gnn_bias, L1_gnn_proj_w, L1_gnn_proj_b)
    x = x + _L1_ffn_ref((_layernorm(x, axis=-1))[None], L1_ffn_Wr, L1_ffn_br, L1_ffn_ln_g, L1_ffn_ln_b, L1_ffn_W1, L1_ffn_b1, L1_ffn_W2, L1_ffn_b2)[0]
    return x


_drawn_inputs = setup_inputs


def setup_inputs(seed=0):
    import zlib

    import numpy as np

    out = dict(_drawn_inputs(seed))
    spreads = {'L0_ffn_gate_b': (0.0, 0.1),
     'L0_ffn_b1': (0.0, 0.511),
     'L0_ffn_b2': (0.0, 0.1),
     'L1_ffn_br': (0.0, 0.1),
     'L1_ffn_ln_g': (1.0, 0.2),
     'L1_ffn_ln_b': (0.0, 0.273),
     'L1_ffn_b1': (0.0, 0.284),
     'L1_ffn_b2': (0.0, 0.1)}
    factors = {}
    for name, (base, spread) in spreads.items():
        noise = np.random.default_rng([zlib.crc32(name.encode()), seed]).standard_normal(out[name].shape)
        drawn = base * np.exp(spread * noise) if base else spread * noise
        out[name] = jnp.asarray(drawn.astype(out[name].dtype))
    for name, factor in factors.items():
        out[name] = (out[name] * factor).astype(out[name].dtype)
    return out
```

```python
from contextlib import ExitStack

import concourse.bass as bass
from concourse import mybir

ALU = mybir.AluOpType
ACT = mybir.ActivationFunctionType
F32 = mybir.dt.float32
BF16 = mybir.dt.bfloat16
U8 = mybir.dt.uint8
I32 = mybir.dt.int32
AXX = mybir.AxisListType.X

P = 128
NODES = 3327
T = 26
NP = T * P
D = 256
KC = D // P
VW = 260
E = 8
EPS = 1e-5
SLOPE = 0.2
PAIRS = T // 2
RUN_TILES = 2 * T + 8
SLOT_TILES = RUN_TILES + 2

MASK_AT = 0
MASK_WORDS = NP * T // 4
V_AT = MASK_AT + MASK_WORDS
WORK_AT = V_AT + T * VW
ARENA = 43000


def at(start, size):
    return bass.ds(start, size)


class Layer:

    def __init__(self, heads, bins, width):
        self.H = heads
        self.HD = D // heads
        self.B = bins
        self.W = width
        self.NQ = 3 if heads > 1 else 2
        self.blocks = NP // width
        self.tail = NP - self.blocks * width
        assert self.blocks % 2 == 0 and self.tail == 2 * P


L0 = Layer(1, 64, 512)
L1 = Layer(4, 32, 384)


def program(nc, x_in, adjT, w0T, w0, r0, w1, w1T, uv1, proj_wT, bias1, proj_b1,
            gate0, gate_b0, m0w1, m0b1, m0w2, m0b2, gate1, gate_b1, ln_g1, ln_b1, m1w1, m1b1, m1w2, m1b2,
            qd, xd, xs, ys, out):
    ctx = ExitStack()
    with ctx:
        def sb(name, shape, dt=F32):
            return ctx.enter_context(nc.sbuf_tensor(name, shape, dt))

        def sem(name):
            held.append(nc.alloc_semaphore(name=name))
            return held[-1]

        held = []

        def hand_over():
            got, ones_ = list(held), list(start_at_one)
            held.clear()
            start_at_one.clear()
            return got, ones_

        bank = [ctx.enter_context(nc.psum_tensor(f"bank{i}", [P, 512], F32)) for i in range(8)]

        X = sb("X", [P, T * D])
        arena = sb("arena", [P, ARENA])

        def words(start, n):
            return arena[:, start:start + n]

        mask = words(MASK_AT, MASK_WORDS).bitcast(U8)
        V = words(V_AT, T * VW)

        ident = sb("ident", [P, P])
        zeros = sb("zeros", [P, 512], BF16)
        bin_no = sb("bin_no", [P, 64])
        stats = sb("stats", [P, T * 6])
        mv = sb("mv", [P, T * 3])
        rstd = sb("rstd", [P, T])
        s_all = sb("s_all", [P, 2 * 4 * T])
        reach = sb("reach", [P, 8])
        reach_all = sb("reach_all", [P, 8])
        bin_w = sb("bin_w", [P, 4])
        s_min = sb("s_min", [P, 4])
        top_add = sb("top_add", [P, 4])
        edges = sb("edges", [P, 128])
        found = sb("found", [P, 4 * T])
        m_row = sb("m_row", [P, 4 * T])
        q_cols = sb("q_cols", [P, 3 * 4 * T])
        d_all = sb("d_all", [P, 4 * T])
        neg_sj = sb("neg_sj", [P, 4 * T])
        ones = sb("ones", [P, P], BF16)
        earlier = sb("earlier", [P, P], BF16)
        order8 = sb("order8", [P, E])
        fill_at = sb("fill_at", [P, T])
        tile_no = sb("tile_no", [P, SLOT_TILES])
        ones_t = sb("ones_t", [P, T])
        slot_of = sb("slot_of", [P, 2 * T], I32)
        expert_of = sb("expert_of", [1, SLOT_TILES], I32)
        weight_of = sb("weight_of", [P, 2 * T])
        den = sb("den", [P, 16])
        rden = sb("rden", [P, 16])

        start_at_one = []

        x_loaded = sem("x_loaded")
        const_ready = sem("const_ready")
        mask_loaded = [sem("mask_loaded0"), sem("mask_loaded1")]

        def loads_sync(sp):
            for g in range(2):
                sp.dma_start(X[:, g * PAIRS * D:(g + 1) * PAIRS * D].rearrange("p (t d) -> p t d", d=D),
                             x_in[g * PAIRS * P:(g + 1) * PAIRS * P, :].rearrange("(t p) d -> p t d", p=P)
                             ).then_inc(x_loaded, 16)

        id_zero = sem("id_zero")
        tri_base = sem("tri_base")

        def constants_gpsimd(pool):
            pool.memset(ident[:, :], 0.0).then_inc(id_zero, 1)
            pool.wait_ge(id_zero, 1)
            pool.affine_select(out=ident[:, :], in_=ident[:, :], compare_op=ALU.not_equal, fill=1.0, base=0,
                               pattern=[[-1, P]], channel_multiplier=1).then_inc(const_ready, 1)
            pool.memset(zeros[:, :], 0.0).then_inc(const_ready, 1)
            pool.iota(bin_no[:, :], [[1, 64]], base=0, channel_multiplier=0,
                      allow_small_or_imprecise_dtypes=True).then_inc(const_ready, 1)
            pool.memset(ones[:, :], 1.0).then_inc(tri_base, 1)
            pool.memset(earlier[:, :], 1.0).then_inc(tri_base, 1)
            pool.wait_ge(tri_base, 2)
            pool.affine_select(out=earlier[:, :], in_=earlier[:, :], compare_op=ALU.is_gt, fill=0.0, base=0,
                               pattern=[[1, P]], channel_multiplier=-1).then_inc(const_ready, 1)
            pool.iota(order8[:, :], [[-1, E]], base=E, channel_multiplier=0,
                      allow_small_or_imprecise_dtypes=True).then_inc(const_ready, 1)
            pool.iota(fill_at[:, :], [[P, T]], base=0, channel_multiplier=0,
                      allow_small_or_imprecise_dtypes=True).then_inc(const_ready, 1)
            pool.iota(tile_no[:, :], [[1, SLOT_TILES]], base=0, channel_multiplier=0,
                      allow_small_or_imprecise_dtypes=True).then_inc(const_ready, 1)
            pool.memset(ones_t[:, :], 1.0).then_inc(const_ready, 1)
        CONSTS = 8

        def mask_loads_gpsimd(pool, between):
            def load(pair, slot):
                for half in range(2):
                    c = 2 * pair + half
                    pool.dma_start(mask[:, at(c * NP, NP)].rearrange("p (a n) -> p a n", a=2),
                                   adjT[at(c * P, P), :].rearrange("p (a n) -> p a n", a=2)
                                   ).then_inc(mask_loaded[slot], 16)
            load(0, 0)
            load(1, 1)
            for first, last in ((0, 3), (3, 5)):
                with pool.Fori(first, last) as g:
                    for slot in range(2):
                        pool.wait_ge(mask_loaded[slot], 32 * g + 32)
                        load(2 * g + 2 + slot, slot)
                if first == 0:
                    between(pool)
            pool.wait_ge(mask_loaded[0], 32 * 6)
            load(12, 0)

        class Attention:
            def __init__(self, L, tag):
                self.L, self.tag = L, tag
                H, B = L.H, L.B
                k = WORK_AT
                self.w_cols = H * L.HD + 2 * H
                self.wmat = words(k, KC * self.w_cols)
                k += KC * self.w_cols
                self.wT = words(k, KC * D)
                k += KC * D
                self.attn_vec = words(k, KC * 2 * H)
                k += KC * 2 * H
                self.proj = words(k, KC * D)
                k += KC * D
                self.pbias = words(k, 2 * D)
                k += 2 * D
                self.xn = [words(k + s * D, D) for s in range(2)]
                k += 2 * D
                self.xt = [words(k + s * D, D) for s in range(2)]
                k += 2 * D
                self.conv = [words(k + s * NP // 2, NP // 2).bitcast(BF16) for s in range(2)]
                k += NP
                self.above = words(k, T * H * B // 2).bitcast(BF16)
                k += T * H * B // 2
                self.cpos = words(k, T * H * B)
                k += T * H * B
                self.qt = words(k, L.NQ * P)
                k += L.NQ * P
                assert k <= ARENA, (tag, k)
                k = WORK_AT
                RW = L.NQ * H * L.W
                self.rows = [words(k + r * RW, RW) for r in range(2)]
                k += 2 * RW
                self.prob = [words(k + s * H * L.W, H * L.W) for s in range(2)]
                k += 2 * H * L.W
                if H > 1:
                    self.live = [words(k + s * H * L.W // 4, H * L.W // 4).bitcast(U8) for s in range(2)]
                    k += 2 * H * L.W // 4
                else:
                    self.attn_out = words(k, T * D)
                    k += T * D
                assert k <= ARENA, (tag, k)
                self.nt = L.W // P
                if H > 1:
                    self.exp_bank = [bank[4 + h] for h in range(4)]
                else:
                    self.exp_bank = [bank[4], bank[5]]
                self.w_loaded = sem(tag + "w_loaded")
                self.stat = sem(tag + "stat")
                self.aggr = sem(tag + "aggr")
                self.var_ready = sem(tag + "var_ready")
                self.sd_ready = sem(tag + "sd_ready")
                self.rstd_ready = sem(tag + "rstd_ready")
                self.wvec_ready = sem(tag + "wvec_ready")
                self.wvec_copied = sem(tag + "wvec_copied")
                self.v_done = sem(tag + "v_done")
                self.reach_part = sem(tag + "reach_part")
                self.reach_ready = sem(tag + "reach_ready")
                self.bin_steps = sem(tag + "bin_steps")
                self.edge_ready = sem(tag + "edge_ready")
                self.above_ready = sem(tag + "above_ready")
                self.cnt_zero = sem(tag + "cnt_zero")
                self.cnt_done = sem(tag + "cnt_done")
                self.cpos_done = sem(tag + "cpos_done")
                self.found_done = sem(tag + "found_done")
                self.top_done = sem(tag + "top_done")
                self.m_steps = sem(tag + "m_steps")
                self.exps = sem(tag + "exps")
                self.qt_ready = sem(tag + "qt_ready")
                self.qt_copied = sem(tag + "qt_copied")
                self.q_stored = sem(tag + "q_stored")
                self.pb = sem(tag + "pb")
                self.xn_ready = [sem(f"{tag}xn_ready{s}") for s in range(2)]
                self.tp_ready = [sem(f"{tag}tp_ready{s}") for s in range(2)]
                self.xt_ready = [sem(f"{tag}xt_ready{s}") for s in range(2)]
                self.vp_ready = [sem(f"{tag}vp_ready{s}") for s in range(2)]
                self.vp_free = [sem(f"{tag}vp_free{s}") for s in range(2)]
                self.conv_a = [sem(f"{tag}conv_a{s}") for s in range(2)]
                self.conv_v = [sem(f"{tag}conv_v{s}") for s in range(2)]
                self.conv_used = [sem(f"{tag}conv_used{s}") for s in range(2)]
                self.rows_loaded = [sem(f"{tag}rows_loaded{s}") for s in range(2)]
                self.rows_free = [sem(f"{tag}rows_free{s}") for s in range(2)]
                self.prob_ready = [sem(f"{tag}prob_ready{s}") for s in range(2)]
                self.prob_used = [sem(f"{tag}prob_used{s}") for s in range(2)]
                n_exp = len(self.exp_bank)
                self.exp_ready = [sem(f"{tag}exp_ready{k}") for k in range(n_exp)]
                self.exp_used = [sem(f"{tag}exp_used{k}") for k in range(n_exp)]
                self.live_ready = sem(tag + "live_ready")
                self.acc_free = sem(tag + "acc_free")
                self.b_done = sem(tag + "b_done")
                self.out_ready = sem(tag + "out_ready")
                start_at_one.extend(self.tp_ready + self.vp_ready + self.xt_ready + self.vp_free + self.conv_used
                                    + self.rows_free + self.exp_used + self.prob_used + [self.acc_free])

            def scol(self, which, h):
                k = (which * self.L.H + h) * T
                return s_all[:, k:k + T]

            def values_sync(self, sp):
                wc = self.w_cols
                mats = [(w0T, w0, r0), (w1, w1T, uv1)][self.L.H > 1]
                nw = self.L.H * self.L.HD
                sp.dma_start(self.wmat.rearrange("p (k n) -> p k n", n=wc)[:, :, 0:nw],
                             mats[0].rearrange("(k p) n -> p k n", p=P)).then_inc(self.w_loaded, 16)
                sp.dma_start(self.wT.rearrange("p (k n) -> p k n", n=D),
                             mats[1].rearrange("(k p) n -> p k n", p=P)).then_inc(self.w_loaded, 16)
                sp.dma_start(self.attn_vec.rearrange("p (k n) -> p k n", k=KC),
                             mats[2].rearrange("(k p) n -> p k n", p=P)).then_inc(self.w_loaded, 16)
                self.w_all = 48
                if self.L.H > 1:
                    sp.dma_start(self.proj.rearrange("p (k n) -> p k n", n=D),
                                 proj_wT.rearrange("(k p) n -> p k n", p=P)).then_inc(self.w_loaded, 16)
                    sp.dma_start(self.pbias[:, 0:D], bias1.partition_broadcast(P)).then_inc(self.w_loaded, 16)
                    sp.dma_start(self.pbias[:, D:2 * D], proj_b1.partition_broadcast(P)).then_inc(self.w_loaded, 16)
                    self.w_all = 96

            def values_vector(self, v):
                L, H = self.L, self.L.H
                layer_norm_stats(v, self)
                v.wait_ge(self.wvec_ready, 1)
                nw = H * L.HD
                v.tensor_copy(self.wmat.rearrange("p (k n) -> p k n", k=KC)[:, :, nw:],
                              bank[4][:, 0:KC * 2 * H].rearrange("p (k n) -> p k n", k=KC)
                              ).then_inc(self.wvec_copied, 1)
                if H > 1:
                    v.memset(V.rearrange("p (c n) -> p c n", n=65)[:, :, 64:65], 1.0)
                    v.tensor_tensor(self.pbias[:, 0:D], self.pbias[:, 0:D], self.pbias[:, D:2 * D],
                                    ALU.add).then_inc(self.pb, 1)
                    v.wait_ge(self.pb, 1)
                else:
                    v.memset(V.rearrange("p (c n) -> p c n", n=VW)[:, :, D:D + 1], 1.0)
                s_cols = s_all[:, 0:2 * H * T].rearrange("p (q t) -> p t q", t=T)
                with v.Fori(0, PAIRS) as i:
                    for s in range(2):
                        t = 2 * i + s
                        v.wait_ge(self.tp_ready[s], i + 1)
                        v.tensor_scalar(self.xn[s], X[:, at(t * D, D)], mv[:, at(t, 1)], rstd[:, at(t, 1)],
                                        ALU.subtract, ALU.mult).then_inc(self.xn_ready[s], 1)
                    for s in range(2):
                        t = 2 * i + s
                        vb = bank[2 + s]
                        v.wait_ge(self.vp_ready[s], i + 1 + 1)
                        if H > 1:
                            v.tensor_copy(V[:, at(t * VW, VW)].rearrange("p (h n) -> p h n", n=65)[:, :, 0:64],
                                          vb[:, 0:D].rearrange("p (h n) -> p h n", n=64))
                            v.tensor_tensor(X[:, at(t * D, D)], X[:, at(t * D, D)], self.pbias[:, 0:D],
                                            ALU.add).then_inc(self.pb, 1)
                            v.wait_ge(self.pb, t + 2)
                            v.tensor_tensor(X[:, at(t * D, D)], bank[5 + s][:, 0:D], X[:, at(t * D, D)], ALU.add)
                        else:
                            v.tensor_copy(V[:, at(t * VW, D)], vb[:, 0:D])
                        v.tensor_copy(s_cols[:, at(t, 1), :], vb[:, D:D + 2 * H].rearrange("p (o q) -> p o q", o=1)
                                      ).then_inc(self.vp_free[s], 1)

            def values_scalar(self, a):
                layer_norm_sqrt(a, self)
                with a.Fori(0, PAIRS) as i:
                    for s in range(2):
                        a.wait_ge(self.tp_ready[s], i + 1 + 1)
                        a.wait_ge(self.vp_ready[s], i + 1)
                        a.copy(self.xt[s], bank[s][:, 0:D]).then_inc(self.xt_ready[s], 1)

            def values_tensor(self, pe):
                L, H = self.L, self.L.H
                pe.wait_ge(const_ready, CONSTS)
                pe.wait_ge(self.w_loaded, 48 if H == 1 else 96)
                for k in range(KC):
                    for o in range(KC):
                        last = pe.matmul(bank[4][:, k * 2 * H:(k + 1) * 2 * H],
                                         self.wT[:, o * D + k * P:o * D + k * P + P],
                                         self.attn_vec[:, o * 2 * H:(o + 1) * 2 * H],
                                         start=(o == 0), stop=(o == KC - 1))
                last.then_inc(self.wvec_ready, 1)
                pe.wait_ge(self.wvec_copied, 1)
                with pe.Fori(0, PAIRS) as i:
                    for s in range(2):
                        pe.wait_ge(self.xn_ready[s], i + 1)
                        pe.wait_ge(self.xt_ready[s], i + 1)
                        for k in range(KC):
                            last = pe.transpose(bank[s][:, k * P:(k + 1) * P], self.xn[s][:, k * P:(k + 1) * P],
                                                ident[:, :])
                        last.then_inc(self.tp_ready[s], 1)
                    for s in range(2):
                        pe.wait_ge(self.xt_ready[s], i + 1 + 1)
                        pe.wait_ge(self.vp_free[s], i + 1)
                        if H > 1:
                            for k in range(KC):
                                pe.matmul(bank[5 + s][:, 0:D], self.xt[s][:, k * P:(k + 1) * P],
                                          self.proj[:, k * D:(k + 1) * D], start=(k == 0), stop=(k == KC - 1))
                        for k in range(KC):
                            last = pe.matmul(bank[2 + s][:, 0:self.w_cols], self.xt[s][:, k * P:(k + 1) * P],
                                             self.wmat[:, k * self.w_cols:(k + 1) * self.w_cols],
                                             start=(k == 0), stop=(k == KC - 1))
                        last.then_inc(self.vp_ready[s], 1)

            def bins_vector(self, v):
                L, H, B = self.L, self.L.H, self.L.B
                sj = s_all[:, 0:H * T].rearrange("p (h t) -> p h t", t=T)
                for s in range(2):
                    v.wait_ge(self.vp_free[s], PAIRS + 1)
                v.tensor_reduce(reach[:, 0:H], sj, AXX, ALU.max).then_inc(self.reach_part, 1)
                v.tensor_reduce(reach[:, H:2 * H], sj, AXX, ALU.min, negate=True).then_inc(self.reach_part, 1)
                if H > 1:
                    v.tensor_scalar(neg_sj[:, 0:H * T], s_all[:, 0:H * T], -1.0, None, ALU.mult)
                v.wait_ge(self.reach_ready, 1)
                v.tensor_tensor(bin_w[:, 0:H], reach_all[:, 0:H], reach_all[:, H:2 * H], ALU.add
                                ).then_inc(self.bin_steps, 1)
                v.tensor_scalar(s_min[:, 0:H], reach_all[:, H:2 * H], -1.0, None, ALU.mult
                                ).then_inc(self.bin_steps, 1)
                v.wait_ge(self.bin_steps, 2)
                v.tensor_scalar(bin_w[:, 0:H], bin_w[:, 0:H], 1.0 / B, None, ALU.mult).then_inc(self.bin_steps, 1)
                v.wait_ge(self.bin_steps, 3)
                v.scalar_tensor_tensor(out=top_add[:, 0:H], in0=bin_w[:, 0:H], scalar=0.125, in1=s_min[:, 0:H],
                                       op0=ALU.mult, op1=ALU.add).then_inc(self.bin_steps, 1)
                v.wait_ge(const_ready, CONSTS)
                for h in range(H):
                    v.tensor_scalar(edges[:, h * B:(h + 1) * B], bin_no[:, 0:B], bin_w[:, h:h + 1], s_min[:, h:h + 1],
                                    ALU.mult, ALU.add).then_inc(self.edge_ready, 1)
                v.wait_ge(self.edge_ready, H)
                e3 = edges[:, 0:H * B].rearrange("p (h b) -> p h b", b=B)
                with v.Fori(0, T) as t:
                    v.tensor_tensor(self.above[:, at(t * H * B, H * B)].rearrange("p (h b) -> p h b", b=B),
                                    sj[:, :, at(t, 1)].to_broadcast([P, H, B]), e3, ALU.is_ge
                                    ).then_inc(self.above_ready, 1)

            def bins_gpsimd(self, pool):
                H = self.L.H
                pool.wait_ge(self.reach_part, 2)
                pool.partition_all_reduce(reach_all[:, 0:2 * H], reach[:, 0:2 * H], P, bass.bass_isa.ReduceOp.max
                                          ).then_inc(self.reach_ready, 1)

            CA = 1792

            def count_pairs(self, eng, body):
                with eng.Fori(0, PAIRS // 2) as g:
                    for half in range(2):
                        body(2 * g + half, g, half)
                body(PAIRS - 1, PAIRS // 2, 0)

            def count_scalar(self, a):
                def body(pair, g, half):
                    a.wait_ge(mask_loaded[half], 32 * (g + 1))
                    for s in range(2):
                        a.wait_ge(self.conv_used[s], pair + 1)
                        a.copy(self.conv[s][:, 0:self.CA], mask[:, at((2 * pair + s) * NP, self.CA)]
                               ).then_inc(self.conv_a[s], 1)
                self.count_pairs(a, body)

            def count_vector(self, v):
                def body(pair, g, half):
                    v.wait_ge(mask_loaded[half], 32 * (g + 1))
                    for s in range(2):
                        v.wait_ge(self.conv_used[s], pair + 1)
                        v.tensor_copy(self.conv[s][:, self.CA:NP],
                                      mask[:, at((2 * pair + s) * NP + self.CA, NP - self.CA)]
                                      ).then_inc(self.conv_v[s], 1)
                self.count_pairs(v, body)

            def count_tensor(self, pe):
                H, B = self.L.H, self.L.B
                HB = H * B
                per = 512 // HB
                nb = -(-T // per)
                pe.wait_ge(self.edge_ready, H)
                for b in range(nb):
                    pe.matmul(bank[b][:, :], zeros[:, 0:P], zeros[:, :], start=True, stop=True)
                pe.wait_ge(self.above_ready, T)
                with pe.Fori(0, PAIRS) as pair:
                    for s in range(2):
                        pe.wait_ge(self.conv_a[s], pair + 1)
                        pe.wait_ge(self.conv_v[s], pair + 1)
                        for t in range(T):
                            last = pe.matmul(bank[t // per][:, t % per * HB:(t % per + 1) * HB],
                                             self.conv[s][:, t * P:(t + 1) * P],
                                             self.above[:, at((2 * pair + s) * HB, HB)],
                                             start=False, stop=False, skip_group_check=True)
                        last.then_inc(self.conv_used[s], 1)

            def rows_vector(self, v):
                L, H, B = self.L, self.L.H, self.L.B
                HB, HT = H * B, H * T
                per = 512 // HB
                nb = -(-T // per)
                for s in range(2):
                    v.wait_ge(self.conv_used[s], PAIRS + 1)
                for b in range(nb):
                    n = min(per, T - b * per) * HB
                    v.tensor_scalar(self.cpos[:, b * per * HB:b * per * HB + n], bank[b][:, 0:n], 0.0, None, ALU.is_gt
                                    ).then_inc(self.cpos_done, 1)
                v.wait_ge(self.cpos_done, nb)
                f3 = found[:, 0:HT].rearrange("p (h t) -> p h t", t=T)
                for h in range(H):
                    v.tensor_reduce(f3[:, h, :], self.cpos.rearrange("p (t h b) -> p h t b", h=H, b=B)[:, h, :, :],
                                    AXX, ALU.add).then_inc(self.found_done, 1)
                v.wait_ge(self.found_done, H)
                for h in range(H):
                    v.tensor_scalar(m_row[:, h * T:(h + 1) * T], found[:, h * T:(h + 1) * T], bin_w[:, h:h + 1],
                                    top_add[:, h:h + 1], ALU.mult, ALU.add).then_inc(self.top_done, 1)
                v.wait_ge(self.top_done, H)
                si = s_all[:, HT:2 * HT]
                m = m_row[:, 0:HT]
                v.tensor_tensor(m, si, m, ALU.add).then_inc(self.m_steps, 1)
                v.wait_ge(self.m_steps, 1)
                v.scalar_tensor_tensor(out=found[:, 0:HT], in0=m, scalar=SLOPE, in1=m, op0=ALU.mult, op1=ALU.max
                                       ).then_inc(self.m_steps, 1)
                v.wait_ge(self.m_steps, 2)
                v.tensor_tensor(q_cols[:, 0:HT], si, found[:, 0:HT], ALU.subtract).then_inc(self.m_steps, 1)
                v.scalar_tensor_tensor(out=q_cols[:, HT:2 * HT], in0=si, scalar=SLOPE, in1=found[:, 0:HT],
                                       op0=ALU.mult, op1=ALU.subtract).then_inc(self.m_steps, 1)
                if H > 1:
                    v.tensor_copy(q_cols[:, 2 * HT:3 * HT], si).then_inc(self.m_steps, 1)
                for q in range(L.NQ):
                    v.wait_ge(self.qt_ready, q + 1)
                    last = v.tensor_copy(self.qt[0:HT, q * P:(q + 1) * P], bank[q][0:HT, 0:P]
                                         ).then_inc(self.qt_copied, 1)

            def rows_scalar(self, a):
                HT = self.L.H * T
                a.activation(d_all[:, 0:HT], s_all[:, 0:HT], ACT.Exp, scale=SLOPE)
                a.wait_ge(self.m_steps, 4 if self.L.H == 1 else 5)
                a.activation(q_cols[:, HT:2 * HT], q_cols[:, HT:2 * HT], ACT.Exp).then_inc(self.exps, 1)

            def rows_tensor(self, pe):
                HT = self.L.H * T
                pe.wait_ge(self.exps, 1)
                pe.wait_ge(self.cpos_done, 1)
                for q in range(self.L.NQ):
                    pe.transpose(bank[q][0:HT, 0:P], q_cols[:, q * HT:(q + 1) * HT], ident[:, :]
                                 ).then_inc(self.qt_ready, 1)

            def rows_sync(self, sp):
                HT = self.L.H * T
                sp.wait_ge(self.qt_copied, self.L.NQ)
                sp.dma_start(qd[0:self.L.NQ * HT, :].rearrange("(q r) p -> r q p", r=HT),
                             self.qt[0:HT, :].rearrange("r (q p) -> r q p", p=P)).then_inc(self.q_stored, 16)
                sp.wait_ge(self.q_stored, 16)

            def each_block(self, eng, body):
                with eng.Fori(0, self.L.blocks // 2) as bp:
                    for r in range(2):
                        body(2 * bp + r, bp, r, self.nt)
                body(self.L.blocks, self.L.blocks // 2, 0, self.L.tail // P)

            def attend_sync(self, sp):
                L = self.L
                q_all = qd[0:L.NQ * L.H * T, :].rearrange("(r t) p -> r (t p)", t=T)

                def body(b, bp, r, nt):
                    sp.wait_ge(self.rows_free[r], bp + 1)
                    w = nt * P
                    sp.dma_start(self.rows[r].rearrange("p (q w) -> p q w", w=L.W)[:, :, 0:w],
                                 q_all[:, at(b * L.W, w)].partition_broadcast(P)).then_inc(self.rows_loaded[r], 16)
                self.each_block(sp, body)

            def exp_slot(self, s, h, b, i):
                if self.L.H > 1:
                    return h, b * T + 2 * i + s
                return s, b * PAIRS + i

            def attend_scalar(self, a):
                L, H = self.L, self.L.H

                def body(b, bp, r, nt):
                    a.wait_ge(self.rows_loaded[r], 16 * (bp + 1))
                    with a.Fori(0, PAIRS) as i:
                        for s in range(2):
                            for h in range(H):
                                k, used = self.exp_slot(s, h, b, i)
                                a.wait_ge(self.exp_used[k], used + 1)
                                a.activation(self.exp_bank[k][:, 0:nt * P], self.rows[r][:, h * L.W:h * L.W + nt * P],
                                             ACT.Exp, bias=s_all[:, at(h * T + 2 * i + s, 1)]
                                             ).then_inc(self.exp_ready[k], 1)
                self.each_block(a, body)

            def attend_vector(self, v):
                L, H, W = self.L, self.L.H, self.L.W

                def body(b, bp, r, nt):
                    w = nt * P
                    rows = self.rows[r]
                    with v.Fori(0, PAIRS) as i:
                        for s in range(2):
                            c = 2 * i + s
                            v.wait_ge(self.prob_used[s], b * PAIRS + i + 1)
                            for h in range(H):
                                k, used = self.exp_slot(s, h, b, i)
                                v.wait_ge(self.exp_ready[k], used + 1)
                                v.scalar_tensor_tensor(
                                    out=self.prob[s][:, h * W:h * W + w], in0=rows[:, (H + h) * W:(H + h) * W + w],
                                    scalar=d_all[:, at(h * T + c, 1)], in1=self.exp_bank[k][:, 0:w],
                                    op0=ALU.mult, op1=ALU.max).then_inc(self.exp_used[k], 1)
                                if H > 1:
                                    v.scalar_tensor_tensor(
                                        out=self.live[s][:, h * W:h * W + w],
                                        in0=rows[:, (2 * H + h) * W:(2 * H + h) * W + w],
                                        scalar=neg_sj[:, at(h * T + c, 1)], in1=mask[:, at(c * NP + b * W, w)],
                                        op0=ALU.not_equal, op1=ALU.mult).then_inc(self.live_ready, 1)
                            v.wait_ge(self.exp_used[k], used + 1 + 1)
                            if H > 1:
                                v.wait_ge(self.live_ready, H * (b * T + c + 1))
                                pv = self.prob[s].rearrange("p (h w) -> p h w", w=W)[:, :, 0:w]
                                v.tensor_tensor(pv, pv, self.live[s].rearrange("p (h w) -> p h w", w=W)[:, :, 0:w],
                                                ALU.min).then_inc(self.prob_ready[s], 1)
                            else:
                                v.tensor_tensor(self.prob[s][:, 0:w], self.prob[s][:, 0:w],
                                                mask[:, at(c * NP + b * W, w)], ALU.min
                                                ).then_inc(self.prob_ready[s], 1)
                    for s in range(2):
                        v.wait_ge(self.prob_used[s], (b + 1) * PAIRS + 1)
                    dcol = L.HD
                    for n in range(nt):
                        acc = bank[n][:, 0:H * (L.HD + 1)].rearrange("p (h x) -> p h x", h=H)
                        if H > 1:
                            v.tensor_copy(den[:, n * H:(n + 1) * H], acc[:, :, dcol]).then_inc(self.b_done, 1)
                        else:
                            v.reciprocal(rden[:, n:n + 1], bank[n][:, D:D + 1]).then_inc(self.b_done, 1)
                    v.wait_ge(self.b_done, self.steps(b, nt, 1))
                    if H > 1:
                        v.scalar_tensor_tensor(out=den[:, 0:nt * H], in0=den[:, 0:nt * H], scalar=0.0,
                                               in1=den[:, 0:nt * H], op0=ALU.is_equal, op1=ALU.add
                                               ).then_inc(self.b_done, 1)
                        v.wait_ge(self.b_done, self.steps(b, nt, 2))
                        v.reciprocal(rden[:, 0:nt * H], den[:, 0:nt * H]).then_inc(self.b_done, 1)
                        v.wait_ge(self.b_done, self.steps(b, nt, 3))
                    for n in range(nt):
                        t = b * self.nt + n
                        for h in range(H):
                            if H > 1:
                                xh = X[:, at(t * D + h * 64, 64)]
                                last = v.scalar_tensor_tensor(out=xh, in0=bank[n][:, h * 65:h * 65 + 64],
                                                              scalar=rden[:, n * H + h:n * H + h + 1], in1=xh,
                                                              op0=ALU.mult, op1=ALU.add)
                            else:
                                last = v.tensor_scalar(self.attn_out[:, at(t * D, D)], bank[n][:, 0:D],
                                                       rden[:, n:n + 1], None, ALU.mult)
                    last.then_inc(self.acc_free, 1)
                    v.wait_ge(self.acc_free, b + 1 + 1)
                    v.tensor_copy(den[:, 15:16], ident[:, 0:1]).then_inc(self.rows_free[r], 1)
                self.each_block(v, body)

            def steps(self, b, nt, k):
                if self.L.H == 1:
                    return b * self.nt + nt
                return b * (self.nt + 2) + nt + (k - 1)

            def attend_tensor(self, pe):
                L, H, W = self.L, self.L.H, self.L.W
                cols = H * (L.HD + 1)

                def body(b, bp, r, nt):
                    pe.wait_ge(self.acc_free, b + 1)
                    for n in range(nt):
                        pe.matmul(bank[n][:, 0:cols], zeros[:, 0:P], zeros[:, 0:cols], start=True, stop=True)
                    with pe.Fori(0, PAIRS) as i:
                        for s in range(2):
                            c = 2 * i + s
                            pe.wait_ge(self.prob_ready[s], b * PAIRS + i + 1)
                            for n in range(nt):
                                for h in range(H):
                                    hw = L.HD + 1
                                    last = pe.matmul(bank[n][:, h * hw:(h + 1) * hw],
                                                     self.prob[s][:, h * W + n * P:h * W + (n + 1) * P],
                                                     V[:, at(c * VW + h * hw, hw)],
                                                     start=False, stop=False, skip_group_check=True)
                            last.then_inc(self.prob_used[s], 1)
                self.each_block(pe, body)

            def gelu_scalar(self, a):
                a.wait_ge(self.acc_free, self.L.blocks + 1 + 1)
                with a.Fori(0, PAIRS) as i:
                    o = self.attn_out[:, at(i * 2 * D, 2 * D)]
                    a.activation(o, o, ACT.Gelu).then_inc(self.out_ready, 1)

            def gelu_vector(self, v):
                with v.Fori(0, PAIRS) as i:
                    v.wait_ge(self.out_ready, i + 1)
                    xs = X[:, at(i * 2 * D, 2 * D)]
                    v.tensor_tensor(xs, xs, self.attn_out[:, at(i * 2 * D, 2 * D)], ALU.add)


        class Experts:
            def __init__(self, hidden, tag, weights_at, scratch_at, second_norm):
                self.HID, self.tag, self.second_norm = hidden, tag, second_norm
                self.HC = hidden // P
                self.HB = hidden // 512
                self.W1 = words(weights_at, E * KC * hidden)
                self.W2 = words(weights_at + E * KC * hidden, E * self.HC * D)
                b1_at = weights_at + E * KC * hidden + E * self.HC * D
                self.b1 = words(b1_at, E * hidden)
                assert b1_at + E * hidden <= ARENA
                k = scratch_at
                TE = T * E
                self.logits = words(k, TE)
                k += TE
                self.pick1 = words(k, TE)
                k += TE
                self.pick2 = words(k, TE)
                k += TE
                self.work = words(k, TE)
                k += TE
                self.posx = words(k, TE)
                k += TE
                self.incl = words(k, TE)
                k += TE
                self.routed = words(k, TE // 2).bitcast(BF16)
                k += TE // 2
                self.top1 = words(k, T)
                k += T
                self.top2 = words(k, T)
                k += T
                self.best = words(k, T)
                k += T
                self.sums = words(k, T)
                k += T
                self.e2 = words(k, T)
                k += T
                self.gate = words(k, KC * E)
                k += KC * E
                self.gate_b = words(k, E)
                k += E
                self.used = words(k, E)
                k += E
                self.end = words(k, E)
                k += E
                self.base = words(k, E)
                k += E
                self.fills = words(k, E * T)
                self.below = words(k, SLOT_TILES * E)
                k += SLOT_TILES * E
                self.tile_e = words(k, SLOT_TILES)
                k += SLOT_TILES
                self.xn = [words(k + s * D, D) for s in range(2)]
                k += 2 * D
                self.xt = [words(k + s * D, D) for s in range(2)]
                k += 2 * D
                assert k <= ARENA, (k, ARENA)
                k = 0

                def ring(n, size):
                    nonlocal k
                    got = [X[:, k + s * size:k + (s + 1) * size] for s in range(n)]
                    k += n * size
                    return got
                self.rx = ring(2, D)
                self.rxt = ring(2, D)
                self.ry = ring(2, D)
                self.ht = ring(2, hidden)
                self.hid = ring(1, hidden)[0]
                self.b2 = ring(1, E * D)[0]
                assert k <= T * D
                self.got = words(weights_at, 2 * T * D)
                self.loaded = sem(tag + "loaded")
                self.stat = sem(tag + "stat")
                self.aggr = sem(tag + "aggr")
                self.var_ready = sem(tag + "var_ready")
                self.sd_ready = sem(tag + "sd_ready")
                self.rstd_ready = sem(tag + "rstd_ready")
                self.x_spilled = sem(tag + "x_spilled")
                self.x_normed = sem(tag + "x_normed")
                self.lg_done = sem(tag + "lg_done")
                self.lg_copied = sem(tag + "lg_copied")
                self.route = sem(tag + "route")
                self.exps = sem(tag + "exps")
                self.picked = sem(tag + "picked")
                self.cnt_done = sem(tag + "cnt_done")
                self.tiles_known = sem(tag + "tiles_known")
                self.scattered = sem(tag + "scattered")
                self.w_loaded = sem(tag + "w_loaded")
                self.b_loaded = sem(tag + "b_loaded")
                self.folded = sem(tag + "folded")
                self.fold_used = sem(tag + "fold_used")
                self.fold_mm = sem(tag + "fold_mm")
                self.lnb_ready = sem(tag + "lnb_ready")
                self.lng_loaded = sem(tag + "lng_loaded")
                self.hid_ready = sem(tag + "hid_ready")
                self.h2 = sem(tag + "h2")
                self.x_back = sem(tag + "x_back")
                self.sum_step = sem(tag + "sum_step")
                self.g_lists = sem(tag + "g_lists")
                self.xn_ready = [sem(f"{tag}xn_ready{s}") for s in range(2)]
                self.tp_ready = [sem(f"{tag}tp_ready{s}") for s in range(2)]
                self.xt_ready = [sem(f"{tag}xt_ready{s}") for s in range(2)]
                self.rx_loaded = [sem(f"{tag}rx_loaded{s}") for s in range(2)]
                self.tx_ready = [sem(f"{tag}tx_ready{s}") for s in range(2)]
                self.xgt_ready = [sem(f"{tag}xgt_ready{s}") for s in range(2)]
                self.h_ready = [sem(f"{tag}h_ready{s}") for s in range(2)]
                self.th_ready = [sem(f"{tag}th_ready{s}") for s in range(2)]
                self.ht_ready = [sem(f"{tag}ht_ready{s}") for s in range(2)]
                self.y_ready = [sem(f"{tag}y_ready{s}") for s in range(2)]
                self.ry_ready = [sem(f"{tag}ry_ready{s}") for s in range(2)]
                self.stored = [sem(f"{tag}stored{s}") for s in range(2)]
                self.ry_free = [sem(f"{tag}ry_free{s}") for s in range(2)]
                self.gathered = [sem(f"{tag}gathered{g}") for g in range(4)]
                start_at_one.extend(self.tp_ready + self.xt_ready + self.xn_ready + self.tx_ready + self.th_ready
                                    + self.h_ready + self.ht_ready + self.y_ready + self.ry_ready + self.ry_free
                                    + [self.fold_used])

            def route_sync(self, sp, gate_w, gate_b, w1m, w2m):
                sp.dma_start(self.gate.rearrange("p (k e) -> p k e", e=E),
                             gate_w.rearrange("(k p) e -> p k e", p=P)).then_inc(self.loaded, 16)
                sp.dma_start(self.gate_b, gate_b.partition_broadcast(P)).then_inc(self.loaded, 16)
                sp.dma_start(xd.rearrange("(t p) d -> p t d", p=P), X[:, :].rearrange("p (t d) -> p t d", d=D)
                             ).then_inc(self.x_spilled, 16)
                for w, m in ((self.W1, w1m), (self.W2, w2m)):
                    n = m.shape[1] // 4
                    for g in range(4):
                        sp.dma_start(w[:, g * n:(g + 1) * n], m[:, g * n:(g + 1) * n]).then_inc(self.w_loaded, 16)

            def norm_in_place(self, v):
                with v.Fori(0, T) as t:
                    v.tensor_scalar(X[:, at(t * D, D)], X[:, at(t * D, D)], mv[:, at(t, 1)], rstd[:, at(t, 1)],
                                    ALU.subtract, ALU.mult).then_inc(self.x_normed, 1)

            def route_vector(self, v):
                layer_norm_stats(v, self)
                v.wait_ge(self.x_spilled, 16)
                self.norm_in_place(v)
                TE = T * E
                lg3 = self.logits.rearrange("p (t e) -> p t e", e=E)
                w3 = self.work.rearrange("p (t e) -> p t e", e=E)
                r = self.route
                n = [0]

                def step(ins):
                    n[0] += 1
                    ins.then_inc(r, 1)
                    v.wait_ge(r, n[0])

                def spread(a):
                    return a.rearrange("p (t o) -> p t o", o=1).to_broadcast([P, T, E])

                def spread_t(a):
                    return a.rearrange("p (o e) -> p o e", o=1).to_broadcast([P, T, E])

                v.wait_ge(self.lg_done, T)
                v.wait_ge(self.loaded, 32)
                step(v.tensor_tensor(lg3, bank[2][:, 0:TE].rearrange("p (t e) -> p t e", e=E), spread_t(self.gate_b),
                                     ALU.add))
                for top, pick in ((self.top1, self.pick1), (self.top2, self.pick2)):
                    p3 = pick.rearrange("p (t e) -> p t e", e=E)
                    step(v.tensor_reduce(top, lg3, AXX, ALU.max))
                    step(v.tensor_tensor(w3, lg3, spread(top), ALU.is_equal))
                    step(v.tensor_tensor(w3, w3, spread_t(order8[:, :]), ALU.mult))
                    step(v.tensor_reduce(self.best, w3, AXX, ALU.max))
                    step(v.tensor_tensor(p3, w3, spread(self.best), ALU.is_equal))
                    if top is self.top1:
                        step(v.tensor_tensor(w3, lg3, spread(top), ALU.subtract))
                        v.tensor_copy(self.posx, self.work).then_inc(self.picked, 1)
                        step(v.scalar_tensor_tensor(out=self.logits, in0=pick, scalar=-3.0e38, in1=self.logits,
                                                    op0=ALU.mult, op1=ALU.add))
                v.tensor_tensor(self.e2, self.top2, self.top1, ALU.subtract).then_inc(self.picked, 1)
                v.tensor_tensor(self.routed, self.pick1, self.pick2, ALU.add).then_inc(self.picked, 1)
                v.wait_ge(self.exps, 2)
                if self.second_norm:
                    step(v.tensor_scalar(self.sums, self.e2, 1.0, None, ALU.add))
                else:
                    step(v.tensor_reduce(self.sums, self.posx.rearrange("p (t e) -> p t e", e=E), AXX, ALU.add))
                step(v.reciprocal(weight_of[:, 0:T], self.sums))
                step(v.tensor_tensor(weight_of[:, T:2 * T], self.e2, weight_of[:, 0:T], ALU.mult))
                v.wait_ge(self.cnt_done, 1)
                step(v.tensor_copy(self.work, bank[4][:, 0:TE]))
                i3 = self.incl.rearrange("p (e t) -> p e t", t=T)
                for e in range(E):
                    last = v.tensor_tensor_scan(i3[:, e, :], ones_t[:, :], w3[:, :, e], 0.0, ALU.mult, ALU.add)
                step(last)
                f3 = self.fills.rearrange("p (e t) -> p e t", t=T)
                step(v.tensor_tensor(f3, i3[:, :, T - 1:T].to_broadcast([P, E, T]),
                                     fill_at[:, :].rearrange("p (o t) -> p o t", o=1).to_broadcast([P, E, T]),
                                     ALU.is_gt))
                step(v.tensor_reduce(self.used, f3, AXX, ALU.add))
                step(v.tensor_tensor_scan(self.end, ones_t[:, 0:E], self.used, 0.0, ALU.mult, ALU.add))
                step(v.tensor_tensor(self.base, self.end, self.used, ALU.subtract))
                step(v.tensor_scalar(self.base, self.base, float(P), None, ALU.mult))
                p3 = self.posx.rearrange("p (t e) -> p t e", e=E)
                step(v.tensor_tensor(p3, i3.rearrange("p e t -> p t e"), w3, ALU.subtract))
                step(v.tensor_tensor(p3, p3, spread_t(self.base), ALU.add))
                step(v.tensor_tensor(self.posx, bank[3][:, 0:TE], self.posx, ALU.add))
                for k, pick in enumerate((self.pick1, self.pick2)):
                    step(v.tensor_tensor(self.work, self.posx, pick, ALU.mult))
                    step(v.tensor_reduce(self.best, w3, AXX, ALU.add))
                    step(v.tensor_copy(slot_of[:, k * T:(k + 1) * T], self.best))
                b3 = self.below.rearrange("p (g e) -> p g e", e=E)[0:1]
                step(v.tensor_tensor(b3, self.end[0:1].rearrange("p (o e) -> p o e", o=1)
                                     .to_broadcast([1, SLOT_TILES, E]),
                                     tile_no[0:1].rearrange("p (g o) -> p g o", o=1).to_broadcast([1, SLOT_TILES, E]),
                                     ALU.is_le))
                step(v.tensor_reduce(self.tile_e[0:1], b3, AXX, ALU.add))
                step(v.tensor_scalar(self.tile_e[0:1], self.tile_e[0:1], float(E - 1), None, ALU.min))
                v.tensor_copy(expert_of[:, :], self.tile_e[0:1]).then_inc(self.tiles_known, 1)
                if self.second_norm:
                    v.wait_ge(self.xn_ready[1], PAIRS + 1)
                    layer_norm_stats(v, self, 2)
                    self.norm_in_place(v)
                v.wait_ge(self.x_normed, T * (1 + self.second_norm))
                v.tensor_copy(den[:, 15:16], ident[:, 0:1]).then_inc(self.tiles_known, 1)

            def route_scalar(self, a):
                layer_norm_sqrt(a, self)
                with a.Fori(0, PAIRS) as i:
                    for s in range(2):
                        t = 2 * i + s
                        a.wait_ge(self.x_normed, t + 1)
                        a.wait_ge(self.tp_ready[s], i + 1)
                        a.copy(self.xn[s], X[:, at(t * D, D)]).then_inc(self.xn_ready[s], 1)
                    for s in range(2):
                        a.wait_ge(self.tp_ready[s], i + 2)
                        a.copy(self.xt[s], bank[s][:, 0:D]).then_inc(self.xt_ready[s], 1)
                a.wait_ge(self.picked, 3)
                a.activation(self.posx, self.posx, ACT.Exp).then_inc(self.exps, 1)
                a.activation(self.e2, self.e2, ACT.Exp).then_inc(self.exps, 1)
                if self.second_norm:
                    layer_norm_sqrt(a, self, 2)

            def route_tensor(self, pe):
                pe.wait_ge(self.loaded, 32)
                with pe.Fori(0, PAIRS) as i:
                    for s in range(2):
                        pe.wait_ge(self.xn_ready[s], i + 2)
                        pe.wait_ge(self.xt_ready[s], i + 1)
                        for k in range(KC):
                            last = pe.transpose(bank[s][:, k * P:(k + 1) * P], self.xn[s][:, k * P:(k + 1) * P],
                                                ident[:, :])
                        last.then_inc(self.tp_ready[s], 1)
                    for s in range(2):
                        pe.wait_ge(self.xt_ready[s], i + 2)
                        for k in range(KC):
                            last = pe.matmul(bank[2][:, at((2 * i + s) * E, E)], self.xt[s][:, k * P:(k + 1) * P],
                                             self.gate[:, k * E:(k + 1) * E], start=(k == 0), stop=(k == KC - 1))
                        last.then_inc(self.lg_done, 1)
                pe.wait_ge(self.picked, 3)
                pe.matmul(bank[3][:, 0:T * E], earlier[:, :], self.routed, start=True, stop=True)
                pe.matmul(bank[4][:, 0:T * E], ones[:, :], self.routed, start=True, stop=True
                          ).then_inc(self.cnt_done, 1)

            def route_gpsimd(self, pool):
                pool.wait_ge(self.tiles_known, 2)
                for t in range(T):
                    for k in range(2):
                        pool.indirect_dma_start(xs[:, :],
                                                bass.IndirectOffsetOnAxis(ap=slot_of[:, k * T + t:k * T + t + 1], axis=0),
                                                X[:, t * D:(t + 1) * D], None).then_inc(self.scattered, 16)
                pool.wait_ge(self.scattered, 16 * 2 * T)

            def tiles_sync(self, sp, b1m, b2m):
                sp.dma_start(self.b1, b1m.partition_broadcast(P)).then_inc(self.b_loaded, 16)
                sp.dma_start(self.b2, b2m.partition_broadcast(P)).then_inc(self.b_loaded, 16)
                for s in range(2):
                    sp.dma_start(self.rx[s], xs[s * P:(s + 1) * P, :]).then_inc(self.rx_loaded[s], 16)
                with sp.Fori(0, RUN_TILES // 2) as i:
                    for s in range(2):
                        sp.wait_ge(self.tx_ready[s], i + 2)
                        sp.dma_start(self.rx[s], xs[at((2 * i + s + 2) * P, P), :]).then_inc(self.rx_loaded[s], 16)

            def tiles_gpsimd(self, pool):
                with pool.Fori(0, RUN_TILES // 2) as i:
                    for s in range(2):
                        pool.wait_ge(self.ry_ready[s], i + 2)
                        pool.dma_start(ys[at((2 * i + s) * P, P), :], self.ry[s]).then_inc(self.stored[s], 16)
                        pool.wait_ge(self.stored[s], 16 * (i + 1))
                        pool.sem_inc(self.ry_free[s], 1)

            def tiles_tensor(self, pe):
                HID, HC = self.HID, self.HC

                def hidden(e, s):
                    for b in range(self.HB):
                        for k in range(KC):
                            last = pe.matmul(bank[b][:, :], self.rxt[s][:, k * P:(k + 1) * P],
                                             self.W1[:, at(e * (KC * HID) + k * HID + b * 512, 512)],
                                             start=(k == 0), stop=(k == KC - 1))
                    last.then_inc(self.h_ready[s], 1)

                def turn_x(s):
                    for k in range(KC):
                        last = pe.transpose(bank[4][:, k * P:(k + 1) * P], self.rx[s][:, k * P:(k + 1) * P],
                                            ident[:, :])
                    last.then_inc(self.tx_ready[s], 1)

                pe.wait_ge(self.w_loaded, 16 * 8)
                if self.second_norm:
                    self.fold_tensor(pe)
                pe.wait_ge(self.rx_loaded[0], 16)
                turn_x(0)
                pe.wait_ge(self.rx_loaded[1], 16)
                pe.wait_ge(self.xgt_ready[0], 1)
                turn_x(1)
                e0 = pe.value_load(expert_of[0:1, 0:1], min_val=0, max_val=E - 1)
                hidden(e0, 0)
                with pe.Fori(0, RUN_TILES // 2) as i:
                    for s in range(2):
                        o = 1 - s
                        g = 2 * i + s
                        pe.wait_ge(self.hid_ready, g + 1)
                        pe.wait_ge(self.ht_ready[o], i + 1 + s)
                        for c in range(HC):
                            last = pe.transpose(bank[2 + c // 4][:, c % 4 * P:(c % 4 + 1) * P],
                                                self.hid[:, c * P:(c + 1) * P], ident[:, :])
                        last.then_inc(self.th_ready[s], 1)
                        pe.wait_ge(self.rx_loaded[s], 16 * (i + 2))
                        pe.wait_ge(self.xgt_ready[o], i + 1 + s)
                        turn_x(s)
                        e = pe.value_load(expert_of[0:1, at(g + 1, 1)], min_val=0, max_val=E - 1)
                        hidden(e, o)
                        e = pe.value_load(expert_of[0:1, at(g, 1)], min_val=0, max_val=E - 1)
                        pe.wait_ge(self.ht_ready[s], i + 2)
                        pe.wait_ge(self.ry_ready[s], i + 1)
                        for c in range(HC):
                            last = pe.matmul(bank[5 + s][:, 0:D], self.ht[s][:, c * P:(c + 1) * P],
                                             self.W2[:, at(e * (HC * D) + c * D, D)],
                                             start=(c == 0), stop=(c == HC - 1))
                        last.then_inc(self.y_ready[s], 1)

            def tiles_scalar(self, a):
                for s in range(2):
                    a.wait_ge(self.tx_ready[s], 2)
                    a.copy(self.rxt[s], bank[4][:, 0:D]).then_inc(self.xgt_ready[s], 1)
                with a.Fori(0, RUN_TILES // 2) as i:
                    for s in range(2):
                        a.wait_ge(self.th_ready[s], i + 2)
                        a.wait_ge(self.y_ready[s], i + 1)
                        for b in range(self.HB):
                            last = a.activation(self.ht[s][:, b * 512:(b + 1) * 512], bank[2 + b][:, :], ACT.Gelu)
                        last.then_inc(self.ht_ready[s], 1)
                        a.wait_ge(self.tx_ready[s], i + 3)
                        a.wait_ge(self.h_ready[s], i + 2)
                        a.copy(self.rxt[s], bank[4][:, 0:D]).then_inc(self.xgt_ready[s], 1)

            def tiles_vector(self, v):
                HID = self.HID

                def add_bias(e, s, use):
                    v.wait_ge(self.h_ready[s], use + 2)
                    for b in range(self.HB):
                        last = v.tensor_tensor(self.hid[:, b * 512:(b + 1) * 512], bank[b][:, :],
                                               self.b1[:, at(e * HID + b * 512, 512)], ALU.add)
                    last.then_inc(self.hid_ready, 1)

                v.wait_ge(self.b_loaded, 32)
                if self.second_norm:
                    self.fold_vector(v)
                e0 = v.value_load(expert_of[0:1, 0:1], min_val=0, max_val=E - 1)
                add_bias(e0, 0, 0)
                with v.Fori(0, RUN_TILES // 2) as i:
                    for s in range(2):
                        o = 1 - s
                        g = 2 * i + s
                        e = v.value_load(expert_of[0:1, at(g + 1, 1)], min_val=0, max_val=E - 1)
                        v.wait_ge(self.th_ready[s], i + 2)
                        add_bias(e, o, i + s)
                        e = v.value_load(expert_of[0:1, at(g, 1)], min_val=0, max_val=E - 1)
                        v.wait_ge(self.y_ready[s], i + 2)
                        v.wait_ge(self.ry_free[s], i + 1)
                        v.tensor_tensor(self.ry[s], bank[5 + s][:, 0:D], self.b2[:, at(e * D, D)], ALU.add
                                        ).then_inc(self.ry_ready[s], 1)

            def fold_scratch(self):
                k = 0
                self.lnb = [self.ht[s][:, 0:KC * P] for s in range(2)]
                self.ln_g = self.hid[:, 0:KC * E]
                self.ln_b = self.hid[:, KC * E:2 * KC * E]

            def fold_sync(self, sp, ln_gm, ln_bm):
                self.fold_scratch()
                sp.dma_start(self.ln_g, ln_gm).then_inc(self.lng_loaded, 16)
                sp.dma_start(self.ln_b, ln_bm).then_inc(self.lng_loaded, 16)

            def fold_tensor(self, pe):
                self.fold_scratch()
                HID = self.HID
                with pe.Fori(0, E // 2) as i:
                    for s in range(2):
                        e = 2 * i + s
                        pe.wait_ge(self.lnb_ready, e + 1)
                        pe.wait_ge(self.fold_used, e + 1)
                        for b in range(self.HB):
                            for k in range(KC):
                                last = pe.matmul(bank[2 * s + b][:, :], self.lnb[s][:, k * P:(k + 1) * P],
                                                 self.W1[:, at(e * (KC * HID) + k * HID + b * 512, 512)],
                                                 start=(k == 0), stop=(k == KC - 1))
                        last.then_inc(self.fold_mm, 1)
                pe.wait_ge(self.fold_used, E + 1)
                pe.wait_ge(self.folded, E)

            def fold_vector(self, v):
                self.fold_scratch()
                HID = self.HID
                v.wait_ge(self.lng_loaded, 32)
                v.wait_ge(self.w_loaded, 16 * 8)

                def shift(e, s):
                    for k in range(KC):
                        last = v.tensor_copy(self.lnb[s][:, k * P:(k + 1) * P],
                                             self.ln_b[:, at(e * KC + k, 1)].to_broadcast([P, P]))
                    last.then_inc(self.lnb_ready, 1)
                with v.Fori(0, E // 2) as i:
                    for s in range(2):
                        shift(2 * i + s, s)
                    for s in range(2):
                        e = 2 * i + s
                        v.wait_ge(self.fold_mm, e + 1)
                        for b in range(self.HB):
                            bv = self.b1[:, at(e * HID + b * 512, 512)]
                            last = v.tensor_tensor(bv, bank[2 * s + b][:, :], bv, ALU.add)
                        last.then_inc(self.fold_used, 1)
                        for k in range(KC):
                            wv = self.W1[:, at(e * (KC * HID) + k * HID, HID)]
                            last = v.tensor_scalar(wv, wv, self.ln_g[:, at(e * KC + k, 1)], None, ALU.mult)
                        last.then_inc(self.folded, 1)
                v.wait_ge(self.folded, E)

            def combine_sync(self, sp):
                sp.dma_start(X[:, :].rearrange("p (t d) -> p t d", d=D), xd.rearrange("(t p) d -> p t d", p=P)
                             ).then_inc(self.x_back, 16)

            GROUPS = ((0, 6), (6, 12), (12, 19), (19, 26))

            def combine_gpsimd(self, pool):
                for g, (lo, hi) in enumerate(self.GROUPS):
                    for t in range(lo, hi):
                        for k in range(2):
                            q = 2 * t + k
                            pool.indirect_dma_start(self.got[:, q * D:(q + 1) * D], None, ys[:, :],
                                                    bass.IndirectOffsetOnAxis(
                                                        ap=slot_of[:, k * T + t:k * T + t + 1], axis=0)
                                                    ).then_inc(self.gathered[g], 16)

            def combine_vector(self, v):
                v.wait_ge(self.x_back, 16)
                for g, (lo, hi) in enumerate(self.GROUPS):
                    v.wait_ge(self.gathered[g], 32 * (hi - lo))
                    for k in range(2):
                        with v.Fori(lo, hi) as t:
                            xv = X[:, at(t * D, D)]
                            v.scalar_tensor_tensor(out=xv, in0=self.got[:, at(t * (2 * D) + k * D, D)],
                                                   scalar=weight_of[:, at(t + k * T, 1)], in1=xv,
                                                   op0=ALU.mult, op1=ALU.add).then_inc(self.sum_step, 1)
                        v.wait_ge(self.sum_step, 2 * lo + (k + 1) * (hi - lo))

        def layer_norm_stats(v, sems, nth=1):
            with v.Fori(0, T) as t:
                v.bn_stats(stats[:, at(t * 6, 6)], X[:, at(t * D, D)]).then_inc(sems.stat, 1)
            v.wait_ge(sems.stat, T * nth)
            st = stats[:, :].rearrange("p (t k) -> p t k", k=6)
            half_sum, half_diff, m2 = mv[:, 0:T], mv[:, T:2 * T], mv[:, 2 * T:3 * T]
            v.tensor_tensor(half_sum, st[:, :, 1], st[:, :, 4], ALU.add).then_inc(sems.aggr, 1)
            v.tensor_tensor(half_diff, st[:, :, 1], st[:, :, 4], ALU.subtract).then_inc(sems.aggr, 1)
            v.tensor_tensor(m2, st[:, :, 2], st[:, :, 5], ALU.add).then_inc(sems.aggr, 1)
            v.wait_ge(sems.aggr, 6 * nth - 3)
            v.tensor_scalar(half_sum, half_sum, 0.5, None, ALU.mult).then_inc(sems.aggr, 1)
            v.scalar_tensor_tensor(out=half_diff, in0=half_diff, scalar=0.25, in1=half_diff, op0=ALU.mult,
                                   op1=ALU.mult).then_inc(sems.aggr, 1)
            v.wait_ge(sems.aggr, 6 * nth - 1)
            v.scalar_tensor_tensor(out=m2, in0=m2, scalar=1.0 / D, in1=half_diff, op0=ALU.mult, op1=ALU.add
                                   ).then_inc(sems.aggr, 1)
            v.wait_ge(sems.aggr, 6 * nth)
            v.tensor_scalar(rstd[:, :], m2, EPS, None, ALU.add).then_inc(sems.var_ready, 1)
            v.wait_ge(sems.sd_ready, nth)
            v.reciprocal(rstd[:, :], rstd[:, :]).then_inc(sems.rstd_ready, 1)
            v.wait_ge(sems.rstd_ready, nth)

        def layer_norm_sqrt(a, sems, nth=1):
            a.wait_ge(sems.var_ready, nth)
            a.activation(rstd[:, :], rstd[:, :], ACT.Sqrt).then_inc(sems.sd_ready, 1)

        x_stored = sem("x_stored")

        def store_sync(sp):
            for g in range(2):
                sp.dma_start(out[g * PAIRS * P:(g + 1) * PAIRS * P, :].rearrange("(t p) d -> p t d", p=P),
                             X[:, g * PAIRS * D:(g + 1) * PAIRS * D].rearrange("p (t d) -> p t d", d=D)
                             ).then_inc(x_stored, 16)
            sp.wait_ge(x_stored, 32)

        xs_clean = sem("xs_clean")
        hand_over()
        A0 = Attention(L0, "a0_")
        a0_sems, a0_ones = hand_over()

        def give_ones(eng, sems):
            for free in sems:
                eng.sem_inc(free, 1)

        with nc.Block() as block:
            @block.sync
            def _(sp):
                loads_sync(sp)
                give_ones(sp, a0_ones[0::2])

            @block.tensor
            def _(pe):
                give_ones(pe, a0_ones[1::2])

            @block.gpsimd
            def _(pool):
                constants_gpsimd(pool)

        with nc.Block() as block:
            @block.sync
            def _(sp):
                A0.values_sync(sp)
                A0.rows_sync(sp)

            @block.gpsimd
            def _(pool):
                mask_loads_gpsimd(pool, A0.bins_gpsimd)

            @block.vector
            def _(v):
                v.wait_ge(x_loaded, 32)
                A0.values_vector(v)
                A0.bins_vector(v)
                A0.count_vector(v)
                A0.rows_vector(v)

            @block.scalar
            def _(a):
                A0.values_scalar(a)
                A0.count_scalar(a)
                A0.rows_scalar(a)

            @block.tensor
            def _(pe):
                A0.values_tensor(pe)
                A0.count_tensor(pe)
                A0.rows_tensor(pe)

        X0 = Experts(512, "x0_", V_AT, 38016, False)
        x0_sems, x0_ones = hand_over()

        with nc.Block() as block:
            @block.sync
            def _(sp):
                A0.attend_sync(sp)
                give_ones(sp, x0_ones)
                sp.dma_start(xs.rearrange("(g p) d -> p g d", p=P),
                             zeros[:, :].bitcast(F32).rearrange("p (o d) -> p o d", o=1)
                             .to_broadcast([P, SLOT_TILES, D])).then_inc(xs_clean, 16)
                sp.wait_ge(xs_clean, 16)

            @block.vector
            def _(v):
                A0.attend_vector(v)
                A0.gelu_vector(v)

            @block.scalar
            def _(a):
                A0.attend_scalar(a)
                A0.gelu_scalar(a)

            @block.tensor
            def _(pe):
                A0.attend_tensor(pe)

        nc.clear_and_free_semaphores(a0_sems)

        def experts_blocks(X_, next_ones, gate_w, gate_b, w1m, b1m, w2m, b2m, ln=None):
            with nc.Block() as block:
                @block.sync
                def _(sp):
                    X_.route_sync(sp, gate_w, gate_b, w1m, w2m)

                @block.gpsimd
                def _(pool):
                    X_.route_gpsimd(pool)

                @block.vector
                def _(v):
                    X_.route_vector(v)

                @block.scalar
                def _(a):
                    X_.route_scalar(a)

                @block.tensor
                def _(pe):
                    X_.route_tensor(pe)

            with nc.Block() as block:
                @block.sync
                def _(sp):
                    if ln is not None:
                        X_.fold_sync(sp, *ln)
                    X_.tiles_sync(sp, b1m, b2m)

                @block.gpsimd
                def _(pool):
                    X_.tiles_gpsimd(pool)

                @block.vector
                def _(v):
                    X_.tiles_vector(v)

                @block.scalar
                def _(a):
                    X_.tiles_scalar(a)

                @block.tensor
                def _(pe):
                    X_.tiles_tensor(pe)

            with nc.Block() as block:
                @block.sync
                def _(sp):
                    X_.combine_sync(sp)
                    give_ones(sp, next_ones)

                @block.gpsimd
                def _(pool):
                    X_.combine_gpsimd(pool)

                @block.vector
                def _(v):
                    X_.combine_vector(v)

        A1 = Attention(L1, "a1_")
        a1_sems, a1_ones = hand_over()
        experts_blocks(X0, a1_ones, gate0, gate_b0, m0w1, m0b1, m0w2, m0b2)

        nc.clear_and_free_semaphores(x0_sems)
        X1 = Experts(1024, "x1_", 0, 32768, True)
        x1_sems, x1_ones = hand_over()
        with nc.Block() as block:
            @block.sync
            def _(sp):
                A1.values_sync(sp)
                A1.rows_sync(sp)

            @block.gpsimd
            def _(pool):
                A1.bins_gpsimd(pool)

            @block.vector
            def _(v):
                A1.values_vector(v)
                A1.bins_vector(v)
                A1.count_vector(v)
                A1.rows_vector(v)

            @block.scalar
            def _(a):
                A1.values_scalar(a)
                A1.count_scalar(a)
                A1.rows_scalar(a)

            @block.tensor
            def _(pe):
                A1.values_tensor(pe)
                A1.count_tensor(pe)
                A1.rows_tensor(pe)

        with nc.Block() as block:
            @block.sync
            def _(sp):
                A1.attend_sync(sp)
                give_ones(sp, x1_ones)

            @block.vector
            def _(v):
                A1.attend_vector(v)

            @block.scalar
            def _(a):
                A1.attend_scalar(a)

            @block.tensor
            def _(pe):
                A1.attend_tensor(pe)

        nc.clear_and_free_semaphores(a1_sems)
        experts_blocks(X1, [], gate1, gate_b1, m1w1, m1b1, m1w2, m1b2, (ln_g1, ln_b1))

        with nc.Block() as block:
            @block.sync
            def _(sp):
                store_sync(sp)


def kernel(x, adj, L0_gnn_W, L0_gnn_r, L0_ffn_gate_w, L0_ffn_gate_b, L0_ffn_W1, L0_ffn_b1, L0_ffn_W2, L0_ffn_b2,
           L1_gnn_weight, L1_gnn_weight_u, L1_gnn_weight_v, L1_gnn_bias, L1_gnn_proj_w, L1_gnn_proj_b,
           L1_ffn_Wr, L1_ffn_br, L1_ffn_ln_g, L1_ffn_ln_b, L1_ffn_W1, L1_ffn_b1, L1_ffn_W2, L1_ffn_b2):
    import numpy as np
    import concourse.bacc as bacc
    from concourse.bass_utils import run_bass_kernel_spmd as run

    x = np.asarray(x)
    xp = np.zeros((NP, D), x.dtype)
    xp[:NODES] = x
    adjT = np.zeros((NP, NP), np.int32)
    adjT[:NODES, :NODES] = np.asarray(adj).T
    for n in range(NODES, NP):
        adjT[n, n] = 1
    w0 = np.asarray(L0_gnn_W)
    r0 = np.asarray(L0_gnn_r).reshape(2, D)
    w1 = np.asarray(L1_gnn_weight)
    uv = np.zeros((D, 8), w1.dtype)
    for h in range(4):
        uv[h * 64:(h + 1) * 64, h] = np.asarray(L1_gnn_weight_u)[h, :, 0]
        uv[h * 64:(h + 1) * 64, 4 + h] = np.asarray(L1_gnn_weight_v)[h, :, 0]
    arrays = {
        "x_in": xp, "adjT": adjT, "w0T": w0.T, "w0": w0, "r0": r0[::-1].T,
        "w1": w1, "w1T": w1.T, "uv1": uv, "proj_wT": np.asarray(L1_gnn_proj_w).T,
        "bias1": np.asarray(L1_gnn_bias).reshape(D), "proj_b1": np.asarray(L1_gnn_proj_b).reshape(D),
    }

    def up(w):
        w = np.asarray(w)
        return w.reshape(E, KC, P, -1).transpose(2, 0, 1, 3).reshape(P, -1)

    def down(w):
        w = np.asarray(w)
        return w.reshape(E, -1, P, D).transpose(2, 0, 1, 3).reshape(P, -1)

    def cols(w):
        return np.asarray(w).reshape(E, KC, P).transpose(2, 0, 1).reshape(P, -1)

    arrays.update({
        "gate0": np.asarray(L0_ffn_gate_w), "gate_b0": np.asarray(L0_ffn_gate_b),
        "m0w1": up(L0_ffn_W1), "m0b1": np.asarray(L0_ffn_b1).reshape(-1),
        "m0w2": down(L0_ffn_W2), "m0b2": np.asarray(L0_ffn_b2).reshape(-1),
        "gate1": np.asarray(L1_ffn_Wr), "gate_b1": np.asarray(L1_ffn_br),
        "ln_g1": cols(L1_ffn_ln_g), "ln_b1": cols(L1_ffn_ln_b),
        "m1w1": up(L1_ffn_W1), "m1b1": np.asarray(L1_ffn_b1).reshape(-1),
        "m1w2": down(L1_ffn_W2), "m1b2": np.asarray(L1_ffn_b2).reshape(-1),
    })
    arrays = {k: np.ascontiguousarray(a) for k, a in arrays.items()}
    nc = bacc.Bacc("TRN2", target_bir_lowering=False, num_devices=1)
    args = {k: nc.dram_tensor(k, a.shape, mybir.dt.from_np(a.dtype), kind="ExternalInput").ap()
            for k, a in arrays.items()}
    out = nc.dram_tensor("out", (NP, D), F32, kind="ExternalOutput").ap()
    qd = nc.dram_tensor("qd", (3 * 4 * T, P), F32, kind="Internal").ap()
    xd = nc.dram_tensor("xd", (NP, D), F32, kind="Internal").ap()
    xs = nc.dram_tensor("xs", (SLOT_TILES * P, D), F32, kind="Internal").ap()
    ys = nc.dram_tensor("ys", (RUN_TILES * P, D), F32, kind="Internal").ap()
    program(nc, out=out, qd=qd, xd=xd, xs=xs, ys=ys, **args)
    r = run(nc, [arrays], core_ids=[0])
    return r.results[0]["out"][:NODES]
```

```python
from contextlib import ExitStack

import concourse.bass as bass
from concourse import mybir

ALU = mybir.AluOpType
ACT = mybir.ActivationFunctionType
F32 = mybir.dt.float32
BF16 = mybir.dt.bfloat16
U8 = mybir.dt.uint8
I8 = mybir.dt.int8
U32 = mybir.dt.uint32
F8 = mybir.dt.float8e4
I32 = mybir.dt.int32
AXX = mybir.AxisListType.X

P = 128
NODES = 3327
T = 26
NP = T * P
D = 256
KC = D // P
VW = 260
E = 8
EPS = 1e-5
SLOPE = 0.2
PAIRS = T // 2
RUN_TILES = 2 * T + 8
SLOT_TILES = RUN_TILES + 2

MASK_AT = 0
MASK_WORDS = NP * T // 4
V_AT = MASK_AT + MASK_WORDS
WORK_AT = V_AT + T * VW
ARENA = 44184
QUICK_REACH = 60.0


def at(start, size):
    return bass.ds(start, size)


class Layer:

    def __init__(self, heads, bins, width):
        self.H = heads
        self.HD = D // heads
        self.B = bins
        self.W = width
        self.NQ = 3 if heads > 1 else 2
        self.blocks = NP // width
        self.tail = NP - self.blocks * width
        assert self.blocks % 2 == 0 and self.tail == 2 * P


L0 = Layer(1, 64, 512)
L1 = Layer(4, 32, 384)


def program(nc, x_in, adjT, w0T, w0, r0, w1, w1T, uv1, proj_wT, bias1, proj_b1,
            gate0, gate_b0, m0w1, m0b1, m0w2, m0b2, gate1, gate_b1, ln_g1, ln_b1, m1w1, m1b1, m1w2, m1b2,
            qd, xd, xs, out):
    ctx = ExitStack()
    with ctx:
        def sb(name, shape, dt=F32):
            return ctx.enter_context(nc.sbuf_tensor(name, shape, dt))

        def sem(name):
            held.append(nc.alloc_semaphore(name=name))
            return held[-1]

        held = []

        def hand_over():
            got, ones_ = list(held), list(start_at_one)
            held.clear()
            start_at_one.clear()
            return got, ones_

        bank = [ctx.enter_context(nc.psum_tensor(f"bank{i}", [P, 512], F32)) for i in range(8)]

        X = sb("X", [P, T * D])
        arena = sb("arena", [P, ARENA])

        def words(start, n):
            return arena[:, start:start + n]

        mask = words(MASK_AT, MASK_WORDS).bitcast(U8)
        V = words(V_AT, T * VW)

        ident = sb("ident", [P, P])
        zeros = sb("zeros", [P, 512], BF16)
        bin_no = sb("bin_no", [P, 64])
        stats = sb("stats", [P, T * 6])
        mv = sb("mv", [P, T * 3])
        rstd = sb("rstd", [P, T])
        s_all = sb("s_all", [P, 2 * 4 * T])
        reach = sb("reach", [P, 8])
        reach_all = sb("reach_all", [P, 8])
        bin_w = sb("bin_w", [P, 4])
        s_min = sb("s_min", [P, 4])
        top_add = sb("top_add", [P, 4])
        edges = sb("edges", [P, 128])
        found = sb("found", [P, 4 * T])
        m_row = sb("m_row", [P, 4 * T])
        q_cols = sb("q_cols", [P, 3 * 4 * T])
        d_all = sb("d_all", [P, 4 * T])
        neg_sj = sb("neg_sj", [P, 4 * T])
        far = sb("far", [P, 1])
        is_far = sb("is_far", [P, 1], I32)
        ones = sb("ones", [P, P], BF16)
        earlier = sb("earlier", [P, P], BF16)
        order8 = sb("order8", [P, E])
        fill_at = sb("fill_at", [P, T])
        tile_no = sb("tile_no", [P, SLOT_TILES])
        ones_t = sb("ones_t", [P, T])
        row_id = sb("row_id", [P, T])
        spare_row = sb("spare_row", [P, 1])
        slot_row = sb("slot_row", [P, SLOT_TILES], I32)
        expert_of = sb("expert_of", [1, SLOT_TILES], I32)
        slot_w = sb("slot_w", [P, SLOT_TILES])
        den = sb("den", [P, 16])
        rden = sb("rden", [P, 16])

        start_at_one = []

        x_loaded = sem("x_loaded")
        const_ready = sem("const_ready")
        mask_loaded = [sem("mask_loaded0"), sem("mask_loaded1")]

        def loads_sync(sp):
            for g in range(2):
                sp.dma_start(X[:, g * PAIRS * D:(g + 1) * PAIRS * D].rearrange("p (t d) -> p t d", d=D),
                             x_in[g * PAIRS * P:(g + 1) * PAIRS * P, :].rearrange("(t p) d -> p t d", p=P)
                             ).then_inc(x_loaded, 16)

        mask_scaled = sem("mask_scaled")
        spare_clean = sem("spare_clean")
        id_zero = sem("id_zero")
        tri_base = sem("tri_base")

        def constants_gpsimd(pool):
            pool.memset(ident[:, :], 0.0).then_inc(id_zero, 1)
            pool.wait_ge(id_zero, 1)
            pool.affine_select(out=ident[:, :], in_=ident[:, :], compare_op=ALU.not_equal, fill=1.0, base=0,
                               pattern=[[-1, P]], channel_multiplier=1).then_inc(const_ready, 1)
            pool.memset(zeros[:, :], 0.0).then_inc(const_ready, 1)
            pool.iota(bin_no[:, :], [[1, 64]], base=0, channel_multiplier=0,
                      allow_small_or_imprecise_dtypes=True).then_inc(const_ready, 1)
            pool.memset(ones[:, :], 1.0).then_inc(tri_base, 1)
            pool.memset(earlier[:, :], 1.0).then_inc(tri_base, 1)
            pool.wait_ge(tri_base, 2)
            pool.affine_select(out=earlier[:, :], in_=earlier[:, :], compare_op=ALU.is_gt, fill=0.0, base=0,
                               pattern=[[1, P]], channel_multiplier=-1).then_inc(const_ready, 1)
            pool.iota(order8[:, :], [[-1, E]], base=E, channel_multiplier=0,
                      allow_small_or_imprecise_dtypes=True).then_inc(const_ready, 1)
            pool.iota(fill_at[:, :], [[P, T]], base=0, channel_multiplier=0,
                      allow_small_or_imprecise_dtypes=True).then_inc(const_ready, 1)
            pool.iota(tile_no[:, :], [[1, SLOT_TILES]], base=0, channel_multiplier=0,
                      allow_small_or_imprecise_dtypes=True).then_inc(const_ready, 1)
            pool.memset(ones_t[:, :], 1.0).then_inc(const_ready, 1)
            pool.iota(row_id[:, :], [[P, T]], base=1, channel_multiplier=1,
                      allow_small_or_imprecise_dtypes=True).then_inc(const_ready, 1)
            pool.iota(spare_row[:, :], [[1, 1]], base=NP + 1, channel_multiplier=1,
                      allow_small_or_imprecise_dtypes=True).then_inc(const_ready, 1)
        CONSTS = 10

        def mask_loads_gpsimd(pool, between):
            def load(pair, slot):
                for half in range(2):
                    c = 2 * pair + half
                    pool.dma_start(mask[:, at(c * NP, NP)].rearrange("p (a n) -> p a n", a=2),
                                   adjT[at(c * P, P), :].rearrange("p (a n) -> p a n", a=2)
                                   ).then_inc(mask_loaded[slot], 16)
            load(0, 0)
            load(1, 1)
            for first, last in ((0, 3), (3, 5)):
                with pool.Fori(first, last) as g:
                    for slot in range(2):
                        pool.wait_ge(mask_loaded[slot], 32 * g + 32)
                        load(2 * g + 2 + slot, slot)
                if first == 0:
                    between(pool)
            pool.wait_ge(mask_loaded[0], 32 * 6)
            load(12, 0)

        class Attention:
            def __init__(self, L, tag):
                self.L, self.tag = L, tag
                H, B = L.H, L.B
                k = WORK_AT
                self.w_cols = H * L.HD + 2 * H
                self.wmat = words(k, KC * self.w_cols)
                k += KC * self.w_cols
                self.wT = words(k, KC * D)
                k += KC * D
                self.attn_vec = words(k, KC * 2 * H)
                k += KC * 2 * H
                self.proj = words(k, KC * D)
                k += KC * D
                self.pbias = words(k, 2 * D)
                k += 2 * D
                self.xn = [words(k + s * D, D) for s in range(2)]
                k += 2 * D
                self.xt = [words(k + s * D, D) for s in range(2)]
                k += 2 * D
                self.conv = [words(k + s * NP // 2, NP // 2).bitcast(BF16) for s in range(2)]
                k += NP
                self.above = words(k, T * H * B // 2).bitcast(BF16)
                k += T * H * B // 2
                self.cpos = words(k, T * H * B)
                k += T * H * B
                self.qt = words(k, L.NQ * P)
                k += L.NQ * P
                assert k <= ARENA, (tag, k)
                k = WORK_AT
                RW = L.NQ * H * L.W
                self.rows = [words(k + r * RW, RW) for r in range(2)]
                k += 2 * RW
                self.prob = [words(k + s * H * L.W, H * L.W) for s in range(2)]
                k += 2 * H * L.W
                if H > 1:
                    self.live = [words(k + s * H * L.W // 4, H * L.W // 4).bitcast(U8) for s in range(2)]
                    k += 2 * H * L.W // 4
                else:
                    self.attn_out = words(k, T * D)
                    k += T * D
                assert k <= ARENA, (tag, k)
                self.nt = L.W // P
                if H > 1:
                    self.exp_bank = [bank[4 + h] for h in range(4)]
                else:
                    self.exp_bank = [bank[4], bank[5]]
                self.w_loaded = sem(tag + "w_loaded")
                self.stat = sem(tag + "stat")
                self.aggr = sem(tag + "aggr")
                self.var_ready = sem(tag + "var_ready")
                self.sd_ready = sem(tag + "sd_ready")
                self.rstd_ready = sem(tag + "rstd_ready")
                self.wvec_ready = sem(tag + "wvec_ready")
                self.wvec_copied = sem(tag + "wvec_copied")
                self.v_done = sem(tag + "v_done")
                self.reach_part = sem(tag + "reach_part")
                self.reach_ready = sem(tag + "reach_ready")
                self.bin_steps = sem(tag + "bin_steps")
                self.far_steps = sem(tag + "far_steps")
                self.edge_ready = sem(tag + "edge_ready")
                self.above_ready = sem(tag + "above_ready")
                self.cnt_zero = sem(tag + "cnt_zero")
                self.cnt_done = sem(tag + "cnt_done")
                self.cpos_done = sem(tag + "cpos_done")
                self.found_done = sem(tag + "found_done")
                self.top_done = sem(tag + "top_done")
                self.m_steps = sem(tag + "m_steps")
                self.exps = sem(tag + "exps")
                self.qt_ready = sem(tag + "qt_ready")
                self.qt_copied = sem(tag + "qt_copied")
                self.q_stored = sem(tag + "q_stored")
                self.pb = sem(tag + "pb")
                self.xn_ready = [sem(f"{tag}xn_ready{s}") for s in range(2)]
                self.tp_ready = [sem(f"{tag}tp_ready{s}") for s in range(2)]
                self.xt_ready = [sem(f"{tag}xt_ready{s}") for s in range(2)]
                self.vp_ready = [sem(f"{tag}vp_ready{s}") for s in range(2)]
                self.vp_free = [sem(f"{tag}vp_free{s}") for s in range(2)]
                self.conv_a = [sem(f"{tag}conv_a{s}") for s in range(2)]
                self.conv_v = [sem(f"{tag}conv_v{s}") for s in range(2)]
                self.conv_used = [sem(f"{tag}conv_used{s}") for s in range(2)]
                self.before_attend = list(held)
                self.rows_loaded = [sem(f"{tag}rows_loaded{s}") for s in range(2)]
                self.rows_free = [sem(f"{tag}rows_free{s}") for s in range(2)]
                self.prob_ready = [sem(f"{tag}prob_ready{s}") for s in range(2)]
                self.prob_used = [sem(f"{tag}prob_used{s}") for s in range(2)]
                n_exp = len(self.exp_bank)
                self.exp_ready = [sem(f"{tag}exp_ready{k}") for k in range(n_exp)]
                self.exp_used = [sem(f"{tag}exp_used{k}") for k in range(n_exp)]
                self.live_ready = sem(tag + "live_ready")
                self.acc_free = sem(tag + "acc_free")
                self.b_done = sem(tag + "b_done")
                self.out_ready = sem(tag + "out_ready")
                start_at_one.extend(self.tp_ready + self.vp_ready + self.xt_ready + self.vp_free + self.conv_used
                                    + self.rows_free + self.exp_used + self.prob_used + [self.acc_free])

            def scol(self, which, h):
                k = (which * self.L.H + h) * T
                return s_all[:, k:k + T]

            def values_sync(self, sp):
                wc = self.w_cols
                mats = [(w0T, w0, r0), (w1, w1T, uv1)][self.L.H > 1]
                nw = self.L.H * self.L.HD
                sp.dma_start(self.wmat.rearrange("p (k n) -> p k n", n=wc)[:, :, 0:nw],
                             mats[0].rearrange("(k p) n -> p k n", p=P)).then_inc(self.w_loaded, 16)
                sp.dma_start(self.wT.rearrange("p (k n) -> p k n", n=D),
                             mats[1].rearrange("(k p) n -> p k n", p=P)).then_inc(self.w_loaded, 16)
                sp.dma_start(self.attn_vec.rearrange("p (k n) -> p k n", k=KC),
                             mats[2].rearrange("(k p) n -> p k n", p=P)).then_inc(self.w_loaded, 16)
                self.w_all = 48
                if self.L.H > 1:
                    sp.dma_start(self.proj.rearrange("p (k n) -> p k n", n=D),
                                 proj_wT.rearrange("(k p) n -> p k n", p=P)).then_inc(self.w_loaded, 16)
                    sp.dma_start(self.pbias[:, 0:D], bias1.partition_broadcast(P)).then_inc(self.w_loaded, 16)
                    sp.dma_start(self.pbias[:, D:2 * D], proj_b1.partition_broadcast(P)).then_inc(self.w_loaded, 16)
                    self.w_all = 96

            def values_vector(self, v):
                L, H = self.L, self.L.H
                layer_norm_stats(v, self)
                v.wait_ge(self.wvec_ready, 1)
                nw = H * L.HD
                v.tensor_copy(self.wmat.rearrange("p (k n) -> p k n", k=KC)[:, :, nw:],
                              bank[4][:, 0:KC * 2 * H].rearrange("p (k n) -> p k n", k=KC)
                              ).then_inc(self.wvec_copied, 1)
                if H > 1:
                    v.memset(V.rearrange("p (c n) -> p c n", n=65)[:, :, 64:65], 1.0)
                    v.tensor_tensor(self.pbias[:, 0:D], self.pbias[:, 0:D], self.pbias[:, D:2 * D],
                                    ALU.add).then_inc(self.pb, 1)
                    v.wait_ge(self.pb, 1)
                else:
                    v.memset(V.rearrange("p (c n) -> p c n", n=VW)[:, :, D:D + 1], 1.0)
                s_cols = s_all[:, 0:2 * H * T].rearrange("p (q t) -> p t q", t=T)
                with v.Fori(0, PAIRS) as i:
                    for s in range(2):
                        t = 2 * i + s
                        v.wait_ge(self.tp_ready[s], i + 1)
                        v.tensor_scalar(self.xn[s], X[:, at(t * D, D)], mv[:, at(t, 1)], rstd[:, at(t, 1)],
                                        ALU.subtract, ALU.mult).then_inc(self.xn_ready[s], 1)
                    for s in range(2):
                        t = 2 * i + s
                        vb = bank[2 + s]
                        v.wait_ge(self.vp_ready[s], i + 1 + 1)
                        if H > 1:
                            v.tensor_copy(V[:, at(t * VW, VW)].rearrange("p (h n) -> p h n", n=65)[:, :, 0:64],
                                          vb[:, 0:D].rearrange("p (h n) -> p h n", n=64))
                            v.tensor_tensor(X[:, at(t * D, D)], X[:, at(t * D, D)], self.pbias[:, 0:D],
                                            ALU.add).then_inc(self.pb, 1)
                            v.wait_ge(self.pb, t + 2)
                            v.tensor_tensor(X[:, at(t * D, D)], bank[5 + s][:, 0:D], X[:, at(t * D, D)], ALU.add)
                        else:
                            v.tensor_copy(V[:, at(t * VW, D)], vb[:, 0:D])
                        v.tensor_copy(s_cols[:, at(t, 1), :], vb[:, D:D + 2 * H].rearrange("p (o q) -> p o q", o=1)
                                      ).then_inc(self.vp_free[s], 1)

            def values_scalar(self, a):
                layer_norm_sqrt(a, self)
                with a.Fori(0, PAIRS) as i:
                    for s in range(2):
                        a.wait_ge(self.tp_ready[s], i + 1 + 1)
                        a.wait_ge(self.vp_ready[s], i + 1)
                        a.copy(self.xt[s], bank[s][:, 0:D]).then_inc(self.xt_ready[s], 1)

            def values_tensor(self, pe):
                L, H = self.L, self.L.H
                pe.wait_ge(const_ready, CONSTS)
                pe.wait_ge(self.w_loaded, 48 if H == 1 else 96)
                for k in range(KC):
                    for o in range(KC):
                        last = pe.matmul(bank[4][:, k * 2 * H:(k + 1) * 2 * H],
                                         self.wT[:, o * D + k * P:o * D + k * P + P],
                                         self.attn_vec[:, o * 2 * H:(o + 1) * 2 * H],
                                         start=(o == 0), stop=(o == KC - 1))
                last.then_inc(self.wvec_ready, 1)
                pe.wait_ge(self.wvec_copied, 1)
                with pe.Fori(0, PAIRS) as i:
                    for s in range(2):
                        pe.wait_ge(self.xn_ready[s], i + 1)
                        pe.wait_ge(self.xt_ready[s], i + 1)
                        for k in range(KC):
                            last = pe.transpose(bank[s][:, k * P:(k + 1) * P], self.xn[s][:, k * P:(k + 1) * P],
                                                ident[:, :])
                        last.then_inc(self.tp_ready[s], 1)
                    for s in range(2):
                        pe.wait_ge(self.xt_ready[s], i + 1 + 1)
                        pe.wait_ge(self.vp_free[s], i + 1)
                        if H > 1:
                            for k in range(KC):
                                pe.matmul(bank[5 + s][:, 0:D], self.xt[s][:, k * P:(k + 1) * P],
                                          self.proj[:, k * D:(k + 1) * D], start=(k == 0), stop=(k == KC - 1))
                        for k in range(KC):
                            last = pe.matmul(bank[2 + s][:, 0:self.w_cols], self.xt[s][:, k * P:(k + 1) * P],
                                             self.wmat[:, k * self.w_cols:(k + 1) * self.w_cols],
                                             start=(k == 0), stop=(k == KC - 1))
                        last.then_inc(self.vp_ready[s], 1)

            def bins_vector(self, v):
                L, H, B = self.L, self.L.H, self.L.B
                sj = s_all[:, 0:H * T].rearrange("p (h t) -> p h t", t=T)
                for s in range(2):
                    v.wait_ge(self.vp_free[s], PAIRS + 1)
                v.tensor_reduce(reach[:, 0:H], sj, AXX, ALU.max).then_inc(self.reach_part, 1)
                v.tensor_reduce(reach[:, H:2 * H], sj, AXX, ALU.min, negate=True).then_inc(self.reach_part, 1)
                if H > 1:
                    v.tensor_scalar(neg_sj[:, 0:H * T], s_all[:, 0:H * T], -1.0, None, ALU.mult)
                v.wait_ge(self.reach_ready, 1)
                if H > 1:
                    v.tensor_reduce(far[:, :], reach_all[:, 0:2 * H], AXX, ALU.max).then_inc(self.far_steps, 1)
                    v.wait_ge(self.far_steps, 1)
                    v.tensor_scalar(is_far[:, :], far[:, :], QUICK_REACH, None, ALU.is_ge)
                v.tensor_tensor(bin_w[:, 0:H], reach_all[:, 0:H], reach_all[:, H:2 * H], ALU.add
                                ).then_inc(self.bin_steps, 1)
                v.tensor_scalar(s_min[:, 0:H], reach_all[:, H:2 * H], -1.0, None, ALU.mult
                                ).then_inc(self.bin_steps, 1)
                v.wait_ge(self.bin_steps, 2)
                v.tensor_scalar(bin_w[:, 0:H], bin_w[:, 0:H], 1.0 / B, None, ALU.mult).then_inc(self.bin_steps, 1)
                v.wait_ge(self.bin_steps, 3)
                v.scalar_tensor_tensor(out=top_add[:, 0:H], in0=bin_w[:, 0:H], scalar=0.125, in1=s_min[:, 0:H],
                                       op0=ALU.mult, op1=ALU.add).then_inc(self.bin_steps, 1)
                v.wait_ge(const_ready, CONSTS)
                for h in range(H):
                    v.tensor_scalar(edges[:, h * B:(h + 1) * B], bin_no[:, 0:B], bin_w[:, h:h + 1], s_min[:, h:h + 1],
                                    ALU.mult, ALU.add).then_inc(self.edge_ready, 1)
                v.wait_ge(self.edge_ready, H)
                e3 = edges[:, 0:H * B].rearrange("p (h b) -> p h b", b=B)
                with v.Fori(0, T) as t:
                    v.tensor_tensor(self.above[:, at(t * H * B, H * B)].rearrange("p (h b) -> p h b", b=B),
                                    sj[:, :, at(t, 1)].to_broadcast([P, H, B]), e3, ALU.is_ge
                                    ).then_inc(self.above_ready, 1)

            def bins_gpsimd(self, pool):
                H = self.L.H
                pool.wait_ge(self.reach_part, 2)
                pool.partition_all_reduce(reach_all[:, 0:2 * H], reach[:, 0:2 * H], P, bass.bass_isa.ReduceOp.max
                                          ).then_inc(self.reach_ready, 1)

            CA = 1792

            def count_pairs(self, eng, body):
                with eng.Fori(0, PAIRS // 2) as g:
                    for half in range(2):
                        body(2 * g + half, g, half)
                body(PAIRS - 1, PAIRS // 2, 0)

            def count_scalar(self, a):
                def body(pair, g, half):
                    a.wait_ge(mask_loaded[half], 32 * (g + 1))
                    for s in range(2):
                        a.wait_ge(self.conv_used[s], pair + 1)
                        a.copy(self.conv[s][:, 0:self.CA], mask[:, at((2 * pair + s) * NP, self.CA)]
                               ).then_inc(self.conv_a[s], 1)
                self.count_pairs(a, body)

            def count_vector(self, v):
                def body(pair, g, half):
                    v.wait_ge(mask_loaded[half], 32 * (g + 1))
                    for s in range(2):
                        v.wait_ge(self.conv_used[s], pair + 1)
                        v.tensor_copy(self.conv[s][:, self.CA:NP],
                                      mask[:, at((2 * pair + s) * NP + self.CA, NP - self.CA)]
                                      ).then_inc(self.conv_v[s], 1)
                self.count_pairs(v, body)

            def count_tensor(self, pe):
                H, B = self.L.H, self.L.B
                HB = H * B
                per = 512 // HB
                nb = -(-T // per)
                pe.wait_ge(self.edge_ready, H)
                for b in range(nb):
                    pe.matmul(bank[b][:, :], zeros[:, 0:P], zeros[:, :], start=True, stop=True)
                pe.wait_ge(self.above_ready, T)
                with pe.Fori(0, PAIRS) as pair:
                    for s in range(2):
                        pe.wait_ge(self.conv_a[s], pair + 1)
                        pe.wait_ge(self.conv_v[s], pair + 1)
                        for t in range(T):
                            last = pe.matmul(bank[t // per][:, t % per * HB:(t % per + 1) * HB],
                                             self.conv[s][:, t * P:(t + 1) * P],
                                             self.above[:, at((2 * pair + s) * HB, HB)],
                                             start=False, stop=False, skip_group_check=True)
                        last.then_inc(self.conv_used[s], 1)

            def rows_vector(self, v):
                L, H, B = self.L, self.L.H, self.L.B
                HB, HT = H * B, H * T
                per = 512 // HB
                nb = -(-T // per)
                for s in range(2):
                    v.wait_ge(self.conv_used[s], PAIRS + 1)
                for b in range(nb):
                    n = min(per, T - b * per) * HB
                    v.tensor_scalar(self.cpos[:, b * per * HB:b * per * HB + n], bank[b][:, 0:n], 0.0, None, ALU.is_gt
                                    ).then_inc(self.cpos_done, 1)
                v.wait_ge(self.cpos_done, nb)
                f3 = found[:, 0:HT].rearrange("p (h t) -> p h t", t=T)
                for h in range(H):
                    v.tensor_reduce(f3[:, h, :], self.cpos.rearrange("p (t h b) -> p h t b", h=H, b=B)[:, h, :, :],
                                    AXX, ALU.add).then_inc(self.found_done, 1)
                v.wait_ge(self.found_done, H)
                for h in range(H):
                    v.tensor_scalar(m_row[:, h * T:(h + 1) * T], found[:, h * T:(h + 1) * T], bin_w[:, h:h + 1],
                                    top_add[:, h:h + 1], ALU.mult, ALU.add).then_inc(self.top_done, 1)
                v.wait_ge(self.top_done, H)
                si = s_all[:, HT:2 * HT]
                m = m_row[:, 0:HT]
                v.tensor_tensor(m, si, m, ALU.add).then_inc(self.m_steps, 1)
                v.wait_ge(self.m_steps, 1)
                v.scalar_tensor_tensor(out=found[:, 0:HT], in0=m, scalar=SLOPE, in1=m, op0=ALU.mult, op1=ALU.max
                                       ).then_inc(self.m_steps, 1)
                v.wait_ge(self.m_steps, 2)
                v.tensor_tensor(q_cols[:, 0:HT], si, found[:, 0:HT], ALU.subtract).then_inc(self.m_steps, 1)
                v.scalar_tensor_tensor(out=q_cols[:, HT:2 * HT], in0=si, scalar=SLOPE, in1=found[:, 0:HT],
                                       op0=ALU.mult, op1=ALU.subtract).then_inc(self.m_steps, 1)
                if H > 1:
                    v.tensor_copy(q_cols[:, 2 * HT:3 * HT], si).then_inc(self.m_steps, 1)
                for q in range(L.NQ):
                    v.wait_ge(self.qt_ready, q + 1)
                    last = v.tensor_copy(self.qt[0:HT, q * P:(q + 1) * P], bank[q][0:HT, 0:P]
                                         ).then_inc(self.qt_copied, 1)

            def rows_scalar(self, a):
                HT = self.L.H * T
                a.activation(d_all[:, 0:HT], s_all[:, 0:HT], ACT.Exp, scale=SLOPE)
                a.wait_ge(self.m_steps, 4 if self.L.H == 1 else 5)
                a.activation(q_cols[:, HT:2 * HT], q_cols[:, HT:2 * HT], ACT.Exp).then_inc(self.exps, 1)

            def rows_tensor(self, pe):
                HT = self.L.H * T
                pe.wait_ge(self.exps, 1)
                pe.wait_ge(self.cpos_done, 1)
                for q in range(self.L.NQ):
                    pe.transpose(bank[q][0:HT, 0:P], q_cols[:, q * HT:(q + 1) * HT], ident[:, :]
                                 ).then_inc(self.qt_ready, 1)

            def rows_sync(self, sp):
                HT = self.L.H * T
                sp.wait_ge(self.qt_copied, self.L.NQ)
                sp.dma_start(qd[0:self.L.NQ * HT, :].rearrange("(q r) p -> r q p", r=HT),
                             self.qt[0:HT, :].rearrange("r (q p) -> r q p", p=P)).then_inc(self.q_stored, 16)
                sp.wait_ge(self.q_stored, 16)

            def each_block(self, eng, body):
                with eng.Fori(0, self.L.blocks // 2) as bp:
                    for r in range(2):
                        body(2 * bp + r, bp, r, self.nt)
                body(self.L.blocks, self.L.blocks // 2, 0, self.L.tail // P)

            def attend_sync(self, sp):
                L = self.L
                q_all = qd[0:L.NQ * L.H * T, :].rearrange("(r t) p -> r (t p)", t=T)

                def body(b, bp, r, nt):
                    sp.wait_ge(self.rows_free[r], bp + 1)
                    w = nt * P
                    sp.dma_start(self.rows[r].rearrange("p (q w) -> p q w", w=L.W)[:, :, 0:w],
                                 q_all[:, at(b * L.W, w)].partition_broadcast(P)).then_inc(self.rows_loaded[r], 16)
                self.each_block(sp, body)

            def exp_slot(self, s, h, b, i):
                if self.L.H > 1:
                    return h, b * T + 2 * i + s
                return s, b * PAIRS + i

            def attend_scalar(self, a):
                L, H = self.L, self.L.H

                def body(b, bp, r, nt):
                    a.wait_ge(self.rows_loaded[r], 16 * (bp + 1))
                    with a.Fori(0, PAIRS) as i:
                        for s in range(2):
                            for h in range(H):
                                k, used = self.exp_slot(s, h, b, i)
                                a.wait_ge(self.exp_used[k], used + 1)
                                a.activation(self.exp_bank[k][:, 0:nt * P], self.rows[r][:, h * L.W:h * L.W + nt * P],
                                             ACT.Exp, bias=s_all[:, at(h * T + 2 * i + s, 1)]
                                             ).then_inc(self.exp_ready[k], 1)
                self.each_block(a, body)

            def attend_vector(self, v):
                L, H, W = self.L, self.L.H, self.L.W

                def body(b, bp, r, nt):
                    w = nt * P
                    rows = self.rows[r]
                    with v.Fori(0, PAIRS) as i:
                        for s in range(2):
                            c = 2 * i + s
                            v.wait_ge(self.prob_used[s], b * PAIRS + i + 1)
                            for h in range(H):
                                k, used = self.exp_slot(s, h, b, i)
                                v.wait_ge(self.exp_ready[k], used + 1)
                                v.scalar_tensor_tensor(
                                    out=self.prob[s][:, h * W:h * W + w], in0=rows[:, (H + h) * W:(H + h) * W + w],
                                    scalar=d_all[:, at(h * T + c, 1)], in1=self.exp_bank[k][:, 0:w],
                                    op0=ALU.mult, op1=ALU.max).then_inc(self.exp_used[k], 1)
                                if H > 1:
                                    v.scalar_tensor_tensor(
                                        out=self.live[s][:, h * W:h * W + w],
                                        in0=rows[:, (2 * H + h) * W:(2 * H + h) * W + w],
                                        scalar=neg_sj[:, at(h * T + c, 1)], in1=mask[:, at(c * NP + b * W, w)],
                                        op0=ALU.not_equal, op1=ALU.mult).then_inc(self.live_ready, 1)
                            v.wait_ge(self.exp_used[k], used + 1 + 1)
                            if H > 1:
                                v.wait_ge(self.live_ready, H * (b * T + c + 1))
                                pv = self.prob[s].rearrange("p (h w) -> p h w", w=W)[:, :, 0:w]
                                v.tensor_tensor(pv, pv, self.live[s].rearrange("p (h w) -> p h w", w=W)[:, :, 0:w],
                                                ALU.min).then_inc(self.prob_ready[s], 1)
                            else:
                                v.tensor_tensor(self.prob[s][:, 0:w], self.prob[s][:, 0:w],
                                                mask[:, at(c * NP + b * W, w)], ALU.min
                                                ).then_inc(self.prob_ready[s], 1)
                    for s in range(2):
                        v.wait_ge(self.prob_used[s], (b + 1) * PAIRS + 1)
                    dcol = L.HD
                    for n in range(nt):
                        acc = bank[n][:, 0:H * (L.HD + 1)].rearrange("p (h x) -> p h x", h=H)
                        if H > 1:
                            v.tensor_copy(den[:, n * H:(n + 1) * H], acc[:, :, dcol]).then_inc(self.b_done, 1)
                        else:
                            v.reciprocal(rden[:, n:n + 1], bank[n][:, D:D + 1]).then_inc(self.b_done, 1)
                    v.wait_ge(self.b_done, self.steps(b, nt, 1))
                    if H > 1:
                        v.scalar_tensor_tensor(out=den[:, 0:nt * H], in0=den[:, 0:nt * H], scalar=0.0,
                                               in1=den[:, 0:nt * H], op0=ALU.is_equal, op1=ALU.add
                                               ).then_inc(self.b_done, 1)
                        v.wait_ge(self.b_done, self.steps(b, nt, 2))
                        v.reciprocal(rden[:, 0:nt * H], den[:, 0:nt * H]).then_inc(self.b_done, 1)
                        v.wait_ge(self.b_done, self.steps(b, nt, 3))
                    for n in range(nt):
                        t = b * self.nt + n
                        for h in range(H):
                            if H > 1:
                                xh = X[:, at(t * D + h * 64, 64)]
                                last = v.scalar_tensor_tensor(out=xh, in0=bank[n][:, h * 65:h * 65 + 64],
                                                              scalar=rden[:, n * H + h:n * H + h + 1], in1=xh,
                                                              op0=ALU.mult, op1=ALU.add)
                            else:
                                last = v.tensor_scalar(self.attn_out[:, at(t * D, D)], bank[n][:, 0:D],
                                                       rden[:, n:n + 1], None, ALU.mult)
                    last.then_inc(self.acc_free, 1)
                    v.wait_ge(self.acc_free, b + 1 + 1)
                    v.tensor_copy(den[:, 15:16], ident[:, 0:1]).then_inc(self.rows_free[r], 1)
                self.each_block(v, body)

            def steps(self, b, nt, k):
                if self.L.H == 1:
                    return b * self.nt + nt
                return b * (self.nt + 2) + nt + (k - 1)

            def attend_tensor(self, pe):
                L, H, W = self.L, self.L.H, self.L.W
                cols = H * (L.HD + 1)

                def body(b, bp, r, nt):
                    pe.wait_ge(self.acc_free, b + 1)
                    for n in range(nt):
                        pe.matmul(bank[n][:, 0:cols], zeros[:, 0:P], zeros[:, 0:cols], start=True, stop=True)
                    with pe.Fori(0, PAIRS) as i:
                        for s in range(2):
                            c = 2 * i + s
                            pe.wait_ge(self.prob_ready[s], b * PAIRS + i + 1)
                            for n in range(nt):
                                for h in range(H):
                                    hw = L.HD + 1
                                    last = pe.matmul(bank[n][:, h * hw:(h + 1) * hw],
                                                     self.prob[s][:, h * W + n * P:h * W + (n + 1) * P],
                                                     V[:, at(c * VW + h * hw, hw)],
                                                     start=False, stop=False, skip_group_check=True)
                            last.then_inc(self.prob_used[s], 1)
                self.each_block(pe, body)

            def gelu_scalar(self, a):
                a.wait_ge(self.acc_free, self.L.blocks + 1 + 1)
                with a.Fori(0, PAIRS) as i:
                    o = self.attn_out[:, at(i * 2 * D, 2 * D)]
                    a.activation(o, o, ACT.Gelu).then_inc(self.out_ready, 1)

            def gelu_vector(self, v):
                with v.Fori(0, PAIRS) as i:
                    v.wait_ge(self.out_ready, i + 1)
                    xs = X[:, at(i * 2 * D, 2 * D)]
                    v.tensor_tensor(xs, xs, self.attn_out[:, at(i * 2 * D, 2 * D)], ALU.add)


        class Signed:

            W = 512
            NT = W // P
            BLOCKS = NP // W
            STEP = 4
            STEPS = T // STEP
            HC = 65
            KW = 3 * HC
            FIRST = 6

            def __init__(self, A, tag):
                self.A, self.H = A, A.L.H
                assert self.BLOCKS == 6 and NP - 6 * self.W == self.W // 2 and T == 4 * self.STEPS + 2
                k = WORK_AT
                pw = T * 2 * self.KW // 2
                self.parts = [words(k + s * pw, pw).bitcast(BF16) for s in range(2)]
                k += 2 * pw
                self.row = [words(k + r * self.W, self.W) for r in range(2)]
                k += 2 * self.W
                sw = self.STEP * self.W // 4
                self.sign = [words(k + s * sw, sw) for s in range(2)]
                k += 2 * sw
                self.split = []
                for size in (sw, sw, sw // 2):
                    self.split.append([words(k, size), words(k + size, size)])
                    k += 2 * size
                tw = 2 * 2 * self.HC
                self.scaled = [words(k + s * tw, tw) for s in range(2)]
                k += 2 * tw
                self.sums = words(k, self.NT * 2 * self.HC)
                k += self.NT * 2 * self.HC
                assert k <= ARENA, k
                self.exp_sj = neg_sj
                self.exp_ready = sem(tag + "exp_ready")
                self.scale_steps = [sem(tag + "scale_pool"), sem(tag + "scale_dve")]
                self.parts_ready = [sem(f"{tag}parts_ready{s}") for s in range(2)]
                self.first_ready = sem(tag + "first_ready")
                self.parts_used = [sem(f"{tag}parts_used{s}") for s in range(2)]
                self.row_loaded = [sem(f"{tag}row_loaded{r}") for r in range(2)]
                self.row_used = [sem(f"{tag}row_used{r}") for r in range(2)]
                self.sign_ready = [sem(f"{tag}sign_ready{s}") for s in range(2)]
                self.sign_used = [sem(f"{tag}sign_used{s}") for s in range(2)]
                self.differs = sem(tag + "differs")
                self.split_ready = [sem(f"{tag}split_ready{s}") for s in range(3)]
                self.split_used = [sem(f"{tag}split_used{s}") for s in range(3)]
                self.block_done = [sem(f"{tag}block_done{r}") for r in range(2)]
                self.bank_free = [sem(f"{tag}bank_free{r}") for r in range(2)]
                self.fold_steps = sem(tag + "fold_steps")
                self.waited = {e: sem(tag + "waited_" + e) for e in ("a", "dve", "pe", "pool")}
                start_at_one.extend(self.row_used + self.sign_used + self.split_used + self.bank_free)

            def each_block(self, eng, body):
                with eng.Fori(0, self.BLOCKS // 2) as j:
                    for r in range(2):
                        body(j, r, self.NT)
                body(self.BLOCKS // 2, 0, self.NT // 2)

            def row_sync(self, sp):
                H = self.H
                flat = qd.rearrange("r p -> (r p)")
                with sp.Fori(0, H) as h:
                    def body(j, r, nt):
                        sp.wait_ge(self.row_used[r], h * (4 - r) + j + 1)
                        sp.dma_start(self.row[r][:, 0:nt * P],
                                     flat[at(((2 * H + h) * T) * P + (2 * j + r) * self.W, nt * P)]
                                     .partition_broadcast(P)).then_inc(self.row_loaded[r], 16)
                    self.each_block(sp, body)

            def sign_scalar(self, a):
                H, W = self.H, self.W
                a.activation(self.exp_sj[:, 0:H * T], s_all[:, 0:H * T], ACT.Exp).then_inc(self.exp_ready, 1)
                a.activation(q_cols[:, 0:H * T], q_cols[:, 0:H * T], ACT.Exp).then_inc(self.exp_ready, 1)
                with a.Fori(0, H) as h:
                    def body(j, r, nt):
                        b = h * 7 + 2 * j + r

                        def step(c, chunks, slot, nth):
                            a.wait_ge(self.sign_used[slot], nth + 1)
                            a.sem_inc(self.waited["a"], 1)
                            for q in range(chunks):
                                last = a.activation(self.sign[slot].bitcast(I8)[:, q * W:q * W + nt * P],
                                                    self.row[r][:, 0:nt * P], ACT.Sign,
                                                    bias=s_all[:, at(h * T + c + q, 1)])
                            last.then_inc(self.sign_ready[slot], 1)
                            return last

                        a.wait_ge(self.row_loaded[r], (h * (4 - r) + j + 1) * 16)
                        with a.Fori(0, self.STEPS // 2) as i:
                            for s in range(2):
                                step((2 * i + s) * 4, 4, s, b * (4 - s) + i)
                        step(T - 2, 2, 0, b * 4 + 3)
                        a.wait_ge(self.sign_ready[0], b * 4 + 4)
                        a.sem_inc(self.row_used[r], 1)
                    self.each_block(a, body)

            def scale(self, eng, who, h, slot, first, last, before):
                HC, steps = self.HC, self.scale_steps[who]
                f = self.scaled[who].rearrange("p (k c x) -> p k c x", k=2, c=2)
                with eng.Fori(first, last) as i:
                    done = before + (i - first) * 5
                    vals = V[:, at(2 * i * VW, 2 * VW)].rearrange("p (c n) -> p c n", c=2)[:, :, h * HC:(h + 1) * HC]
                    out_ = self.parts[slot][:, at(2 * i * 2 * self.KW, 4 * self.KW)].rearrange(
                        "p (c k g x) -> p k c g x", c=2, k=2, g=3)
                    for kind, e in enumerate((self.exp_sj, d_all)):
                        last_ = eng.tensor_tensor(f[:, kind, :, :], vals,
                                                  e[:, at(h * T + 2 * i, 2)].rearrange("p (c o) -> p c o", o=1)
                                                  .to_broadcast([P, 2, HC]), ALU.mult)
                    last_.then_inc(steps, 1)
                    eng.wait_ge(steps, done + 1)
                    for g in range(2):
                        eng.tensor_copy(out_[:, :, :, g, :], f).then_inc(steps, 1)
                        eng.wait_ge(steps, done + 2 * g + 2)
                        if who == 0:
                            eng.sem_inc(self.waited["pool"], 1)
                        sub_out = f if g == 0 else out_[:, :, :, 2, :]
                        eng.tensor_tensor(sub_out, f, out_[:, :, :, g, :], ALU.subtract).then_inc(steps, 1)
                        eng.wait_ge(steps, done + 2 * g + 3)

            def scale_gpsimd(self, pool):
                n = PAIRS - self.FIRST
                for h in range(self.H):
                    if h == 0:
                        pool.wait_ge(self.exp_ready, 2)
                    if h >= 2:
                        pool.wait_ge(self.parts_used[h % 2], h // 2)
                    before = 0 if h == 0 else 5 * (n + (h - 1) * PAIRS)
                    self.scale(pool, 0, h, h % 2, self.FIRST if h == 0 else 0, PAIRS, before)
                    total = 5 * (n + h * PAIRS)
                    pool.wait_ge(self.scale_steps[0], total)
                    pool.sem_inc(self.parts_ready[h % 2], 1)

            def split_vector(self, v):
                H, W, NT, HC = self.H, self.W, self.NT, self.HC
                v.wait_ge(self.exp_ready, 2)
                self.scale(v, 1, 0, 0, 0, self.FIRST, 0)
                v.wait_ge(self.scale_steps[1], 5 * self.FIRST)
                v.sem_inc(self.first_ready, 1)
                m32 = words(MASK_AT, MASK_WORDS).bitcast(U32)
                NW = NP // 4

                def step(b, k, c, chunks, nt, sslot, sn, slot, n_slot, nth):
                    w = nt * P // 4

                    def ring(t):
                        return t.bitcast(U32).rearrange("p (q w) -> p q w", w=W // 4)[:, 0:chunks, 0:w]
                    m = m32[:, at(c * NW, chunks * NW)].rearrange("p (q w) -> p q w", w=NW)[:, :, at(k * (W // 4), w)]
                    sg = ring(self.sign[sslot])
                    pos, neg = (ring(t) for t in self.split[slot])
                    v.wait_ge(self.sign_ready[sslot], sn + 1)
                    v.wait_ge(self.split_used[slot], n_slot + 1)
                    v.scalar_tensor_tensor(out=pos, in0=sg, scalar=1, in1=sg, op0=ALU.logical_shift_right,
                                           op1=ALU.bitwise_xor).then_inc(self.differs, 1)
                    v.tensor_tensor(neg, sg, m, ALU.bitwise_and).then_inc(self.sign_used[sslot], 1)
                    v.wait_ge(self.differs, nth + 1)
                    v.scalar_tensor_tensor(out=pos, in0=pos, scalar=3, in1=m, op0=ALU.logical_shift_left,
                                           op1=ALU.bitwise_and).then_inc(self.split_ready[slot], 1)

                def fold(h, k, j, r, nt):
                    base = (h * 7 + k) * 7
                    st = self.fold_steps
                    v.wait_ge(self.block_done[r], h * (4 - r) + j + 1)
                    for n in range(nt):
                        last = v.tensor_reduce(self.sums[:, n * 2 * HC:(n + 1) * 2 * HC]
                                               .rearrange("p (k x) -> p k x", k=2),
                                               bank[r * NT + n][:, 0:6 * HC]
                                               .rearrange("p (k g x) -> p k x g", k=2, g=3), AXX, ALU.add)
                    last.then_inc(st, 1)
                    v.wait_ge(st, base + 1)
                    v.sem_inc(self.bank_free[r], 1)
                    s4 = self.sums[:, 0:nt * 2 * HC].rearrange("p (n k x) -> p n k x", n=nt, k=2)
                    ac = q_cols[:, 0:2 * H * T].rearrange("p (k q) -> p q k", k=2)[:, at(h * T + k * NT, nt), :]
                    v.tensor_tensor(s4, s4, ac.rearrange("p n (k o) -> p n k o", o=1).to_broadcast([P, nt, 2, HC]),
                                    ALU.mult).then_inc(st, 1)
                    v.wait_ge(st, base + 2)
                    v.tensor_tensor(s4[:, :, 0, :], s4[:, :, 0, :], s4[:, :, 1, :], ALU.add).then_inc(st, 1)
                    v.wait_ge(st, base + 3)
                    dn = s4[:, :, 0, HC - 1]
                    v.scalar_tensor_tensor(out=den[:, 0:nt], in0=dn, scalar=0.0, in1=dn, op0=ALU.is_equal,
                                           op1=ALU.add).then_inc(st, 1)
                    v.wait_ge(st, base + 4)
                    v.reciprocal(rden[:, 0:nt], den[:, 0:nt]).then_inc(st, 1)
                    v.wait_ge(st, base + 5)
                    o = s4[:, :, 0, 0:64]
                    v.tensor_tensor(o, o, rden[:, 0:nt].rearrange("p (n o) -> p n o", o=1)
                                    .to_broadcast([P, nt, 64]), ALU.mult).then_inc(st, 1)
                    v.wait_ge(st, base + 6)
                    xh = X[:, at(k * NT * D, nt * D)].rearrange("p (n d) -> p n d", d=D)[:, :, at(h * 64, 64)]
                    v.tensor_tensor(xh, xh, o, ALU.add).then_inc(st, 1)
                    v.wait_ge(st, base + 7)
                    v.sem_inc(self.waited["dve"], 1)

                def block_(h, k, nt, fold_before):
                    b = h * 7 + k
                    for s in range(2):
                        step(b, k, 4 * s, 4, nt, s, b * (4 - s), s, b * 3, b * 7 + s)
                    if fold_before is not None:
                        fold_before()
                    with v.Fori(1, self.STEPS // 2) as i:
                        for s in range(2):
                            step(b, k, (2 * i + s) * 4, 4, nt, s, b * (4 - s) + i, s, b * 3 + i, b * 7 + 2 * i + s)
                    step(b, k, T - 2, 2, nt, 0, b * 4 + 3, 2, b, b * 7 + 6)

                with v.Fori(0, H // 2) as hp:
                    for p in range(2):
                        h = 2 * hp + p
                        block_(h, 0, NT, (lambda: fold(h - 1, 6, 3, 0, NT // 2)) if p == 1 else None)
                        with v.Fori(0, 2) as j:
                            block_(h, 2 * j + 1, NT, lambda: fold(h, 2 * j, j, 0, NT))
                            block_(h, 2 * j + 2, NT, lambda: fold(h, 2 * j + 1, j, 1, NT))
                        block_(h, 5, NT, lambda: fold(h, 4, 2, 0, NT))
                        block_(h, 6, NT // 2, lambda: fold(h, 5, 2, 1, NT))
                        if p == 1:
                            fold(h, 6, 3, 0, NT // 2)

            def products_tensor(self, pe):
                H, W, NT, KW = self.H, self.W, self.NT, self.KW
                pe.wait_ge(self.first_ready, 1)
                with pe.Fori(0, H // 2) as hp:
                    for p in range(2):
                        h = 2 * hp + p

                        def body(j, r, nt):
                            b = h * 7 + 2 * j + r
                            pe.wait_ge(self.bank_free[r], h * (4 - r) + j + 1)
                            pe.wait_ge(self.parts_ready[p], hp + 1)
                            for n in range(nt):
                                pe.matmul(bank[r * NT + n][:, 0:2 * KW], zeros[:, 0:P], zeros[:, 0:2 * KW],
                                          start=True, stop=True)
                            for st in range(self.STEPS + 1):
                                slot, nth = (st % 2, b * 3 + st // 2) if st < self.STEPS else (2, b)
                                pe.wait_ge(self.split_ready[slot], nth + 1)
                                pe.sem_inc(self.waited["pe"], 1)
                                for q in range(4 if st < self.STEPS else 2):
                                    c = st * 4 + q
                                    for n in range(nt):
                                        for kind in range(2):
                                            last = pe.matmul(
                                                bank[r * NT + n][:, kind * KW:(kind + 1) * KW],
                                                self.split[slot][kind].bitcast(F8)[:, q * W + n * P:q * W + (n + 1) * P],
                                                self.parts[p][:, (2 * c + kind) * KW:(2 * c + kind + 1) * KW],
                                                start=False, stop=False, skip_group_check=True)
                                last.then_inc(self.split_used[slot], 1)
                            pe.matmul(bank[r * NT][:, 0:64], zeros[:, 0:P], zeros[:, 0:64],
                                      start=False, stop=False, skip_group_check=True
                                      ).then_inc(self.block_done[r], 1)
                        self.each_block(pe, body)
                        pe.wait_ge(self.block_done[0], h * 4 + 4)
                        pe.sem_inc(self.parts_used[p], 1)

        class Experts:
            def __init__(self, hidden, tag, weights_at, scratch_at, second_norm):
                self.HID, self.tag, self.second_norm = hidden, tag, second_norm
                self.HC = hidden // P
                self.HB = hidden // 512
                self.W1 = words(weights_at, E * KC * hidden)
                self.W2 = words(weights_at + E * KC * hidden, E * self.HC * D)
                b1_at = weights_at + E * KC * hidden + E * self.HC * D
                self.b1 = words(b1_at, E * hidden)
                assert b1_at + E * hidden <= ARENA
                k = scratch_at
                TE = T * E
                self.logits = words(k, TE)
                k += TE
                self.pick1 = words(k, TE)
                k += TE
                self.pick2 = words(k, TE)
                k += TE
                self.work = words(k, TE)
                k += TE
                self.posx = words(k, TE)
                k += TE
                self.incl = words(k, TE)
                k += TE
                self.routed = words(k, TE // 2).bitcast(BF16)
                k += TE // 2
                self.top1 = words(k, T)
                k += T
                self.top2 = words(k, T)
                k += T
                self.best = words(k, T)
                k += T
                self.sums = words(k, T)
                k += T
                self.e2 = words(k, T)
                k += T
                self.gate = words(k, KC * E)
                k += KC * E
                self.gate_b = words(k, E)
                k += E
                self.used = words(k, E)
                k += E
                self.end = words(k, E)
                k += E
                self.base = words(k, E)
                k += E
                self.fills = words(k, E * T)
                self.below = words(k, SLOT_TILES * E)
                k += SLOT_TILES * E
                self.tile_e = words(k, SLOT_TILES)
                k += SLOT_TILES
                self.xn = [words(k + s * D, D) for s in range(2)]
                k += 2 * D
                self.xt = [words(k + s * D, D) for s in range(2)]
                k += 2 * D
                self.place_no = words(k, P)
                k += P
                self.weight_of = words(k, 2 * T)
                k += 2 * T
                self.slot_i = words(k, 2 * T).bitcast(I32)
                k += 2 * T
                self.part_i = words(k, 4 * T).bitcast(I32)
                k += 4 * T
                self.tile_of = words(k, 2 * T)
                k += 2 * T
                self.place_of = words(k, 2 * T)
                k += 2 * T
                self.at_place = [words(k + s * P, P) for s in range(2)]
                k += 2 * P
                self.in_tile = [words(k + s * 2 * SLOT_TILES, 2 * SLOT_TILES) for s in range(2)]
                k += 4 * SLOT_TILES
                assert k <= ARENA, (k, ARENA)
                k = b1_at + E * hidden
                self.rx = [words(k + s * D, D) for s in range(4)]
                k += 4 * D
                self.ysum = [words(k + s * D, D) for s in range(2)]
                k += 2 * D
                assert k <= ARENA, (k, ARENA)
                k = 0

                def ring(n, size):
                    nonlocal k
                    got = [X[:, k + s * size:k + (s + 1) * size] for s in range(n)]
                    k += n * size
                    return got
                self.rxt = ring(2, D)
                self.ry = ring(2, D)
                self.ht = ring(2, hidden)
                self.hid = ring(1, hidden)[0]
                self.b2 = ring(1, E * D)[0]
                assert k <= T * D
                self.loaded = sem(tag + "loaded")
                self.stat = sem(tag + "stat")
                self.aggr = sem(tag + "aggr")
                self.var_ready = sem(tag + "var_ready")
                self.sd_ready = sem(tag + "sd_ready")
                self.rstd_ready = sem(tag + "rstd_ready")
                self.x_spilled = sem(tag + "x_spilled")
                self.x_normed = sem(tag + "x_normed")
                self.lg_done = sem(tag + "lg_done")
                self.lg_copied = sem(tag + "lg_copied")
                self.route = sem(tag + "route")
                self.exps = sem(tag + "exps")
                self.picked = sem(tag + "picked")
                self.cnt_done = sem(tag + "cnt_done")
                self.tiles_known = sem(tag + "tiles_known")
                self.hot_ready = [sem(f"{tag}hot_ready{s}") for s in range(2)]
                self.hot_used = [sem(f"{tag}hot_used{s}") for s in range(2)]
                self.places_ready = sem(tag + "places_ready")
                self.xn_stored = sem(tag + "xn_stored")
                self.ysum_ready = sem(tag + "ysum_ready")
                self.w_loaded = sem(tag + "w_loaded")
                self.b_loaded = sem(tag + "b_loaded")
                self.folded = sem(tag + "folded")
                self.fold_used = sem(tag + "fold_used")
                self.fold_mm = sem(tag + "fold_mm")
                self.lnb_ready = sem(tag + "lnb_ready")
                self.lng_loaded = sem(tag + "lng_loaded")
                self.hid_ready = sem(tag + "hid_ready")
                self.h2 = sem(tag + "h2")
                self.x_back = sem(tag + "x_back")
                self.xn_ready = [sem(f"{tag}xn_ready{s}") for s in range(2)]
                self.tp_ready = [sem(f"{tag}tp_ready{s}") for s in range(2)]
                self.xt_ready = [sem(f"{tag}xt_ready{s}") for s in range(2)]
                self.rx_loaded = [sem(f"{tag}rx_loaded{s}") for s in range(4)]
                self.tx_ready = [sem(f"{tag}tx_ready{s}") for s in range(2)]
                self.xgt_ready = [sem(f"{tag}xgt_ready{s}") for s in range(2)]
                self.h_ready = [sem(f"{tag}h_ready{s}") for s in range(2)]
                self.th_ready = [sem(f"{tag}th_ready{s}") for s in range(2)]
                self.ht_ready = [sem(f"{tag}ht_ready{s}") for s in range(2)]
                self.y_ready = [sem(f"{tag}y_ready{s}") for s in range(2)]
                self.ry_ready = [sem(f"{tag}ry_ready{s}") for s in range(2)]
                self.added = sem(tag + "added")
                self.ry_free = [sem(f"{tag}ry_free{s}") for s in range(2)]
                start_at_one.extend(self.tp_ready + self.xt_ready + self.xn_ready + self.tx_ready + self.th_ready
                                    + self.h_ready + self.ht_ready + self.y_ready + self.ry_ready + self.ry_free
                                    + self.hot_used + [self.fold_used])

            def route_sync(self, sp, gate_w, gate_b, w1m, w2m, total):
                sp.dma_start(self.gate.rearrange("p (k e) -> p k e", e=E),
                             gate_w.rearrange("(k p) e -> p k e", p=P)).then_inc(self.loaded, 16)
                sp.dma_start(self.gate_b, gate_b.partition_broadcast(P)).then_inc(self.loaded, 16)
                sp.dma_start(total[0:NP, :].rearrange("(t p) d -> p t d", p=P), X[:, :].rearrange("p (t d) -> p t d", d=D)
                             ).then_inc(self.x_spilled, 16)
                for w, m in ((self.W1, w1m), (self.W2, w2m)):
                    n = m.shape[1] // 4
                    for g in range(4):
                        sp.dma_start(w[:, g * n:(g + 1) * n], m[:, g * n:(g + 1) * n]).then_inc(self.w_loaded, 16)
                sp.wait_ge(self.x_normed, T * (1 + self.second_norm))
                sp.dma_start(xs[0:NP, :].rearrange("(t p) d -> p t d", p=P), X[:, :].rearrange("p (t d) -> p t d", d=D)
                             ).then_inc(self.xn_stored, 16)
                sp.wait_ge(self.xn_stored, 16)

            def norm_in_place(self, v):
                with v.Fori(0, T) as t:
                    v.tensor_scalar(X[:, at(t * D, D)], X[:, at(t * D, D)], mv[:, at(t, 1)], rstd[:, at(t, 1)],
                                    ALU.subtract, ALU.mult).then_inc(self.x_normed, 1)

            def route_vector(self, v):
                layer_norm_stats(v, self)
                v.wait_ge(self.x_spilled, 16)
                self.norm_in_place(v)
                TE = T * E
                lg3 = self.logits.rearrange("p (t e) -> p t e", e=E)
                w3 = self.work.rearrange("p (t e) -> p t e", e=E)
                r = self.route
                n = [0]

                def step(ins):
                    n[0] += 1
                    ins.then_inc(r, 1)
                    v.wait_ge(r, n[0])

                def spread(a):
                    return a.rearrange("p (t o) -> p t o", o=1).to_broadcast([P, T, E])

                def spread_t(a):
                    return a.rearrange("p (o e) -> p o e", o=1).to_broadcast([P, T, E])

                v.wait_ge(self.lg_done, T)
                v.wait_ge(self.loaded, 32)
                step(v.tensor_tensor(lg3, bank[2][:, 0:TE].rearrange("p (t e) -> p t e", e=E), spread_t(self.gate_b),
                                     ALU.add))
                for top, pick in ((self.top1, self.pick1), (self.top2, self.pick2)):
                    p3 = pick.rearrange("p (t e) -> p t e", e=E)
                    step(v.tensor_reduce(top, lg3, AXX, ALU.max))
                    step(v.tensor_tensor(w3, lg3, spread(top), ALU.is_equal))
                    step(v.tensor_tensor(w3, w3, spread_t(order8[:, :]), ALU.mult))
                    step(v.tensor_reduce(self.best, w3, AXX, ALU.max))
                    step(v.tensor_tensor(p3, w3, spread(self.best), ALU.is_equal))
                    if top is self.top1:
                        step(v.tensor_tensor(w3, lg3, spread(top), ALU.subtract))
                        v.tensor_copy(self.posx, self.work).then_inc(self.picked, 1)
                        step(v.scalar_tensor_tensor(out=self.logits, in0=pick, scalar=-3.0e38, in1=self.logits,
                                                    op0=ALU.mult, op1=ALU.add))
                v.tensor_tensor(self.e2, self.top2, self.top1, ALU.subtract).then_inc(self.picked, 1)
                v.tensor_tensor(self.routed, self.pick1, self.pick2, ALU.add).then_inc(self.picked, 1)
                v.wait_ge(self.exps, 2)
                if self.second_norm:
                    step(v.tensor_scalar(self.sums, self.e2, 1.0, None, ALU.add))
                else:
                    step(v.tensor_reduce(self.sums, self.posx.rearrange("p (t e) -> p t e", e=E), AXX, ALU.add))
                wt = self.weight_of
                step(v.reciprocal(wt[:, 0:T], self.sums))
                step(v.tensor_tensor(wt[:, T:2 * T], self.e2, wt[:, 0:T], ALU.mult))
                v.wait_ge(self.cnt_done, 1)
                step(v.tensor_copy(self.work, bank[4][:, 0:TE]))
                i3 = self.incl.rearrange("p (e t) -> p e t", t=T)
                for e in range(E):
                    last = v.tensor_tensor_scan(i3[:, e, :], ones_t[:, :], w3[:, :, e], 0.0, ALU.mult, ALU.add)
                step(last)
                f3 = self.fills.rearrange("p (e t) -> p e t", t=T)
                step(v.tensor_tensor(f3, i3[:, :, T - 1:T].to_broadcast([P, E, T]),
                                     fill_at[:, :].rearrange("p (o t) -> p o t", o=1).to_broadcast([P, E, T]),
                                     ALU.is_gt))
                step(v.tensor_reduce(self.used, f3, AXX, ALU.add))
                step(v.tensor_tensor_scan(self.end, ones_t[:, 0:E], self.used, 0.0, ALU.mult, ALU.add))
                step(v.tensor_tensor(self.base, self.end, self.used, ALU.subtract))
                step(v.tensor_scalar(self.base, self.base, float(P), None, ALU.mult))
                p3 = self.posx.rearrange("p (t e) -> p t e", e=E)
                step(v.tensor_tensor(p3, i3.rearrange("p e t -> p t e"), w3, ALU.subtract))
                step(v.tensor_tensor(p3, p3, spread_t(self.base), ALU.add))
                step(v.tensor_tensor(self.posx, bank[3][:, 0:TE], self.posx, ALU.add))
                for k, pick in enumerate((self.pick1, self.pick2)):
                    step(v.tensor_tensor(self.work, self.posx, pick, ALU.mult))
                    step(v.tensor_reduce(self.best, w3, AXX, ALU.add))
                    step(v.tensor_copy(self.slot_i[:, k * T:(k + 1) * T], self.best))
                step(v.tensor_scalar(self.part_i[:, 0:2 * T], self.slot_i, 7, None, ALU.logical_shift_right))
                step(v.tensor_scalar(self.part_i[:, 2 * T:4 * T], self.slot_i, P - 1, None, ALU.bitwise_and))
                step(v.tensor_copy(self.tile_of, self.part_i[:, 0:2 * T]))
                step(v.tensor_copy(self.place_of, self.part_i[:, 2 * T:4 * T]))
                G = SLOT_TILES
                v.wait_ge(self.places_ready, 1)
                with v.Fori(0, T) as t:
                    for k in range(2):
                        q = at(t + k * T, 1)
                        v.wait_ge(self.hot_used[k], t + 1)
                        v.tensor_scalar(self.at_place[k], self.place_no, self.place_of[:, q], None, ALU.is_equal)
                        v.tensor_scalar(self.in_tile[k][:, 0:G], tile_no[:, :], self.tile_of[:, q],
                                        row_id[:, at(t, 1)], ALU.is_equal, ALU.mult)
                        v.tensor_scalar(self.in_tile[k][:, G:2 * G], tile_no[:, :], self.tile_of[:, q],
                                        wt[:, q], ALU.is_equal, ALU.mult).then_inc(self.hot_ready[k], 1)
                b3 = self.below.rearrange("p (g e) -> p g e", e=E)[0:1]
                step(v.tensor_tensor(b3, self.end[0:1].rearrange("p (o e) -> p o e", o=1)
                                     .to_broadcast([1, SLOT_TILES, E]),
                                     tile_no[0:1].rearrange("p (g o) -> p g o", o=1).to_broadcast([1, SLOT_TILES, E]),
                                     ALU.is_le))
                step(v.tensor_reduce(self.tile_e[0:1], b3, AXX, ALU.add))
                step(v.tensor_scalar(self.tile_e[0:1], self.tile_e[0:1], float(E - 1), None, ALU.min))
                v.tensor_copy(expert_of[:, :], self.tile_e[0:1]).then_inc(self.tiles_known, 1)
                if self.second_norm:
                    v.wait_ge(self.xn_ready[1], PAIRS + 1)
                    layer_norm_stats(v, self, 2)
                    self.norm_in_place(v)
                for k in range(2):
                    v.wait_ge(self.hot_used[k], T + 1)
                step(v.tensor_scalar(self.in_tile[0][:, 0:G], bank[5][:, 0:G], 0.0, spare_row[:, :],
                                     ALU.is_equal, ALU.mult))
                v.scalar_tensor_tensor(out=slot_row[:, :], in0=bank[5][:, 0:G], scalar=1.0,
                                       in1=self.in_tile[0][:, 0:G], op0=ALU.subtract, op1=ALU.add)
                v.tensor_copy(slot_w[:, :], bank[5][:, G:2 * G])

            def route_scalar(self, a):
                layer_norm_sqrt(a, self)
                with a.Fori(0, PAIRS) as i:
                    for s in range(2):
                        t = 2 * i + s
                        a.wait_ge(self.x_normed, t + 1)
                        a.wait_ge(self.tp_ready[s], i + 1)
                        a.copy(self.xn[s], X[:, at(t * D, D)]).then_inc(self.xn_ready[s], 1)
                    for s in range(2):
                        a.wait_ge(self.tp_ready[s], i + 2)
                        a.copy(self.xt[s], bank[s][:, 0:D]).then_inc(self.xt_ready[s], 1)
                a.wait_ge(self.picked, 3)
                a.activation(self.posx, self.posx, ACT.Exp).then_inc(self.exps, 1)
                a.activation(self.e2, self.e2, ACT.Exp).then_inc(self.exps, 1)
                if self.second_norm:
                    layer_norm_sqrt(a, self, 2)

            def route_tensor(self, pe):
                pe.wait_ge(self.loaded, 32)
                with pe.Fori(0, PAIRS) as i:
                    for s in range(2):
                        pe.wait_ge(self.xn_ready[s], i + 2)
                        pe.wait_ge(self.xt_ready[s], i + 1)
                        for k in range(KC):
                            last = pe.transpose(bank[s][:, k * P:(k + 1) * P], self.xn[s][:, k * P:(k + 1) * P],
                                                ident[:, :])
                        last.then_inc(self.tp_ready[s], 1)
                    for s in range(2):
                        pe.wait_ge(self.xt_ready[s], i + 2)
                        for k in range(KC):
                            last = pe.matmul(bank[2][:, at((2 * i + s) * E, E)], self.xt[s][:, k * P:(k + 1) * P],
                                             self.gate[:, k * E:(k + 1) * E], start=(k == 0), stop=(k == KC - 1))
                        last.then_inc(self.lg_done, 1)
                pe.wait_ge(self.picked, 3)
                pe.matmul(bank[3][:, 0:T * E], earlier[:, :], self.routed, start=True, stop=True)
                pe.matmul(bank[4][:, 0:T * E], ones[:, :], self.routed, start=True, stop=True
                          ).then_inc(self.cnt_done, 1)
                pe.matmul(bank[5][:, 0:2 * SLOT_TILES], zeros[:, 0:P], zeros[:, 0:2 * SLOT_TILES],
                          start=True, stop=True)
                with pe.Fori(0, T) as t:
                    for k in range(2):
                        pe.wait_ge(self.hot_ready[k], t + 1)
                        pe.matmul(bank[5][:, 0:2 * SLOT_TILES], self.at_place[k], self.in_tile[k],
                                  start=False, stop=False, skip_group_check=True).then_inc(self.hot_used[k], 1)

            def route_gpsimd(self, pool):
                pool.iota(self.place_no, [[1, P]], base=0, channel_multiplier=0,
                          allow_small_or_imprecise_dtypes=True).then_inc(self.places_ready, 1)

            def tiles_sync(self, sp, b1m, b2m):
                sp.dma_start(self.b1, b1m.partition_broadcast(P)).then_inc(self.b_loaded, 16)
                sp.dma_start(self.b2, b2m.partition_broadcast(P)).then_inc(self.b_loaded, 16)

            def tiles_gpsimd(self, pool, total):
                def gather(g):
                    pool.indirect_dma_start(self.rx[g % 4], None, xs[:, :],
                                            bass.IndirectOffsetOnAxis(ap=slot_row[:, g:g + 1], axis=0)
                                            ).then_inc(self.rx_loaded[g % 4], 16)
                for g in range(4):
                    gather(g)
                for g in range(RUN_TILES):
                    if g + 4 < SLOT_TILES:
                        pool.wait_ge(self.tx_ready[g % 2], g // 2 + 2)
                        gather(g + 4)
                    pool.wait_ge(self.ry_ready[g % 2], g // 2 + 2)
                    if g > 0:
                        pool.wait_ge(self.added, 16 * g)
                        pool.sem_inc(self.ry_free[(g - 1) % 2], 1)
                    pool.indirect_dma_start(total[:, :],
                                            bass.IndirectOffsetOnAxis(ap=slot_row[:, g:g + 1], axis=0),
                                            self.ry[g % 2], None, compute_op=ALU.add).then_inc(self.added, 16)
                pool.wait_ge(self.added, 16 * RUN_TILES)

            def tiles_tensor(self, pe):
                HID, HC = self.HID, self.HC

                def hidden(e, s):
                    for b in range(self.HB):
                        for k in range(KC):
                            last = pe.matmul(bank[b][:, :], self.rxt[s][:, k * P:(k + 1) * P],
                                             self.W1[:, at(e * (KC * HID) + k * HID + b * 512, 512)],
                                             start=(k == 0), stop=(k == KC - 1))
                    last.then_inc(self.h_ready[s], 1)

                def turn_x(q):
                    for k in range(KC):
                        last = pe.transpose(bank[4][:, k * P:(k + 1) * P], self.rx[q][:, k * P:(k + 1) * P],
                                            ident[:, :])
                    last.then_inc(self.tx_ready[q % 2], 1)

                pe.wait_ge(self.w_loaded, 16 * 8)
                if self.second_norm:
                    self.fold_tensor(pe)
                pe.wait_ge(self.rx_loaded[0], 16)
                turn_x(0)
                pe.wait_ge(self.rx_loaded[1], 16)
                pe.wait_ge(self.xgt_ready[0], 1)
                turn_x(1)
                e0 = pe.value_load(expert_of[0:1, 0:1], min_val=0, max_val=E - 1)
                hidden(e0, 0)
                with pe.Fori(0, RUN_TILES // 4) as j:
                    for q in range(4):
                        i, s = 2 * j + q // 2, q % 2
                        o = 1 - s
                        g = 4 * j + q
                        pe.wait_ge(self.hid_ready, g + 1)
                        pe.wait_ge(self.ht_ready[o], i + 1 + s)
                        for c in range(HC):
                            last = pe.transpose(bank[2 + c // 4][:, c % 4 * P:(c % 4 + 1) * P],
                                                self.hid[:, c * P:(c + 1) * P], ident[:, :])
                        last.then_inc(self.th_ready[s], 1)
                        pe.wait_ge(self.rx_loaded[(q + 2) % 4], 16 * (j + 1 + (q >= 2)))
                        pe.wait_ge(self.xgt_ready[o], i + 1 + s)
                        turn_x((q + 2) % 4)
                        e = pe.value_load(expert_of[0:1, at(g + 1, 1)], min_val=0, max_val=E - 1)
                        hidden(e, o)
                        e = pe.value_load(expert_of[0:1, at(g, 1)], min_val=0, max_val=E - 1)
                        pe.wait_ge(self.ht_ready[s], i + 2)
                        pe.wait_ge(self.ry_ready[s], i + 1)
                        for c in range(HC):
                            last = pe.matmul(bank[5 + s][:, 0:D], self.ht[s][:, c * P:(c + 1) * P],
                                             self.W2[:, at(e * (HC * D) + c * D, D)],
                                             start=(c == 0), stop=(c == HC - 1))
                        last.then_inc(self.y_ready[s], 1)

            def tiles_scalar(self, a):
                for s in range(2):
                    a.wait_ge(self.tx_ready[s], 2)
                    a.copy(self.rxt[s], bank[4][:, 0:D]).then_inc(self.xgt_ready[s], 1)
                with a.Fori(0, RUN_TILES // 2) as i:
                    for s in range(2):
                        a.wait_ge(self.th_ready[s], i + 2)
                        a.wait_ge(self.y_ready[s], i + 1)
                        for b in range(self.HB):
                            last = a.activation(self.ht[s][:, b * 512:(b + 1) * 512], bank[2 + b][:, :], ACT.Gelu)
                        last.then_inc(self.ht_ready[s], 1)
                        a.wait_ge(self.tx_ready[s], i + 3)
                        a.wait_ge(self.h_ready[s], i + 2)
                        a.copy(self.rxt[s], bank[4][:, 0:D]).then_inc(self.xgt_ready[s], 1)

            def tiles_vector(self, v):
                HID = self.HID

                def add_bias(e, s, use):
                    v.wait_ge(self.h_ready[s], use + 2)
                    for b in range(self.HB):
                        last = v.tensor_tensor(self.hid[:, b * 512:(b + 1) * 512], bank[b][:, :],
                                               self.b1[:, at(e * HID + b * 512, 512)], ALU.add)
                    last.then_inc(self.hid_ready, 1)

                v.wait_ge(self.b_loaded, 32)
                if self.second_norm:
                    self.fold_vector(v)
                e0 = v.value_load(expert_of[0:1, 0:1], min_val=0, max_val=E - 1)
                add_bias(e0, 0, 0)
                with v.Fori(0, RUN_TILES // 2) as i:
                    for s in range(2):
                        o = 1 - s
                        g = 2 * i + s
                        e = v.value_load(expert_of[0:1, at(g + 1, 1)], min_val=0, max_val=E - 1)
                        v.wait_ge(self.th_ready[s], i + 2)
                        add_bias(e, o, i + s)
                        e = v.value_load(expert_of[0:1, at(g, 1)], min_val=0, max_val=E - 1)
                        v.wait_ge(self.y_ready[s], i + 2)
                        v.wait_ge(self.ry_free[s], i + 1)
                        v.tensor_tensor(self.ysum[s], bank[5 + s][:, 0:D], self.b2[:, at(e * D, D)], ALU.add
                                        ).then_inc(self.ysum_ready, 1)
                        v.wait_ge(self.ysum_ready, g + 1)
                        v.tensor_scalar(self.ry[s], self.ysum[s], slot_w[:, at(g, 1)], None, ALU.mult
                                        ).then_inc(self.ry_ready[s], 1)

            def fold_scratch(self):
                k = 0
                self.lnb = [self.ht[s][:, 0:KC * P] for s in range(2)]
                self.ln_g = self.hid[:, 0:KC * E]
                self.ln_b = self.hid[:, KC * E:2 * KC * E]

            def fold_sync(self, sp, ln_gm, ln_bm):
                self.fold_scratch()
                sp.dma_start(self.ln_g, ln_gm).then_inc(self.lng_loaded, 16)
                sp.dma_start(self.ln_b, ln_bm).then_inc(self.lng_loaded, 16)

            def fold_tensor(self, pe):
                self.fold_scratch()
                HID = self.HID
                with pe.Fori(0, E // 2) as i:
                    for s in range(2):
                        e = 2 * i + s
                        pe.wait_ge(self.lnb_ready, e + 1)
                        pe.wait_ge(self.fold_used, e + 1)
                        for b in range(self.HB):
                            for k in range(KC):
                                last = pe.matmul(bank[2 * s + b][:, :], self.lnb[s][:, k * P:(k + 1) * P],
                                                 self.W1[:, at(e * (KC * HID) + k * HID + b * 512, 512)],
                                                 start=(k == 0), stop=(k == KC - 1))
                        last.then_inc(self.fold_mm, 1)
                pe.wait_ge(self.fold_used, E + 1)
                pe.wait_ge(self.folded, E)

            def fold_vector(self, v):
                self.fold_scratch()
                HID = self.HID
                v.wait_ge(self.lng_loaded, 32)
                v.wait_ge(self.w_loaded, 16 * 8)

                def shift(e, s):
                    for k in range(KC):
                        last = v.tensor_copy(self.lnb[s][:, k * P:(k + 1) * P],
                                             self.ln_b[:, at(e * KC + k, 1)].to_broadcast([P, P]))
                    last.then_inc(self.lnb_ready, 1)
                with v.Fori(0, E // 2) as i:
                    for s in range(2):
                        shift(2 * i + s, s)
                    for s in range(2):
                        e = 2 * i + s
                        v.wait_ge(self.fold_mm, e + 1)
                        for b in range(self.HB):
                            bv = self.b1[:, at(e * HID + b * 512, 512)]
                            last = v.tensor_tensor(bv, bank[2 * s + b][:, :], bv, ALU.add)
                        last.then_inc(self.fold_used, 1)
                        for k in range(KC):
                            wv = self.W1[:, at(e * (KC * HID) + k * HID, HID)]
                            last = v.tensor_scalar(wv, wv, self.ln_g[:, at(e * KC + k, 1)], None, ALU.mult)
                        last.then_inc(self.folded, 1)
                v.wait_ge(self.folded, E)

            def back_sync(self, sp):
                sp.dma_start(X[:, :].rearrange("p (t d) -> p t d", d=D), xd[0:NP, :].rearrange("(t p) d -> p t d", p=P)
                             ).then_inc(self.x_back, 16)
                sp.wait_ge(self.x_back, 16)

        def layer_norm_stats(v, sems, nth=1):
            with v.Fori(0, T) as t:
                v.bn_stats(stats[:, at(t * 6, 6)], X[:, at(t * D, D)]).then_inc(sems.stat, 1)
            v.wait_ge(sems.stat, T * nth)
            st = stats[:, :].rearrange("p (t k) -> p t k", k=6)
            half_sum, half_diff, m2 = mv[:, 0:T], mv[:, T:2 * T], mv[:, 2 * T:3 * T]
            v.tensor_tensor(half_sum, st[:, :, 1], st[:, :, 4], ALU.add).then_inc(sems.aggr, 1)
            v.tensor_tensor(half_diff, st[:, :, 1], st[:, :, 4], ALU.subtract).then_inc(sems.aggr, 1)
            v.tensor_tensor(m2, st[:, :, 2], st[:, :, 5], ALU.add).then_inc(sems.aggr, 1)
            v.wait_ge(sems.aggr, 6 * nth - 3)
            v.tensor_scalar(half_sum, half_sum, 0.5, None, ALU.mult).then_inc(sems.aggr, 1)
            v.scalar_tensor_tensor(out=half_diff, in0=half_diff, scalar=0.25, in1=half_diff, op0=ALU.mult,
                                   op1=ALU.mult).then_inc(sems.aggr, 1)
            v.wait_ge(sems.aggr, 6 * nth - 1)
            v.scalar_tensor_tensor(out=m2, in0=m2, scalar=1.0 / D, in1=half_diff, op0=ALU.mult, op1=ALU.add
                                   ).then_inc(sems.aggr, 1)
            v.wait_ge(sems.aggr, 6 * nth)
            v.tensor_scalar(rstd[:, :], m2, EPS, None, ALU.add).then_inc(sems.var_ready, 1)
            v.wait_ge(sems.sd_ready, nth)
            v.reciprocal(rstd[:, :], rstd[:, :]).then_inc(sems.rstd_ready, 1)
            v.wait_ge(sems.rstd_ready, nth)

        def layer_norm_sqrt(a, sems, nth=1):
            a.wait_ge(sems.var_ready, nth)
            a.activation(rstd[:, :], rstd[:, :], ACT.Sqrt).then_inc(sems.sd_ready, 1)

        hand_over()
        A0 = Attention(L0, "a0_")
        a0_sems, a0_ones = hand_over()

        def give_ones(eng, sems):
            for free in sems:
                eng.sem_inc(free, 1)

        with nc.Block() as block:
            @block.sync
            def _(sp):
                loads_sync(sp)
                give_ones(sp, a0_ones[0::2])

            @block.tensor
            def _(pe):
                give_ones(pe, a0_ones[1::2])

            @block.gpsimd
            def _(pool):
                constants_gpsimd(pool)

        with nc.Block() as block:
            @block.sync
            def _(sp):
                A0.values_sync(sp)
                A0.rows_sync(sp)

            @block.gpsimd
            def _(pool):
                mask_loads_gpsimd(pool, A0.bins_gpsimd)

            @block.vector
            def _(v):
                v.wait_ge(x_loaded, 32)
                A0.values_vector(v)
                A0.bins_vector(v)
                A0.count_vector(v)
                A0.rows_vector(v)

            @block.scalar
            def _(a):
                A0.values_scalar(a)
                A0.count_scalar(a)
                A0.rows_scalar(a)

            @block.tensor
            def _(pe):
                A0.values_tensor(pe)
                A0.count_tensor(pe)
                A0.rows_tensor(pe)

        X0 = Experts(512, "x0_", V_AT, 38016, False)
        x0_sems, x0_ones = hand_over()

        with nc.Block() as block:
            @block.sync
            def _(sp):
                A0.attend_sync(sp)
                give_ones(sp, x0_ones)
                for t in (xs, xd, out):
                    sp.dma_start(t[NP:NP + P, :], zeros[:, :].bitcast(F32)).then_inc(spare_clean, 16)
                sp.wait_ge(spare_clean, 48)

            @block.vector
            def _(v):
                A0.attend_vector(v)
                A0.gelu_vector(v)

            @block.scalar
            def _(a):
                A0.attend_scalar(a)
                A0.gelu_scalar(a)

            @block.tensor
            def _(pe):
                A0.attend_tensor(pe)

        nc.clear_and_free_semaphores(a0_sems)

        def experts_blocks(X_, total, next_ones, gate_w, gate_b, w1m, b1m, w2m, b2m, ln=None):
            with nc.Block() as block:
                @block.sync
                def _(sp):
                    X_.route_sync(sp, gate_w, gate_b, w1m, w2m, total)

                @block.gpsimd
                def _(pool):
                    X_.route_gpsimd(pool)

                @block.vector
                def _(v):
                    X_.route_vector(v)

                @block.scalar
                def _(a):
                    X_.route_scalar(a)

                @block.tensor
                def _(pe):
                    X_.route_tensor(pe)

            with nc.Block() as block:
                @block.sync
                def _(sp):
                    give_ones(sp, next_ones)
                    if ln is not None:
                        X_.fold_sync(sp, *ln)
                    X_.tiles_sync(sp, b1m, b2m)

                @block.gpsimd
                def _(pool):
                    X_.tiles_gpsimd(pool, total)

                @block.vector
                def _(v):
                    X_.tiles_vector(v)

                @block.scalar
                def _(a):
                    X_.tiles_scalar(a)

                @block.tensor
                def _(pe):
                    X_.tiles_tensor(pe)

        A1 = Attention(L1, "a1_")
        a1_sems, a1_ones = hand_over()
        a1_sems = [s for s in a1_sems if s not in A1.before_attend]
        experts_blocks(X0, xd, a1_ones, gate0, gate_b0, m0w1, m0b1, m0w2, m0b2)

        with nc.Block() as block:
            @block.sync
            def _(sp):
                X0.back_sync(sp)

        nc.clear_and_free_semaphores(x0_sems)
        nc.all_engine_barrier()
        Q1 = Signed(A1, "q1_")
        q1_sems, q1_ones = hand_over()
        with nc.Block() as block:
            @block.sync
            def _(sp):
                give_ones(sp, q1_ones)
                A1.values_sync(sp)
                A1.rows_sync(sp)

            @block.gpsimd
            def _(pool):
                A1.bins_gpsimd(pool)

            @block.vector
            def _(v):
                m32 = words(MASK_AT, MASK_WORDS).bitcast(U32)
                for half in range(2):
                    part = m32[:, half * MASK_WORDS // 2:(half + 1) * MASK_WORDS // 2]
                    v.tensor_scalar(part, part, 3, None, ALU.logical_shift_left).then_inc(mask_scaled, 1)
                A1.values_vector(v)
                A1.bins_vector(v)
                A1.count_vector(v)
                A1.rows_vector(v)

            @block.scalar
            def _(a):
                A1.values_scalar(a)
                a.wait_ge(mask_scaled, 2)
                A1.count_scalar(a)
                A1.rows_scalar(a)

            @block.tensor
            def _(pe):
                A1.values_tensor(pe)
                A1.count_tensor(pe)
                A1.rows_tensor(pe)

        nc.clear_and_free_semaphores(A1.before_attend)
        nc.all_engine_barrier()
        X1 = Experts(1024, "x1_", 0, 32768, True)
        x1_sems, x1_ones = hand_over()

        with nc.Block() as block:
            @block.sync
            def _(sp):
                with sp.If(sp.value_load(is_far[0:1, 0:1], min_val=0, max_val=1) > 0):
                    A1.attend_sync(sp)
                with sp.Else():
                    Q1.row_sync(sp)
                give_ones(sp, x1_ones)

            @block.gpsimd
            def _(pool):
                with pool.If(pool.value_load(is_far[0:1, 0:1], min_val=0, max_val=1) < 1):
                    Q1.scale_gpsimd(pool)

            @block.vector
            def _(v):
                with v.If(v.value_load(is_far[0:1, 0:1], min_val=0, max_val=1) > 0):
                    A1.attend_vector(v)
                with v.Else():
                    Q1.split_vector(v)

            @block.scalar
            def _(a):
                with a.If(a.value_load(is_far[0:1, 0:1], min_val=0, max_val=1) > 0):
                    A1.attend_scalar(a)
                with a.Else():
                    Q1.sign_scalar(a)

            @block.tensor
            def _(pe):
                with pe.If(pe.value_load(is_far[0:1, 0:1], min_val=0, max_val=1) > 0):
                    A1.attend_tensor(pe)
                with pe.Else():
                    Q1.products_tensor(pe)

        nc.clear_and_free_semaphores(a1_sems + q1_sems)
        experts_blocks(X1, out, [], gate1, gate_b1, m1w1, m1b1, m1w2, m1b2, (ln_g1, ln_b1))


def kernel(x, adj, L0_gnn_W, L0_gnn_r, L0_ffn_gate_w, L0_ffn_gate_b, L0_ffn_W1, L0_ffn_b1, L0_ffn_W2, L0_ffn_b2,
           L1_gnn_weight, L1_gnn_weight_u, L1_gnn_weight_v, L1_gnn_bias, L1_gnn_proj_w, L1_gnn_proj_b,
           L1_ffn_Wr, L1_ffn_br, L1_ffn_ln_g, L1_ffn_ln_b, L1_ffn_W1, L1_ffn_b1, L1_ffn_W2, L1_ffn_b2):
    import numpy as np
    import concourse.bacc as bacc
    from concourse.bass_utils import run_bass_kernel_spmd as run

    x = np.asarray(x)
    xp = np.zeros((NP, D), x.dtype)
    xp[:NODES] = x
    adjT = np.zeros((NP, NP), np.int32)
    adjT[:NODES, :NODES] = np.asarray(adj).T
    for n in range(NODES, NP):
        adjT[n, n] = 1
    w0 = np.asarray(L0_gnn_W)
    r0 = np.asarray(L0_gnn_r).reshape(2, D)
    w1 = np.asarray(L1_gnn_weight)
    uv = np.zeros((D, 8), w1.dtype)
    for h in range(4):
        uv[h * 64:(h + 1) * 64, h] = np.asarray(L1_gnn_weight_u)[h, :, 0]
        uv[h * 64:(h + 1) * 64, 4 + h] = np.asarray(L1_gnn_weight_v)[h, :, 0]
    arrays = {
        "x_in": xp, "adjT": adjT, "w0T": w0.T, "w0": w0, "r0": r0[::-1].T,
        "w1": w1, "w1T": w1.T, "uv1": uv, "proj_wT": np.asarray(L1_gnn_proj_w).T,
        "bias1": np.asarray(L1_gnn_bias).reshape(D), "proj_b1": np.asarray(L1_gnn_proj_b).reshape(D),
    }

    def up(w):
        w = np.asarray(w)
        return w.reshape(E, KC, P, -1).transpose(2, 0, 1, 3).reshape(P, -1)

    def down(w):
        w = np.asarray(w)
        return w.reshape(E, -1, P, D).transpose(2, 0, 1, 3).reshape(P, -1)

    def cols(w):
        return np.asarray(w).reshape(E, KC, P).transpose(2, 0, 1).reshape(P, -1)

    arrays.update({
        "gate0": np.asarray(L0_ffn_gate_w), "gate_b0": np.asarray(L0_ffn_gate_b),
        "m0w1": up(L0_ffn_W1), "m0b1": np.asarray(L0_ffn_b1).reshape(-1),
        "m0w2": down(L0_ffn_W2), "m0b2": np.asarray(L0_ffn_b2).reshape(-1),
        "gate1": np.asarray(L1_ffn_Wr), "gate_b1": np.asarray(L1_ffn_br),
        "ln_g1": cols(L1_ffn_ln_g), "ln_b1": cols(L1_ffn_ln_b),
        "m1w1": up(L1_ffn_W1), "m1b1": np.asarray(L1_ffn_b1).reshape(-1),
        "m1w2": down(L1_ffn_W2), "m1b2": np.asarray(L1_ffn_b2).reshape(-1),
    })
    arrays = {k: np.ascontiguousarray(a) for k, a in arrays.items()}
    nc = bacc.Bacc("TRN2", target_bir_lowering=False, num_devices=1)
    args = {k: nc.dram_tensor(k, a.shape, mybir.dt.from_np(a.dtype), kind="ExternalInput").ap()
            for k, a in arrays.items()}
    out = nc.dram_tensor("out", (NP + P, D), F32, kind="ExternalOutput").ap()
    qd = nc.dram_tensor("qd", (3 * 4 * T, P), F32, kind="Internal").ap()
    xd = nc.dram_tensor("xd", (NP + P, D), F32, kind="Internal").ap()
    xs = nc.dram_tensor("xs", (NP + P, D), F32, kind="Internal").ap()
    program(nc, out=out, qd=qd, xd=xd, xs=xs, **args)
    r = run(nc, [arrays], core_ids=[0])
    return r.results[0]["out"][:NODES]
```

```python
from contextlib import ExitStack

import concourse.bass as bass
from concourse import mybir

ALU = mybir.AluOpType
ACT = mybir.ActivationFunctionType
F32 = mybir.dt.float32
BF16 = mybir.dt.bfloat16
U8 = mybir.dt.uint8
I8 = mybir.dt.int8
U32 = mybir.dt.uint32
F8 = mybir.dt.float8e4
I32 = mybir.dt.int32
AXX = mybir.AxisListType.X

P = 128
NODES = 3327
T = 26
NP = T * P
D = 256
KC = D // P
VW = 260
E = 8
EPS = 1e-5
SLOPE = 0.2
PAIRS = T // 2
RUN_TILES = 2 * T + 8
SLOT_TILES = RUN_TILES + 2

MASK_AT = 0
MASK_WORDS = NP * T // 4
V_AT = MASK_AT + MASK_WORDS
WORK_AT = V_AT + T * VW
ARENA = 44184
QUICK_REACH = 60.0


def at(start, size):
    return bass.ds(start, size)


class Layer:

    def __init__(self, heads, bins, width):
        self.H = heads
        self.HD = D // heads
        self.B = bins
        self.W = width
        self.NQ = 3 if heads > 1 else 2
        self.blocks = NP // width
        self.tail = NP - self.blocks * width
        assert self.blocks % 2 == 0 and self.tail == 2 * P


L0 = Layer(1, 64, 384)
L1 = Layer(4, 32, 384)


def program(nc, x_in, adjT, w0T, w0, r0, w1, w1T, uv1, proj_wT, bias1, proj_b1,
            gate0, gate_b0, m0w1, m0b1, m0w2, m0b2, gate1, gate_b1, ln_g1, ln_b1, m1w1, m1b1, m1w2, m1b2,
            qd, xd, xs, out):
    ctx = ExitStack()
    with ctx:
        def sb(name, shape, dt=F32):
            return ctx.enter_context(nc.sbuf_tensor(name, shape, dt))

        def sem(name):
            held.append(nc.alloc_semaphore(name=name))
            return held[-1]

        held = []

        def hand_over():
            got, ones_ = list(held), list(start_at_one)
            held.clear()
            start_at_one.clear()
            return got, ones_

        bank = [ctx.enter_context(nc.psum_tensor(f"bank{i}", [P, 512], F32)) for i in range(8)]

        X = sb("X", [P, T * D])
        arena = sb("arena", [P, ARENA])

        def words(start, n):
            return arena[:, start:start + n]

        mask = words(MASK_AT, MASK_WORDS).bitcast(U8)
        V = words(V_AT, T * VW)

        ident = sb("ident", [P, P])
        zeros = sb("zeros", [P, 512], BF16)
        bin_no = sb("bin_no", [P, 64])
        stats = sb("stats", [P, T * 6])
        mv = sb("mv", [P, T * 3])
        rstd = sb("rstd", [P, T])
        s_all = sb("s_all", [P, 2 * 4 * T])
        reach = sb("reach", [P, 8])
        reach_all = sb("reach_all", [P, 8])
        bin_w = sb("bin_w", [P, 4])
        s_min = sb("s_min", [P, 4])
        top_add = sb("top_add", [P, 4])
        edges = sb("edges", [P, 128])
        found = sb("found", [P, 4 * T])
        m_row = sb("m_row", [P, 4 * T])
        q_cols = sb("q_cols", [P, 3 * 4 * T])
        d_all = sb("d_all", [P, 4 * T])
        neg_sj = sb("neg_sj", [P, 4 * T])
        far = sb("far", [P, 1])
        is_far = sb("is_far", [P, 1], I32)
        ones = sb("ones", [P, P], BF16)
        earlier = sb("earlier", [P, P], BF16)
        order8 = sb("order8", [P, E])
        fill_at = sb("fill_at", [P, T])
        tile_no = sb("tile_no", [P, SLOT_TILES])
        ones_t = sb("ones_t", [P, T])
        row_id = sb("row_id", [P, T])
        spare_row = sb("spare_row", [P, 1])
        slot_row = sb("slot_row", [P, SLOT_TILES], I32)
        expert_of = sb("expert_of", [1, SLOT_TILES], I32)
        slot_w = sb("slot_w", [P, SLOT_TILES])
        den = sb("den", [P, 16])
        rden = sb("rden", [P, 16])

        start_at_one = []

        x_loaded = sem("x_loaded")
        const_ready = sem("const_ready")
        mask_loaded = [sem("mask_loaded0"), sem("mask_loaded1")]

        def loads_sync(sp):
            for g in range(2):
                sp.dma_start(X[:, g * PAIRS * D:(g + 1) * PAIRS * D].rearrange("p (t d) -> p t d", d=D),
                             x_in[g * PAIRS * P:(g + 1) * PAIRS * P, :].rearrange("(t p) d -> p t d", p=P)
                             ).then_inc(x_loaded, 16)

        spare_clean = sem("spare_clean")
        id_zero = sem("id_zero")
        tri_base = sem("tri_base")

        def constants_gpsimd(pool):
            pool.memset(ident[:, :], 0.0).then_inc(id_zero, 1)
            pool.wait_ge(id_zero, 1)
            pool.affine_select(out=ident[:, :], in_=ident[:, :], compare_op=ALU.not_equal, fill=1.0, base=0,
                               pattern=[[-1, P]], channel_multiplier=1).then_inc(const_ready, 1)
            pool.memset(zeros[:, :], 0.0).then_inc(const_ready, 1)
            pool.iota(bin_no[:, :], [[1, 64]], base=0, channel_multiplier=0,
                      allow_small_or_imprecise_dtypes=True).then_inc(const_ready, 1)
            pool.memset(ones[:, :], 1.0).then_inc(tri_base, 1)
            pool.memset(earlier[:, :], 1.0).then_inc(tri_base, 1)
            pool.wait_ge(tri_base, 2)
            pool.affine_select(out=earlier[:, :], in_=earlier[:, :], compare_op=ALU.is_gt, fill=0.0, base=0,
                               pattern=[[1, P]], channel_multiplier=-1).then_inc(const_ready, 1)
            pool.iota(order8[:, :], [[-1, E]], base=E, channel_multiplier=0,
                      allow_small_or_imprecise_dtypes=True).then_inc(const_ready, 1)
            pool.iota(fill_at[:, :], [[P, T]], base=0, channel_multiplier=0,
                      allow_small_or_imprecise_dtypes=True).then_inc(const_ready, 1)
            pool.iota(tile_no[:, :], [[1, SLOT_TILES]], base=0, channel_multiplier=0,
                      allow_small_or_imprecise_dtypes=True).then_inc(const_ready, 1)
            pool.memset(ones_t[:, :], 1.0).then_inc(const_ready, 1)
            pool.iota(row_id[:, :], [[P, T]], base=1, channel_multiplier=1,
                      allow_small_or_imprecise_dtypes=True).then_inc(const_ready, 1)
            pool.iota(spare_row[:, :], [[1, 1]], base=NP + 1, channel_multiplier=1,
                      allow_small_or_imprecise_dtypes=True).then_inc(const_ready, 1)
        CONSTS = 10

        def mask_loads_gpsimd(pool):
            def load(pair, slot):
                for half in range(2):
                    c = 2 * pair + half
                    pool.dma_start(mask[:, at(c * NP, NP)].rearrange("p (a n) -> p a n", a=2),
                                   adjT[at(c * P, P), :].rearrange("p (a n) -> p a n", a=2)
                                   ).then_inc(mask_loaded[slot], 16)
            load(0, 0)
            load(1, 1)
            with pool.Fori(0, PAIRS // 2 - 1) as g:
                for slot in range(2):
                    pool.wait_ge(mask_loaded[slot], 32 * g + 32)
                    load(2 * g + 2 + slot, slot)
            pool.wait_ge(mask_loaded[0], 32 * 6)
            load(PAIRS - 1, 0)

        class Attention:
            def __init__(self, L, tag):
                self.L, self.tag = L, tag
                H, B = L.H, L.B
                k = WORK_AT
                self.w_cols = H * L.HD + 2 * H
                self.wmat = words(k, KC * self.w_cols)
                k += KC * self.w_cols
                self.wT = words(k, KC * D)
                k += KC * D
                self.attn_vec = words(k, KC * 2 * H)
                k += KC * 2 * H
                self.proj = words(k, KC * D)
                k += KC * D
                self.pbias = words(k, 2 * D)
                k += 2 * D
                self.xn = [words(k + s * D, D) for s in range(2)]
                k += 2 * D
                self.xt = [words(k + s * D, D) for s in range(2)]
                k += 2 * D
                self.conv = [words(k + s * NP // 2, NP // 2).bitcast(BF16) for s in range(2)]
                k += NP
                self.above = words(k, T * H * B // 2).bitcast(BF16)
                k += T * H * B // 2
                self.cpos = words(k, T * H * B)
                k += T * H * B
                self.qt = words(k, L.NQ * P)
                k += L.NQ * P
                assert k <= ARENA, (tag, k)
                k = WORK_AT
                RW = L.NQ * H * L.W
                self.rows = [words(k + r * RW, RW) for r in range(2)]
                k += 2 * RW
                self.slots = 2 if H > 1 else 4
                self.prob = [words(k + s * H * L.W, H * L.W) for s in range(self.slots)]
                k += self.slots * H * L.W
                if H > 1:
                    self.live = [words(k + s * H * L.W // 4, H * L.W // 4).bitcast(U8) for s in range(2)]
                    k += 2 * H * L.W // 4
                else:
                    self.attn_out = words(k, T * D)
                    k += T * D
                assert k <= ARENA, (tag, k)
                self.nt = L.W // P
                if H > 1:
                    self.exp_bank = [bank[4 + h] for h in range(4)]
                else:
                    self.exp_bank = [bank[6], bank[7]]
                self.w_loaded = sem(tag + "w_loaded")
                self.stat = sem(tag + "stat")
                self.aggr = sem(tag + "aggr")
                self.var_ready = sem(tag + "var_ready")
                self.sd_ready = sem(tag + "sd_ready")
                self.rstd_ready = sem(tag + "rstd_ready")
                self.wvec_ready = sem(tag + "wvec_ready")
                self.wvec_copied = sem(tag + "wvec_copied")
                self.reach_part = sem(tag + "reach_part")
                self.reach_ready = sem(tag + "reach_ready")
                self.bin_steps = sem(tag + "bin_steps")
                self.far_steps = sem(tag + "far_steps")
                self.edge_ready = sem(tag + "edge_ready")
                self.above_ready = sem(tag + "above_ready")
                self.cnt_done = sem(tag + "cnt_done")
                self.cpos_done = sem(tag + "cpos_done")
                self.found_done = sem(tag + "found_done")
                self.top_done = sem(tag + "top_done")
                self.m_steps = sem(tag + "m_steps")
                self.exps = sem(tag + "exps")
                self.qt_ready = sem(tag + "qt_ready")
                self.qt_copied = sem(tag + "qt_copied")
                self.q_stored = sem(tag + "q_stored")
                self.pb = sem(tag + "pb")
                self.xn_ready = [sem(f"{tag}xn_ready{s}") for s in range(2)]
                self.tp_ready = [sem(f"{tag}tp_ready{s}") for s in range(2)]
                self.xt_ready = [sem(f"{tag}xt_ready{s}") for s in range(2)]
                self.vp_ready = [sem(f"{tag}vp_ready{s}") for s in range(2)]
                self.vp_free = [sem(f"{tag}vp_free{s}") for s in range(2)]
                self.conv_a = [sem(f"{tag}conv_a{s}") for s in range(2)]
                self.conv_v = [sem(f"{tag}conv_v{s}") for s in range(2)]
                self.conv_used = [sem(f"{tag}conv_used{s}") for s in range(2)]
                self.before_attend = list(held)
                self.rows_loaded = [sem(f"{tag}rows_loaded{s}") for s in range(2)]
                self.rows_free = [sem(f"{tag}rows_free{s}") for s in range(2)]
                self.prob_ready = [sem(f"{tag}prob_ready{s}") for s in range(self.slots)]
                self.prob_used = [sem(f"{tag}prob_used{s}") for s in range(self.slots)]
                n_exp = len(self.exp_bank)
                self.exp_ready = [sem(f"{tag}exp_ready{k}") for k in range(n_exp)]
                self.exp_used = [sem(f"{tag}exp_used{k}") for k in range(n_exp)]
                self.live_ready = sem(tag + "live_ready")
                self.acc_free = sem(tag + "acc_free")
                self.banks_free = [sem(f"{tag}banks_free{r}") for r in range(2 * (H == 1))]
                self.acc_done = [sem(f"{tag}acc_done{r}") for r in range(2 * (H == 1))]
                self.b_done = sem(tag + "b_done")
                self.out_ready = sem(tag + "out_ready")
                self.x_added = sem(tag + "x_added")
                self.x_kept = sem(tag + "x_kept")
                start_at_one.extend(self.tp_ready + self.vp_ready + self.xt_ready + self.vp_free + self.conv_used
                                    + self.rows_free + self.exp_used + self.prob_used + self.banks_free + [self.acc_free])

            def values_sync(self, sp):
                wc = self.w_cols
                mats = [(w0T, w0, r0), (w1, w1T, uv1)][self.L.H > 1]
                nw = self.L.H * self.L.HD
                sp.dma_start(self.wmat.rearrange("p (k n) -> p k n", n=wc)[:, :, 0:nw],
                             mats[0].rearrange("(k p) n -> p k n", p=P)).then_inc(self.w_loaded, 16)
                sp.dma_start(self.wT.rearrange("p (k n) -> p k n", n=D),
                             mats[1].rearrange("(k p) n -> p k n", p=P)).then_inc(self.w_loaded, 16)
                sp.dma_start(self.attn_vec.rearrange("p (k n) -> p k n", k=KC),
                             mats[2].rearrange("(k p) n -> p k n", p=P)).then_inc(self.w_loaded, 16)
                if self.L.H > 1:
                    sp.dma_start(self.proj.rearrange("p (k n) -> p k n", n=D),
                                 proj_wT.rearrange("(k p) n -> p k n", p=P)).then_inc(self.w_loaded, 16)
                    sp.dma_start(self.pbias[:, 0:D], bias1.partition_broadcast(P)).then_inc(self.w_loaded, 16)
                    sp.dma_start(self.pbias[:, D:2 * D], proj_b1.partition_broadcast(P)).then_inc(self.w_loaded, 16)

            def values_vector(self, v):
                L, H = self.L, self.L.H
                layer_norm_stats(v, self)
                v.wait_ge(self.wvec_ready, 1)
                nw = H * L.HD
                v.tensor_copy(self.wmat.rearrange("p (k n) -> p k n", k=KC)[:, :, nw:],
                              bank[4][:, 0:KC * 2 * H].rearrange("p (k n) -> p k n", k=KC)
                              ).then_inc(self.wvec_copied, 1)
                if H > 1:
                    v.memset(V.rearrange("p (c n) -> p c n", n=65)[:, :, 64:65], 1.0)
                    v.tensor_tensor(self.pbias[:, 0:D], self.pbias[:, 0:D], self.pbias[:, D:2 * D],
                                    ALU.add).then_inc(self.pb, 1)
                    v.wait_ge(self.pb, 1)
                else:
                    v.memset(V.rearrange("p (c n) -> p c n", n=VW)[:, :, D:D + 1], 1.0)
                s_cols = s_all[:, 0:2 * H * T].rearrange("p (q t) -> p t q", t=T)

                def norm(i, s):
                    t = 2 * i + s
                    v.wait_ge(self.tp_ready[s], i + 1)
                    v.tensor_scalar(self.xn[s], X[:, at(t * D, D)], mv[:, at(t, 1)], rstd[:, at(t, 1)],
                                    ALU.subtract, ALU.mult).then_inc(self.xn_ready[s], 1)

                def keep(i, s):
                    t = 2 * i + s
                    vb = bank[2 + s]
                    v.wait_ge(self.vp_ready[s], i + 1 + 1)
                    if H > 1:
                        v.tensor_copy(V[:, at(t * VW, VW)].rearrange("p (h n) -> p h n", n=65)[:, :, 0:64],
                                      vb[:, 0:D].rearrange("p (h n) -> p h n", n=64))
                        v.tensor_tensor(X[:, at(t * D, D)], X[:, at(t * D, D)], self.pbias[:, 0:D],
                                        ALU.add).then_inc(self.pb, 1)
                        v.wait_ge(self.pb, t + 2)
                        v.tensor_tensor(X[:, at(t * D, D)], bank[5 + s][:, 0:D], X[:, at(t * D, D)], ALU.add)
                    else:
                        v.tensor_copy(V[:, at(t * VW, D)], vb[:, 0:D])
                    v.tensor_copy(s_cols[:, at(t, 1), :], vb[:, D:D + 2 * H].rearrange("p (o q) -> p o q", o=1)
                                  ).then_inc(self.vp_free[s], 1)

                for s in range(2):
                    norm(0, s)
                with v.Fori(0, PAIRS - 1) as i:
                    for s in range(2):
                        norm(i + 1, s)
                        keep(i, s)
                for s in range(2):
                    keep(PAIRS - 1, s)

            def values_scalar(self, a):
                layer_norm_sqrt(a, self)
                with a.Fori(0, PAIRS) as i:
                    for s in range(2):
                        a.wait_ge(self.tp_ready[s], i + 1 + 1)
                        a.wait_ge(self.vp_ready[s], i + 1)
                        a.copy(self.xt[s], bank[s][:, 0:D]).then_inc(self.xt_ready[s], 1)

            def values_tensor(self, pe):
                L, H = self.L, self.L.H
                pe.wait_ge(const_ready, CONSTS)
                pe.wait_ge(self.w_loaded, 48 if H == 1 else 96)
                for k in range(KC):
                    for o in range(KC):
                        last = pe.matmul(bank[4][:, k * 2 * H:(k + 1) * 2 * H],
                                         self.wT[:, o * D + k * P:o * D + k * P + P],
                                         self.attn_vec[:, o * 2 * H:(o + 1) * 2 * H],
                                         start=(o == 0), stop=(o == KC - 1))
                last.then_inc(self.wvec_ready, 1)
                pe.wait_ge(self.wvec_copied, 1)

                def turn(i, s):
                    pe.wait_ge(self.xn_ready[s], i + 1)
                    pe.wait_ge(self.xt_ready[s], i + 1)
                    for k in range(KC):
                        last = pe.transpose(bank[s][:, k * P:(k + 1) * P], self.xn[s][:, k * P:(k + 1) * P],
                                            ident[:, :])
                    last.then_inc(self.tp_ready[s], 1)

                def products(i, s):
                    pe.wait_ge(self.xt_ready[s], i + 1 + 1)
                    pe.wait_ge(self.vp_free[s], i + 1)
                    if H > 1:
                        for k in range(KC):
                            pe.matmul(bank[5 + s][:, 0:D], self.xt[s][:, k * P:(k + 1) * P],
                                      self.proj[:, k * D:(k + 1) * D], start=(k == 0), stop=(k == KC - 1))
                    for k in range(KC):
                        last = pe.matmul(bank[2 + s][:, 0:self.w_cols], self.xt[s][:, k * P:(k + 1) * P],
                                         self.wmat[:, k * self.w_cols:(k + 1) * self.w_cols],
                                         start=(k == 0), stop=(k == KC - 1))
                    last.then_inc(self.vp_ready[s], 1)

                turn(0, 0)
                with pe.Fori(0, PAIRS - 1) as i:
                    for s in range(2):
                        turn(i + s, 1 - s)
                        products(i, s)
                turn(PAIRS - 1, 1)
                for s in range(2):
                    products(PAIRS - 1, s)

            def bins_vector(self, v):
                L, H, B = self.L, self.L.H, self.L.B
                sj = s_all[:, 0:H * T].rearrange("p (h t) -> p h t", t=T)
                for s in range(2):
                    v.wait_ge(self.vp_free[s], PAIRS + 1)
                v.tensor_reduce(reach[:, 0:H], sj, AXX, ALU.max).then_inc(self.reach_part, 1)
                v.tensor_reduce(reach[:, H:2 * H], sj, AXX, ALU.min, negate=True).then_inc(self.reach_part, 1)
                if H > 1:
                    v.tensor_scalar(neg_sj[:, 0:H * T], s_all[:, 0:H * T], -1.0, None, ALU.mult)
                v.wait_ge(self.reach_ready, 1)
                if H > 1:
                    v.tensor_reduce(far[:, :], reach_all[:, 0:2 * H], AXX, ALU.max).then_inc(self.far_steps, 1)
                    v.wait_ge(self.far_steps, 1)
                    v.tensor_scalar(is_far[:, :], far[:, :], QUICK_REACH, None, ALU.is_ge)
                v.tensor_tensor(bin_w[:, 0:H], reach_all[:, 0:H], reach_all[:, H:2 * H], ALU.add
                                ).then_inc(self.bin_steps, 1)
                v.tensor_scalar(s_min[:, 0:H], reach_all[:, H:2 * H], -1.0, None, ALU.mult
                                ).then_inc(self.bin_steps, 1)
                v.wait_ge(self.bin_steps, 2)
                v.tensor_scalar(bin_w[:, 0:H], bin_w[:, 0:H], 1.0 / B, None, ALU.mult).then_inc(self.bin_steps, 1)
                v.wait_ge(self.bin_steps, 3)
                v.scalar_tensor_tensor(out=top_add[:, 0:H], in0=bin_w[:, 0:H], scalar=0.125, in1=s_min[:, 0:H],
                                       op0=ALU.mult, op1=ALU.add).then_inc(self.bin_steps, 1)
                v.wait_ge(const_ready, CONSTS)
                for h in range(H):
                    v.tensor_scalar(edges[:, h * B:(h + 1) * B], bin_no[:, 0:B], bin_w[:, h:h + 1], s_min[:, h:h + 1],
                                    ALU.mult, ALU.add).then_inc(self.edge_ready, 1)
                v.wait_ge(self.edge_ready, H)
                e3 = edges[:, 0:H * B].rearrange("p (h b) -> p h b", b=B)
                above = self.above.rearrange("p (t h b) -> p h t b", h=H, b=B)
                for h in range(H):
                    v.tensor_tensor(above[:, h, :, :],
                                    sj[:, h, :].rearrange("p (t o) -> p t o", o=1).to_broadcast([P, T, B]),
                                    e3[:, h, :].rearrange("p (o b) -> p o b", o=1).to_broadcast([P, T, B]),
                                    ALU.is_ge).then_inc(self.above_ready, 1)

            def bins_gpsimd(self, pool):
                H = self.L.H
                pool.wait_ge(self.reach_part, 2)
                pool.partition_all_reduce(reach_all[:, 0:2 * H], reach[:, 0:2 * H], P, bass.bass_isa.ReduceOp.max
                                          ).then_inc(self.reach_ready, 1)

            CA = 1792

            def count_pairs(self, eng, body):
                with eng.Fori(0, PAIRS // 2) as g:
                    for half in range(2):
                        body(2 * g + half, g, half)
                body(PAIRS - 1, PAIRS // 2, 0)

            def count_scalar(self, a):
                def body(pair, g, half):
                    a.wait_ge(mask_loaded[half], 32 * (g + 1))
                    for s in range(2):
                        a.wait_ge(self.conv_used[s], pair + 1)
                        a.copy(self.conv[s][:, 0:self.CA], mask[:, at((2 * pair + s) * NP, self.CA)]
                               ).then_inc(self.conv_a[s], 1)
                self.count_pairs(a, body)

            def count_vector(self, v):
                def body(pair, g, half):
                    v.wait_ge(mask_loaded[half], 32 * (g + 1))
                    for s in range(2):
                        v.wait_ge(self.conv_used[s], pair + 1)
                        v.tensor_copy(self.conv[s][:, self.CA:NP],
                                      mask[:, at((2 * pair + s) * NP + self.CA, NP - self.CA)]
                                      ).then_inc(self.conv_v[s], 1)
                self.count_pairs(v, body)

            def count_tensor(self, pe):
                H, B = self.L.H, self.L.B
                HB = H * B
                per = 512 // HB
                nb = -(-T // per)
                pe.wait_ge(self.edge_ready, H)
                for b in range(nb):
                    pe.matmul(bank[b][:, :], zeros[:, 0:P], zeros[:, :], start=True, stop=True)
                pe.wait_ge(self.above_ready, H)
                with pe.Fori(0, PAIRS) as pair:
                    for s in range(2):
                        pe.wait_ge(self.conv_a[s], pair + 1)
                        pe.wait_ge(self.conv_v[s], pair + 1)
                        for t in range(T):
                            last = pe.matmul(bank[t // per][:, t % per * HB:(t % per + 1) * HB],
                                             self.conv[s][:, t * P:(t + 1) * P],
                                             self.above[:, at((2 * pair + s) * HB, HB)],
                                             start=False, stop=False, skip_group_check=True)
                        last.then_inc(self.conv_used[s], 1)

            def rows_vector(self, v):
                L, H, B = self.L, self.L.H, self.L.B
                HB, HT = H * B, H * T
                per = 512 // HB
                nb = -(-T // per)
                for s in range(2):
                    v.wait_ge(self.conv_used[s], PAIRS + 1)
                for b in range(nb):
                    n = min(per, T - b * per) * HB
                    v.tensor_scalar(self.cpos[:, b * per * HB:b * per * HB + n], bank[b][:, 0:n], 0.0, None, ALU.is_gt
                                    ).then_inc(self.cpos_done, 1)
                v.wait_ge(self.cpos_done, nb)
                f3 = found[:, 0:HT].rearrange("p (h t) -> p h t", t=T)
                for h in range(H):
                    v.tensor_reduce(f3[:, h, :], self.cpos.rearrange("p (t h b) -> p h t b", h=H, b=B)[:, h, :, :],
                                    AXX, ALU.add).then_inc(self.found_done, 1)
                v.wait_ge(self.found_done, H)
                for h in range(H):
                    v.tensor_scalar(m_row[:, h * T:(h + 1) * T], found[:, h * T:(h + 1) * T], bin_w[:, h:h + 1],
                                    top_add[:, h:h + 1], ALU.mult, ALU.add).then_inc(self.top_done, 1)
                v.wait_ge(self.top_done, H)
                si = s_all[:, HT:2 * HT]
                m = m_row[:, 0:HT]
                v.tensor_tensor(m, si, m, ALU.add).then_inc(self.m_steps, 1)
                v.wait_ge(self.m_steps, 1)
                v.scalar_tensor_tensor(out=found[:, 0:HT], in0=m, scalar=SLOPE, in1=m, op0=ALU.mult, op1=ALU.max
                                       ).then_inc(self.m_steps, 1)
                v.wait_ge(self.m_steps, 2)
                v.tensor_tensor(q_cols[:, 0:HT], si, found[:, 0:HT], ALU.subtract).then_inc(self.m_steps, 1)
                v.scalar_tensor_tensor(out=q_cols[:, HT:2 * HT], in0=si, scalar=SLOPE, in1=found[:, 0:HT],
                                       op0=ALU.mult, op1=ALU.subtract).then_inc(self.m_steps, 1)
                if H > 1:
                    v.tensor_copy(q_cols[:, 2 * HT:3 * HT], si).then_inc(self.m_steps, 1)
                for q in range(L.NQ):
                    v.wait_ge(self.qt_ready, q + 1)
                    last = v.tensor_copy(self.qt[0:HT, q * P:(q + 1) * P], bank[q][0:HT, 0:P]
                                         ).then_inc(self.qt_copied, 1)

            def rows_scalar(self, a):
                HT = self.L.H * T
                a.activation(d_all[:, 0:HT], s_all[:, 0:HT], ACT.Exp, scale=SLOPE)
                a.wait_ge(self.m_steps, 4 if self.L.H == 1 else 5)
                a.activation(q_cols[:, HT:2 * HT], q_cols[:, HT:2 * HT], ACT.Exp).then_inc(self.exps, 1)

            def rows_tensor(self, pe):
                HT = self.L.H * T
                pe.wait_ge(self.exps, 1)
                pe.wait_ge(self.cpos_done, 1)
                for q in range(self.L.NQ):
                    pe.transpose(bank[q][0:HT, 0:P], q_cols[:, q * HT:(q + 1) * HT], ident[:, :]
                                 ).then_inc(self.qt_ready, 1)

            def rows_sync(self, sp):
                HT = self.L.H * T
                sp.wait_ge(self.qt_copied, self.L.NQ)
                sp.dma_start(qd[0:self.L.NQ * HT, :].rearrange("(q r) p -> r q p", r=HT),
                             self.qt[0:HT, :].rearrange("r (q p) -> r q p", p=P)).then_inc(self.q_stored, 16)
                sp.wait_ge(self.q_stored, 16)

            def each_block(self, eng, body):
                with eng.Fori(0, self.L.blocks // 2) as bp:
                    for r in range(2):
                        body(2 * bp + r, bp, r, self.nt)
                body(self.L.blocks, self.L.blocks // 2, 0, self.L.tail // P)

            def attend_sync(self, sp):
                L = self.L
                q_all = qd[0:L.NQ * L.H * T, :].rearrange("(r t) p -> r (t p)", t=T)

                def body(b, bp, r, nt):
                    sp.wait_ge(self.rows_free[r], bp + 1)
                    w = nt * P
                    sp.dma_start(self.rows[r].rearrange("p (q w) -> p q w", w=L.W)[:, :, 0:w],
                                 q_all[:, at(b * L.W, w)].partition_broadcast(P)).then_inc(self.rows_loaded[r], 16)
                self.each_block(sp, body)

            def attend_scalar(self, a):
                L, H = self.L, self.L.H

                def body(b, bp, r, nt):
                    a.wait_ge(self.rows_loaded[r], 16 * (bp + 1))
                    with a.Fori(0, PAIRS) as i:
                        for s in range(2):
                            for h in range(H):
                                a.wait_ge(self.exp_used[h], b * T + 2 * i + s + 1)
                                a.activation(self.exp_bank[h][:, 0:nt * P], self.rows[r][:, h * L.W:h * L.W + nt * P],
                                             ACT.Exp, bias=s_all[:, at(h * T + 2 * i + s, 1)]
                                             ).then_inc(self.exp_ready[h], 1)
                self.each_block(a, body)

            def attend_vector(self, v):
                L, H, W = self.L, self.L.H, self.L.W

                def body(b, bp, r, nt):
                    w = nt * P
                    rows = self.rows[r]
                    with v.Fori(0, PAIRS) as i:
                        for s in range(2):
                            c = 2 * i + s
                            v.wait_ge(self.prob_used[s], b * PAIRS + i + 1)
                            for h in range(H):
                                v.wait_ge(self.exp_ready[h], b * T + c + 1)
                                v.scalar_tensor_tensor(
                                    out=self.prob[s][:, h * W:h * W + w], in0=rows[:, (H + h) * W:(H + h) * W + w],
                                    scalar=d_all[:, at(h * T + c, 1)], in1=self.exp_bank[h][:, 0:w],
                                    op0=ALU.mult, op1=ALU.max).then_inc(self.exp_used[h], 1)
                                v.scalar_tensor_tensor(
                                    out=self.live[s][:, h * W:h * W + w],
                                    in0=rows[:, (2 * H + h) * W:(2 * H + h) * W + w],
                                    scalar=neg_sj[:, at(h * T + c, 1)], in1=mask[:, at(c * NP + b * W, w)],
                                    op0=ALU.not_equal, op1=ALU.mult).then_inc(self.live_ready, 1)
                            v.wait_ge(self.exp_used[H - 1], b * T + c + 2)
                            v.wait_ge(self.live_ready, H * (b * T + c + 1))
                            pv = self.prob[s].rearrange("p (h w) -> p h w", w=W)[:, :, 0:w]
                            v.tensor_tensor(pv, pv, self.live[s].rearrange("p (h w) -> p h w", w=W)[:, :, 0:w],
                                            ALU.min).then_inc(self.prob_ready[s], 1)
                    for s in range(2):
                        v.wait_ge(self.prob_used[s], (b + 1) * PAIRS + 1)
                    for n in range(nt):
                        acc = bank[n][:, 0:H * (L.HD + 1)].rearrange("p (h x) -> p h x", h=H)
                        v.tensor_copy(den[:, n * H:(n + 1) * H], acc[:, :, L.HD]).then_inc(self.b_done, 1)
                    done = b * (self.nt + 2) + nt
                    v.wait_ge(self.b_done, done)
                    v.scalar_tensor_tensor(out=den[:, 0:nt * H], in0=den[:, 0:nt * H], scalar=0.0,
                                           in1=den[:, 0:nt * H], op0=ALU.is_equal, op1=ALU.add
                                           ).then_inc(self.b_done, 1)
                    v.wait_ge(self.b_done, done + 1)
                    v.reciprocal(rden[:, 0:nt * H], den[:, 0:nt * H]).then_inc(self.b_done, 1)
                    v.wait_ge(self.b_done, done + 2)
                    for n in range(nt):
                        t = b * self.nt + n
                        for h in range(H):
                            xh = X[:, at(t * D + h * 64, 64)]
                            last = v.scalar_tensor_tensor(out=xh, in0=bank[n][:, h * 65:h * 65 + 64],
                                                          scalar=rden[:, n * H + h:n * H + h + 1], in1=xh,
                                                          op0=ALU.mult, op1=ALU.add)
                    last.then_inc(self.acc_free, 1)
                    v.wait_ge(self.acc_free, b + 1 + 1)
                    v.sem_inc(self.rows_free[r], 1)
                self.each_block(v, body)

            def attend_tensor(self, pe):
                L, H, W = self.L, self.L.H, self.L.W
                cols = H * (L.HD + 1)

                def body(b, bp, r, nt):
                    pe.wait_ge(self.acc_free, b + 1)
                    for n in range(nt):
                        pe.matmul(bank[n][:, 0:cols], zeros[:, 0:P], zeros[:, 0:cols], start=True, stop=True)
                    with pe.Fori(0, PAIRS) as i:
                        for s in range(2):
                            c = 2 * i + s
                            pe.wait_ge(self.prob_ready[s], b * PAIRS + i + 1)
                            for n in range(nt):
                                for h in range(H):
                                    hw = L.HD + 1
                                    last = pe.matmul(bank[n][:, h * hw:(h + 1) * hw],
                                                     self.prob[s][:, h * W + n * P:h * W + (n + 1) * P],
                                                     V[:, at(c * VW + h * hw, hw)],
                                                     start=False, stop=False, skip_group_check=True)
                            last.then_inc(self.prob_used[s], 1)
                self.each_block(pe, body)

            def each_chunk(self, eng, body):
                with eng.Fori(0, T // 4) as i:
                    for q in range(4):
                        body(4 * i + q, q, i)
                for q in range(T % 4):
                    body(T // 4 * 4 + q, q, T // 4)

            def single_scalar(self, a):
                def body(b, bp, r, nt):
                    a.wait_ge(self.rows_loaded[r], 16 * (bp + 1))

                    def chunk(c, q, i):
                        s, used = q % 2, b * PAIRS + 2 * i + q // 2
                        a.wait_ge(self.exp_used[s], used + 1)
                        a.activation(self.exp_bank[s][:, 0:nt * P], self.rows[r][:, 0:nt * P], ACT.Exp,
                                     bias=s_all[:, at(c, 1)]).then_inc(self.exp_ready[s], 1)
                    self.each_chunk(a, chunk)
                self.each_block(a, body)

            def single_vector(self, v):
                L, W, nt_ = self.L, self.L.W, self.nt

                def larger(b, r, nt, c, q, i):
                    w, s, used = nt * P, q % 2, b * PAIRS + 2 * i + q // 2
                    v.wait_ge(self.prob_used[q], b * (7 - q // 2) + i + 1)
                    v.wait_ge(self.exp_ready[s], used + 1)
                    v.scalar_tensor_tensor(out=self.prob[q][:, 0:w], in0=self.rows[r][:, W:W + w],
                                           scalar=d_all[:, at(c, 1)], in1=self.exp_bank[s][:, 0:w],
                                           op0=ALU.mult, op1=ALU.max).then_inc(self.exp_used[s], 1)

                def masked(b, nt, c, q, i):
                    w, s, used = nt * P, q % 2, b * PAIRS + 2 * i + q // 2
                    v.wait_ge(self.exp_used[s], used + 2)
                    v.tensor_tensor(self.prob[q][:, 0:w], self.prob[q][:, 0:w], mask[:, at(c * NP + b * W, w)],
                                    ALU.min).then_inc(self.prob_ready[q], 1)

                def normalise(b, bp, r, nt):
                    v.wait_ge(self.acc_done[r], bp + 1)
                    for n in range(nt):
                        last = v.reciprocal(rden[:, n:n + 1], bank[3 * r + n][:, D:D + 1])
                    last.then_inc(self.b_done, 1)
                    v.wait_ge(self.b_done, b + 1)
                    for n in range(nt):
                        last = v.tensor_scalar(self.attn_out[:, at((b * nt_ + n) * D, D)], bank[3 * r + n][:, 0:D],
                                               rden[:, n:n + 1], None, ALU.mult)
                    last.then_inc(self.banks_free[r], 1)

                def body(b, bp, r, nt, earlier_block=None):
                    larger(b, r, nt, 0, 0, 0)
                    for q in range(4):
                        larger(b, r, nt, q + 1, (q + 1) % 4, (q + 1) // 4)
                        masked(b, nt, q, q, 0)
                    if earlier_block is not None:
                        normalise(*earlier_block)
                    with v.Fori(1, T // 4) as i:
                        for q in range(4):
                            larger(b, r, nt, 4 * i + q + 1, (q + 1) % 4, i + (q + 1) // 4)
                            masked(b, nt, 4 * i + q, q, i)
                    n = T // 4
                    larger(b, r, nt, T - 1, 1, n)
                    for q in range(2):
                        masked(b, nt, 4 * n + q, q, n)
                    v.wait_ge(self.prob_ready[1], (b + 1) * 7)
                    v.sem_inc(self.rows_free[r], 1)

                B = L.blocks
                body(0, 0, 0, nt_)
                with v.Fori(0, (B - 2) // 2) as j:
                    body(2 * j + 1, j, 1, nt_, (2 * j, j, 0, nt_))
                    body(2 * j + 2, j + 1, 0, nt_, (2 * j + 1, j, 1, nt_))
                body(B - 1, B // 2 - 1, 1, nt_, (B - 2, B // 2 - 1, 0, nt_))
                body(B, B // 2, 0, L.tail // P, (B - 1, B // 2 - 1, 1, nt_))
                normalise(B, B // 2, 0, L.tail // P)

            def single_tensor(self, pe):
                L = self.L

                def body(b, bp, r, nt):
                    pe.wait_ge(self.banks_free[r], bp + 1)
                    for n in range(nt):
                        pe.matmul(bank[3 * r + n][:, 0:D + 1], zeros[:, 0:P], zeros[:, 0:D + 1], start=True,
                                  stop=True)

                    def chunk(c, q, i):
                        pe.wait_ge(self.prob_ready[q], b * (7 - q // 2) + i + 1)
                        for n in range(nt):
                            last = pe.matmul(bank[3 * r + n][:, 0:D + 1], self.prob[q][:, n * P:(n + 1) * P],
                                             V[:, at(c * VW, D + 1)], start=False, stop=False,
                                             skip_group_check=True)
                        last.then_inc(self.prob_used[q], 1)
                    self.each_chunk(pe, chunk)
                    pe.matmul(bank[3 * r][:, 0:64], zeros[:, 0:P], zeros[:, 0:64], start=False, stop=False,
                              skip_group_check=True).then_inc(self.acc_done[r], 1)
                self.each_block(pe, body)

            def gelu_scalar(self, a):
                a.wait_ge(self.banks_free[0], self.L.blocks // 2 + 1 + 1)
                for i in range(PAIRS):
                    o = self.attn_out[:, i * 2 * D:(i + 1) * 2 * D]
                    a.activation(o, o, ACT.Gelu).then_inc(self.out_ready, 1)

            def gelu_vector(self, v):
                with v.Fori(0, PAIRS) as i:
                    v.wait_ge(self.out_ready, i + 1)
                    xs = X[:, at(i * 2 * D, 2 * D)]
                    v.tensor_tensor(xs, xs, self.attn_out[:, at(i * 2 * D, 2 * D)], ALU.add
                                    ).then_inc(self.x_added, 1)

            def gelu_sync(self, sp):
                with sp.Fori(0, PAIRS) as i:
                    sp.wait_ge(self.x_added, i + 1)
                    sp.dma_start(xd[at(i * 2 * P, 2 * P), :].rearrange("(t p) d -> p t d", p=P),
                                 X[:, at(i * 2 * D, 2 * D)].rearrange("p (t d) -> p t d", d=D)
                                 ).then_inc(self.x_kept, 16)
                sp.wait_ge(self.x_kept, 16 * PAIRS)


        class Signed:

            W = 512
            NT = W // P
            BLOCKS = NP // W
            STEP = 4
            STEPS = T // STEP
            HC = 65
            KW = 3 * HC
            FIRST = 6

            def __init__(self, A, tag):
                self.A, self.H = A, A.L.H
                assert self.BLOCKS == 6 and NP - 6 * self.W == self.W // 2 and T == 4 * self.STEPS + 2
                k = WORK_AT
                pw = T * 2 * self.KW // 2
                self.parts = [words(k + s * pw, pw).bitcast(BF16) for s in range(2)]
                k += 2 * pw
                self.row = [words(k + r * self.W, self.W) for r in range(2)]
                k += 2 * self.W
                sw = self.STEP * self.W // 4
                self.sign = [words(k + s * sw, sw) for s in range(2)]
                k += 2 * sw
                self.split = []
                for size in (sw, sw, sw // 2):
                    self.split.append([words(k, size), words(k + size, size)])
                    k += 2 * size
                tw = 2 * 2 * self.HC
                self.scaled = [words(k + s * tw, tw) for s in range(2)]
                k += 2 * tw
                self.sums = words(k, self.NT * 2 * self.HC)
                k += self.NT * 2 * self.HC
                assert k <= ARENA, k
                self.exp_sj = neg_sj
                self.exp_ready = sem(tag + "exp_ready")
                self.scale_steps = [sem(tag + "scale_pool"), sem(tag + "scale_dve")]
                self.parts_ready = [sem(f"{tag}parts_ready{s}") for s in range(2)]
                self.first_ready = sem(tag + "first_ready")
                self.parts_used = [sem(f"{tag}parts_used{s}") for s in range(2)]
                self.row_loaded = [sem(f"{tag}row_loaded{r}") for r in range(2)]
                self.row_used = [sem(f"{tag}row_used{r}") for r in range(2)]
                self.sign_ready = [sem(f"{tag}sign_ready{s}") for s in range(2)]
                self.sign_used = [sem(f"{tag}sign_used{s}") for s in range(2)]
                self.differs = sem(tag + "differs")
                self.split_ready = [sem(f"{tag}split_ready{s}") for s in range(3)]
                self.split_used = [sem(f"{tag}split_used{s}") for s in range(3)]
                self.block_done = [sem(f"{tag}block_done{r}") for r in range(2)]
                self.bank_free = [sem(f"{tag}bank_free{r}") for r in range(2)]
                self.fold_steps = sem(tag + "fold_steps")
                self.waited = {e: sem(tag + "waited_" + e) for e in ("a", "dve", "pe", "pool")}
                start_at_one.extend(self.row_used + self.sign_used + self.split_used + self.bank_free)

            def each_block(self, eng, body):
                with eng.Fori(0, self.BLOCKS // 2) as j:
                    for r in range(2):
                        body(j, r, self.NT)
                body(self.BLOCKS // 2, 0, self.NT // 2)

            def row_sync(self, sp):
                H = self.H
                flat = qd.rearrange("r p -> (r p)")
                with sp.Fori(0, H) as h:
                    def body(j, r, nt):
                        sp.wait_ge(self.row_used[r], h * (4 - r) + j + 1)
                        sp.dma_start(self.row[r][:, 0:nt * P],
                                     flat[at(((2 * H + h) * T) * P + (2 * j + r) * self.W, nt * P)]
                                     .partition_broadcast(P)).then_inc(self.row_loaded[r], 16)
                    self.each_block(sp, body)

            def sign_scalar(self, a):
                H, W = self.H, self.W
                a.activation(self.exp_sj[:, 0:H * T], s_all[:, 0:H * T], ACT.Exp).then_inc(self.exp_ready, 1)
                a.activation(q_cols[:, 0:H * T], q_cols[:, 0:H * T], ACT.Exp).then_inc(self.exp_ready, 1)
                with a.Fori(0, H) as h:
                    def body(j, r, nt):
                        b = h * 7 + 2 * j + r

                        def step(c, chunks, slot, nth):
                            a.wait_ge(self.sign_used[slot], nth + 1)
                            a.sem_inc(self.waited["a"], 1)
                            for q in range(chunks):
                                last = a.activation(self.sign[slot].bitcast(I8)[:, q * W:q * W + nt * P],
                                                    self.row[r][:, 0:nt * P], ACT.Sign,
                                                    bias=s_all[:, at(h * T + c + q, 1)])
                            last.then_inc(self.sign_ready[slot], 1)
                            return last

                        a.wait_ge(self.row_loaded[r], (h * (4 - r) + j + 1) * 16)
                        with a.Fori(0, self.STEPS // 2) as i:
                            for s in range(2):
                                step((2 * i + s) * 4, 4, s, b * (4 - s) + i)
                        step(T - 2, 2, 0, b * 4 + 3)
                        a.wait_ge(self.sign_ready[0], b * 4 + 4)
                        a.sem_inc(self.row_used[r], 1)
                    self.each_block(a, body)

            def scale(self, eng, who, h, slot, first, last, before):
                HC, steps = self.HC, self.scale_steps[who]
                f = self.scaled[who].rearrange("p (k c x) -> p k c x", k=2, c=2)
                with eng.Fori(first, last) as i:
                    done = before + (i - first) * 5
                    vals = V[:, at(2 * i * VW, 2 * VW)].rearrange("p (c n) -> p c n", c=2)[:, :, h * HC:(h + 1) * HC]
                    out_ = self.parts[slot][:, at(2 * i * 2 * self.KW, 4 * self.KW)].rearrange(
                        "p (c k g x) -> p k c g x", c=2, k=2, g=3)
                    for kind, e in enumerate((self.exp_sj, d_all)):
                        last_ = eng.tensor_tensor(f[:, kind, :, :], vals,
                                                  e[:, at(h * T + 2 * i, 2)].rearrange("p (c o) -> p c o", o=1)
                                                  .to_broadcast([P, 2, HC]), ALU.mult)
                    last_.then_inc(steps, 1)
                    eng.wait_ge(steps, done + 1)
                    for g in range(2):
                        eng.tensor_copy(out_[:, :, :, g, :], f).then_inc(steps, 1)
                        eng.wait_ge(steps, done + 2 * g + 2)
                        if who == 0:
                            eng.sem_inc(self.waited["pool"], 1)
                        sub_out = f if g == 0 else out_[:, :, :, 2, :]
                        eng.tensor_tensor(sub_out, f, out_[:, :, :, g, :], ALU.subtract).then_inc(steps, 1)
                        eng.wait_ge(steps, done + 2 * g + 3)

            def scale_gpsimd(self, pool):
                n = PAIRS - self.FIRST
                for h in range(self.H):
                    if h == 0:
                        pool.wait_ge(self.exp_ready, 2)
                    if h >= 2:
                        pool.wait_ge(self.parts_used[h % 2], h // 2)
                    before = 0 if h == 0 else 5 * (n + (h - 1) * PAIRS)
                    self.scale(pool, 0, h, h % 2, self.FIRST if h == 0 else 0, PAIRS, before)
                    total = 5 * (n + h * PAIRS)
                    pool.wait_ge(self.scale_steps[0], total)
                    pool.sem_inc(self.parts_ready[h % 2], 1)

            def split_vector(self, v):
                H, W, NT, HC = self.H, self.W, self.NT, self.HC
                v.wait_ge(self.exp_ready, 2)
                self.scale(v, 1, 0, 0, 0, self.FIRST, 0)
                v.wait_ge(self.scale_steps[1], 5 * self.FIRST)
                v.sem_inc(self.first_ready, 1)
                m32 = words(MASK_AT, MASK_WORDS).bitcast(U32)
                NW = NP // 4

                def step(b, k, c, chunks, nt, sslot, sn, slot, n_slot, nth):
                    w = nt * P // 4

                    def ring(t):
                        return t.bitcast(U32).rearrange("p (q w) -> p q w", w=W // 4)[:, 0:chunks, 0:w]
                    m = m32[:, at(c * NW, chunks * NW)].rearrange("p (q w) -> p q w", w=NW)[:, :, at(k * (W // 4), w)]
                    sg = ring(self.sign[sslot])
                    pos, neg = (ring(t) for t in self.split[slot])
                    v.wait_ge(self.sign_ready[sslot], sn + 1)
                    v.wait_ge(self.split_used[slot], n_slot + 1)
                    v.scalar_tensor_tensor(out=pos, in0=sg, scalar=1, in1=sg, op0=ALU.logical_shift_right,
                                           op1=ALU.bitwise_xor).then_inc(self.differs, 1)
                    v.tensor_tensor(neg, sg, m, ALU.bitwise_and).then_inc(self.sign_used[sslot], 1)
                    v.wait_ge(self.differs, nth + 1)
                    v.scalar_tensor_tensor(out=pos, in0=pos, scalar=3, in1=m, op0=ALU.logical_shift_left,
                                           op1=ALU.bitwise_and).then_inc(self.split_ready[slot], 1)

                def add_parts(h, k, j, r, nt):
                    base = (h * 7 + k) * 7
                    st = self.fold_steps
                    v.wait_ge(self.block_done[r], h * (4 - r) + j + 1)
                    for n in range(nt):
                        last = v.tensor_reduce(self.sums[:, n * 2 * HC:(n + 1) * 2 * HC]
                                               .rearrange("p (k x) -> p k x", k=2),
                                               bank[r * NT + n][:, 0:6 * HC]
                                               .rearrange("p (k g x) -> p k x g", k=2, g=3), AXX, ALU.add)
                    last.then_inc(st, 1)
                    v.wait_ge(st, base + 1)
                    v.sem_inc(self.bank_free[r], 1)
                    s4 = self.sums[:, 0:nt * 2 * HC].rearrange("p (n k x) -> p n k x", n=nt, k=2)
                    ac = q_cols[:, 0:2 * H * T].rearrange("p (k q) -> p q k", k=2)[:, at(h * T + k * NT, nt), :]
                    v.tensor_tensor(s4, s4, ac.rearrange("p n (k o) -> p n k o", o=1).to_broadcast([P, nt, 2, HC]),
                                    ALU.mult).then_inc(st, 1)

                def add_output(h, k, j, r, nt):
                    base = (h * 7 + k) * 7
                    st = self.fold_steps
                    s4 = self.sums[:, 0:nt * 2 * HC].rearrange("p (n k x) -> p n k x", n=nt, k=2)
                    v.wait_ge(st, base + 2)
                    v.tensor_tensor(s4[:, :, 0, :], s4[:, :, 0, :], s4[:, :, 1, :], ALU.add).then_inc(st, 1)
                    v.wait_ge(st, base + 3)
                    dn = s4[:, :, 0, HC - 1]
                    v.scalar_tensor_tensor(out=den[:, 0:nt], in0=dn, scalar=0.0, in1=dn, op0=ALU.is_equal,
                                           op1=ALU.add).then_inc(st, 1)
                    v.wait_ge(st, base + 4)
                    v.reciprocal(rden[:, 0:nt], den[:, 0:nt]).then_inc(st, 1)
                    v.wait_ge(st, base + 5)
                    o = s4[:, :, 0, 0:64]
                    v.tensor_tensor(o, o, rden[:, 0:nt].rearrange("p (n o) -> p n o", o=1)
                                    .to_broadcast([P, nt, 64]), ALU.mult).then_inc(st, 1)
                    v.wait_ge(st, base + 6)
                    xh = X[:, at(k * NT * D, nt * D)].rearrange("p (n d) -> p n d", d=D)[:, :, at(h * 64, 64)]
                    v.tensor_tensor(xh, xh, o, ALU.add).then_inc(st, 1)
                    v.wait_ge(st, base + 7)
                    v.sem_inc(self.waited["dve"], 1)

                def block_(h, k, nt, earlier_block=None):
                    b = h * 7 + k
                    for s in range(2):
                        step(b, k, 4 * s, 4, nt, s, b * (4 - s), s, b * 3, b * 7 + s)
                    if earlier_block is not None:
                        add_parts(*earlier_block)
                    for s in range(2):
                        step(b, k, 8 + 4 * s, 4, nt, s, b * (4 - s) + 1, s, b * 3 + 1, b * 7 + 2 + s)
                    if earlier_block is not None:
                        add_output(*earlier_block)
                    for s in range(2):
                        step(b, k, 16 + 4 * s, 4, nt, s, b * (4 - s) + 2, s, b * 3 + 2, b * 7 + 4 + s)
                    step(b, k, T - 2, 2, nt, 0, b * 4 + 3, 2, b, b * 7 + 6)

                with v.Fori(0, H // 2) as hp:
                    for p in range(2):
                        h = 2 * hp + p
                        tail = (6, 3, 0, NT // 2)
                        block_(h, 0, NT, (h - 1, *tail) if p == 1 else None)
                        with v.Fori(0, 2) as j:
                            block_(h, 2 * j + 1, NT, (h, 2 * j, j, 0, NT))
                            block_(h, 2 * j + 2, NT, (h, 2 * j + 1, j, 1, NT))
                        block_(h, 5, NT, (h, 4, 2, 0, NT))
                        block_(h, 6, NT // 2, (h, 5, 2, 1, NT))
                        if p == 1:
                            add_parts(h, *tail)
                            add_output(h, *tail)

            def products_tensor(self, pe):
                H, W, NT, KW = self.H, self.W, self.NT, self.KW
                pe.wait_ge(self.first_ready, 1)
                with pe.Fori(0, H // 2) as hp:
                    for p in range(2):
                        h = 2 * hp + p

                        def body(j, r, nt):
                            b = h * 7 + 2 * j + r
                            pe.wait_ge(self.bank_free[r], h * (4 - r) + j + 1)
                            pe.wait_ge(self.parts_ready[p], hp + 1)
                            for n in range(nt):
                                pe.matmul(bank[r * NT + n][:, 0:2 * KW], zeros[:, 0:P], zeros[:, 0:2 * KW],
                                          start=True, stop=True)
                            for st in range(self.STEPS + 1):
                                slot, nth = (st % 2, b * 3 + st // 2) if st < self.STEPS else (2, b)
                                pe.wait_ge(self.split_ready[slot], nth + 1)
                                pe.sem_inc(self.waited["pe"], 1)
                                for q in range(4 if st < self.STEPS else 2):
                                    c = st * 4 + q
                                    for n in range(nt):
                                        for kind in range(2):
                                            last = pe.matmul(
                                                bank[r * NT + n][:, kind * KW:(kind + 1) * KW],
                                                self.split[slot][kind].bitcast(F8)[:, q * W + n * P:q * W + (n + 1) * P],
                                                self.parts[p][:, (2 * c + kind) * KW:(2 * c + kind + 1) * KW],
                                                start=False, stop=False, skip_group_check=True)
                                last.then_inc(self.split_used[slot], 1)
                            pe.matmul(bank[r * NT][:, 0:64], zeros[:, 0:P], zeros[:, 0:64],
                                      start=False, stop=False, skip_group_check=True
                                      ).then_inc(self.block_done[r], 1)
                        self.each_block(pe, body)
                        pe.wait_ge(self.block_done[0], h * 4 + 4)
                        pe.sem_inc(self.parts_used[p], 1)

        class Experts:
            def __init__(self, hidden, tag, weights_at, scratch_at, second_norm):
                self.HID, self.tag, self.second_norm = hidden, tag, second_norm
                self.HC = hidden // P
                self.HB = hidden // 512
                self.W1 = words(weights_at, E * KC * hidden)
                self.W2 = words(weights_at + E * KC * hidden, E * self.HC * D)
                b1_at = weights_at + E * KC * hidden + E * self.HC * D
                self.b1 = words(b1_at, E * hidden)
                assert b1_at + E * hidden <= ARENA
                k = scratch_at
                TE = T * E
                self.logits = words(k, TE)
                k += TE
                self.pick1 = words(k, TE)
                k += TE
                self.pick2 = words(k, TE)
                k += TE
                self.work = words(k, TE)
                k += TE
                self.posx = words(k, TE)
                k += TE
                self.incl = words(k, TE)
                k += TE
                self.routed = words(k, TE // 2).bitcast(BF16)
                k += TE // 2
                self.top1 = words(k, T)
                k += T
                self.top2 = words(k, T)
                k += T
                self.best = words(k, T)
                k += T
                self.sums = words(k, T)
                k += T
                self.e2 = words(k, T)
                k += T
                self.gate = words(k, KC * E)
                k += KC * E
                self.gate_b = words(k, E)
                k += E
                self.used = words(k, E)
                k += E
                self.end = words(k, E)
                k += E
                self.base = words(k, E)
                k += E
                self.tile_e = words(k, SLOT_TILES)
                k += SLOT_TILES
                self.xn = [words(k + s * D, D) for s in range(2)]
                self.fills = words(k, E * T)
                self.below = words(k, SLOT_TILES * E)
                k += 2 * D
                self.xt = [words(k + s * D, D) for s in range(2)]
                self.spare = words(k, SLOT_TILES)
                k += 2 * D
                self.place_no = words(k, P)
                k += P
                self.weight_of = words(k, 2 * T)
                k += 2 * T
                self.slot_i = words(k, 2 * T).bitcast(I32)
                k += 2 * T
                self.part_i = words(k, 4 * T).bitcast(I32)
                k += 4 * T
                self.tile_of = words(k, 2 * T)
                k += 2 * T
                self.place_of = words(k, 2 * T)
                k += 2 * T
                self.shift_x = words(k, T)
                k += T
                self.scale_x = words(k, T)
                k += T
                if second_norm:
                    self.ln_g = words(k, KC * E)
                    k += KC * E
                    self.ln_b = words(k, KC * E)
                    k += KC * E
                assert k <= ARENA, (k, ARENA)
                w2_at = k = weights_at + E * KC * hidden
                if second_norm:
                    self.lnb = words(k, E * D)
                    k += E * D
                    self.one_row = words(k, P)
                    k += P
                self.hot_from = k - w2_at
                self.hot_place = [words(k + s * PAIRS * P, PAIRS * P) for s in range(2)]
                k += 2 * PAIRS * P
                self.hot_tile = [words(k + s * PAIRS * 2 * SLOT_TILES, PAIRS * 2 * SLOT_TILES) for s in range(2)]
                k += 4 * PAIRS * SLOT_TILES
                self.hot_to = k - w2_at
                assert k <= b1_at
                k = b1_at + E * hidden
                self.rx = [words(k + s * D, D) for s in range(4)]
                k += 4 * D
                self.ysum = [words(k + s * D, D) for s in range(2)]
                k += 2 * D
                assert k <= ARENA, (k, ARENA)
                k = 0

                def ring(n, size):
                    nonlocal k
                    got = [X[:, k + s * size:k + (s + 1) * size] for s in range(n)]
                    k += n * size
                    return got
                self.rxt = ring(2, D)
                self.ry = ring(2, D)
                self.ht = ring(2, hidden)
                self.hid = ring(1, hidden)[0]
                self.b2 = ring(1, E * D)[0]
                assert k <= T * D
                self.loaded = sem(tag + "loaded")
                self.stat = sem(tag + "stat")
                self.aggr = sem(tag + "aggr")
                self.var_ready = sem(tag + "var_ready")
                self.sd_ready = sem(tag + "sd_ready")
                self.rstd_ready = sem(tag + "rstd_ready")
                self.x_spilled = sem(tag + "x_spilled")
                self.lg_done = sem(tag + "lg_done")
                self.route = sem(tag + "route")
                self.exps = sem(tag + "exps")
                self.picked = sem(tag + "picked")
                self.cnt_done = sem(tag + "cnt_done")
                self.tiles_known = sem(tag + "tiles_known")
                self.hot_ready = [sem(f"{tag}hot_ready{s}") for s in range(2)]
                self.hot_used = [sem(f"{tag}hot_used{s}") for s in range(2)]
                self.places_ready = sem(tag + "places_ready")
                self.xn_stored = sem(tag + "xn_stored")
                self.ysum_ready = sem(tag + "ysum_ready")
                self.w_loaded = sem(tag + "w_loaded")
                self.b_loaded = sem(tag + "b_loaded")
                self.fold_used = sem(tag + "fold_used")
                self.fold_mm = sem(tag + "fold_mm")
                self.lnb_ready = sem(tag + "lnb_ready")
                self.w2_loaded = sem(tag + "w2_loaded")
                self.x_scaled = sem(tag + "x_scaled")
                self.scales_ready = sem(tag + "scales_ready")
                self.lng_loaded = sem(tag + "lng_loaded")
                self.hid_ready = sem(tag + "hid_ready")
                self.x_back = sem(tag + "x_back")
                self.xn_ready = [sem(f"{tag}xn_ready{s}") for s in range(2)]
                self.tp_ready = [sem(f"{tag}tp_ready{s}") for s in range(2)]
                self.xt_ready = [sem(f"{tag}xt_ready{s}") for s in range(2)]
                self.rx_loaded = [sem(f"{tag}rx_loaded{s}") for s in range(4)]
                self.tx_ready = [sem(f"{tag}tx_ready{s}") for s in range(2)]
                self.xgt_ready = [sem(f"{tag}xgt_ready{s}") for s in range(2)]
                self.h_ready = [sem(f"{tag}h_ready{s}") for s in range(2)]
                self.th_ready = [sem(f"{tag}th_ready{s}") for s in range(2)]
                self.ht_ready = [sem(f"{tag}ht_ready{s}") for s in range(2)]
                self.y_ready = [sem(f"{tag}y_ready{s}") for s in range(2)]
                self.ry_ready = [sem(f"{tag}ry_ready{s}") for s in range(2)]
                self.added = sem(tag + "added")
                self.ry_free = [sem(f"{tag}ry_free{s}") for s in range(2)]
                start_at_one.extend(self.tp_ready + self.xt_ready + self.xn_ready + self.tx_ready + self.th_ready
                                    + self.h_ready + self.ht_ready + self.y_ready + self.ry_ready + self.ry_free
                                    + self.hot_used)

            def route_sync(self, sp, gate_w, gate_b, w1m, w2m, total, ln):
                sp.dma_start(self.gate.rearrange("p (k e) -> p k e", e=E),
                             gate_w.rearrange("(k p) e -> p k e", p=P)).then_inc(self.loaded, 16)
                sp.dma_start(self.gate_b, gate_b.partition_broadcast(P)).then_inc(self.loaded, 16)
                if self.second_norm:
                    ln_gm, ln_bm, b1m = ln
                    sp.dma_start(self.ln_g, ln_gm).then_inc(self.lng_loaded, 16)
                    sp.dma_start(self.ln_b, ln_bm).then_inc(self.lng_loaded, 16)
                    sp.dma_start(self.b1[0:1, :], b1m.rearrange("(o n) -> o n", o=1)).then_inc(self.lng_loaded, 16)
                    sp.dma_start(total[0:NP, :].rearrange("(t p) d -> p t d", p=P),
                                 X[:, :].rearrange("p (t d) -> p t d", d=D)).then_inc(self.x_spilled, 16)
                    sp.wait_ge(self.x_spilled, 16)
                for g in range(4):
                    n = w1m.shape[1] // 4
                    sp.dma_start(self.W1[:, g * n:(g + 1) * n], w1m[:, g * n:(g + 1) * n]).then_inc(self.w_loaded, 16)
                n = w2m.shape[1] // 8
                after_fold = [g for g in range(8) if g * n < self.hot_from]
                after_hot = [g for g in range(8) if self.hot_from <= g * n < self.hot_to]

                def load_w2(parts):
                    for g in parts:
                        sp.dma_start(self.W2[:, g * n:(g + 1) * n], w2m[:, g * n:(g + 1) * n]
                                     ).then_inc(self.w2_loaded, 16)
                load_w2([g for g in range(8) if g * n >= self.hot_to])
                for g in range(2):
                    sp.wait_ge(self.x_scaled, (g + 1) * PAIRS)
                    sp.dma_start(xs[g * PAIRS * P:(g + 1) * PAIRS * P, :].rearrange("(t p) d -> p t d", p=P),
                                 X[:, g * PAIRS * D:(g + 1) * PAIRS * D].rearrange("p (t d) -> p t d", d=D)
                                 ).then_inc(self.xn_stored, 16)
                for s in range(2):
                    sp.wait_ge(self.hot_used[s], 3)
                load_w2(after_hot)
                if self.second_norm:
                    sp.wait_ge(self.fold_mm, E)
                load_w2(after_fold)
                sp.wait_ge(self.xn_stored, 32)

            def route_vector(self, v):
                layer_norm_stats(v, self)
                r = self.route
                n = [0]

                def step(ins):
                    n[0] += 1
                    ins.then_inc(r, 1)
                    v.wait_ge(r, n[0])

                with v.Fori(0, PAIRS) as i:
                    for s in range(2):
                        t = 2 * i + s
                        v.wait_ge(self.tp_ready[s], i + 1)
                        v.tensor_scalar(self.xn[s], X[:, at(t * D, D)], mv[:, at(t, 1)], rstd[:, at(t, 1)],
                                        ALU.subtract, ALU.mult).then_inc(self.xn_ready[s], 1)
                scale = rstd[:, :]
                if self.second_norm:
                    var = mv[:, 2 * T:3 * T]
                    step(v.tensor_tensor(self.scale_x, var, rstd[:, :], ALU.mult))
                    step(v.tensor_tensor(self.scale_x, self.scale_x, rstd[:, :], ALU.mult))
                    v.tensor_scalar(self.scale_x, self.scale_x, EPS, None, ALU.add).then_inc(self.var_ready, 1)
                    v.wait_ge(self.sd_ready, 2)
                    step(v.reciprocal(self.scale_x, self.scale_x))
                    scale = self.scale_x
                    step(v.tensor_tensor(self.scale_x, self.scale_x, rstd[:, :], ALU.mult))
                else:
                    v.tensor_copy(self.scale_x, rstd[:, :])
                v.scalar_tensor_tensor(out=self.shift_x, in0=mv[:, 0:T], scalar=-1.0, in1=scale, op0=ALU.mult,
                                       op1=ALU.mult).then_inc(self.scales_ready, 1)
                TE = T * E
                lg3 = self.logits.rearrange("p (t e) -> p t e", e=E)
                w3 = self.work.rearrange("p (t e) -> p t e", e=E)
                def spread(a):
                    return a.rearrange("p (t o) -> p t o", o=1).to_broadcast([P, T, E])

                def spread_t(a):
                    return a.rearrange("p (o e) -> p o e", o=1).to_broadcast([P, T, E])

                v.wait_ge(self.lg_done, T)
                v.wait_ge(self.loaded, 32)
                step(v.tensor_tensor(lg3, bank[2][:, 0:TE].rearrange("p (t e) -> p t e", e=E), spread_t(self.gate_b),
                                     ALU.add))
                for top, pick in ((self.top1, self.pick1), (self.top2, self.pick2)):
                    p3 = pick.rearrange("p (t e) -> p t e", e=E)
                    step(v.tensor_reduce(top, lg3, AXX, ALU.max))
                    step(v.tensor_tensor(w3, lg3, spread(top), ALU.is_equal))
                    step(v.tensor_tensor(w3, w3, spread_t(order8[:, :]), ALU.mult))
                    step(v.tensor_reduce(self.best, w3, AXX, ALU.max))
                    step(v.tensor_tensor(p3, w3, spread(self.best), ALU.is_equal))
                    if top is self.top1:
                        step(v.tensor_tensor(w3, lg3, spread(top), ALU.subtract))
                        v.tensor_copy(self.posx, self.work).then_inc(self.picked, 1)
                        step(v.scalar_tensor_tensor(out=self.logits, in0=pick, scalar=-3.0e38, in1=self.logits,
                                                    op0=ALU.mult, op1=ALU.add))
                v.tensor_tensor(self.e2, self.top2, self.top1, ALU.subtract).then_inc(self.picked, 1)
                v.tensor_tensor(self.routed, self.pick1, self.pick2, ALU.add).then_inc(self.picked, 1)
                v.wait_ge(self.exps, 2)
                if self.second_norm:
                    step(v.tensor_scalar(self.sums, self.e2, 1.0, None, ALU.add))
                else:
                    step(v.tensor_reduce(self.sums, self.posx.rearrange("p (t e) -> p t e", e=E), AXX, ALU.add))
                wt = self.weight_of
                step(v.reciprocal(wt[:, 0:T], self.sums))
                step(v.tensor_tensor(wt[:, T:2 * T], self.e2, wt[:, 0:T], ALU.mult))
                v.wait_ge(self.cnt_done, 1)
                step(v.tensor_copy(self.work, bank[4][:, 0:TE]))
                i3 = self.incl.rearrange("p (e t) -> p e t", t=T)
                for e in range(E):
                    last = v.tensor_tensor_scan(i3[:, e, :], ones_t[:, :], w3[:, :, e], 0.0, ALU.mult, ALU.add)
                step(last)
                f3 = self.fills.rearrange("p (e t) -> p e t", t=T)
                step(v.tensor_tensor(f3, i3[:, :, T - 1:T].to_broadcast([P, E, T]),
                                     fill_at[:, :].rearrange("p (o t) -> p o t", o=1).to_broadcast([P, E, T]),
                                     ALU.is_gt))
                step(v.tensor_reduce(self.used, f3, AXX, ALU.add))
                step(v.tensor_tensor_scan(self.end, ones_t[:, 0:E], self.used, 0.0, ALU.mult, ALU.add))
                step(v.tensor_tensor(self.base, self.end, self.used, ALU.subtract))
                step(v.tensor_scalar(self.base, self.base, float(P), None, ALU.mult))
                p3 = self.posx.rearrange("p (t e) -> p t e", e=E)
                step(v.tensor_tensor(p3, i3.rearrange("p e t -> p t e"), w3, ALU.subtract))
                step(v.tensor_tensor(p3, p3, spread_t(self.base), ALU.add))
                step(v.tensor_tensor(self.posx, bank[3][:, 0:TE], self.posx, ALU.add))
                for k, pick in enumerate((self.pick1, self.pick2)):
                    step(v.tensor_tensor(self.work, self.posx, pick, ALU.mult))
                    step(v.tensor_reduce(self.best, w3, AXX, ALU.add))
                    step(v.tensor_copy(self.slot_i[:, k * T:(k + 1) * T], self.best))
                step(v.tensor_scalar(self.part_i[:, 0:2 * T], self.slot_i, 7, None, ALU.logical_shift_right))
                step(v.tensor_scalar(self.part_i[:, 2 * T:4 * T], self.slot_i, P - 1, None, ALU.bitwise_and))
                step(v.tensor_copy(self.tile_of, self.part_i[:, 0:2 * T]))
                step(v.tensor_copy(self.place_of, self.part_i[:, 2 * T:4 * T]))
                G = SLOT_TILES
                v.wait_ge(self.places_ready, 1)
                for c in range(4):
                    q, b = slice(c * PAIRS, (c + 1) * PAIRS), c % 2
                    ids = row_id[:, c % 2 * PAIRS:(c % 2 + 1) * PAIRS]

                    def over(a, n):
                        return a.rearrange("p (q o) -> p q o", o=1).to_broadcast([P, PAIRS, n])
                    tiles_ = self.hot_tile[b].rearrange("p (q k g) -> p q k g", q=PAIRS, k=2)
                    v.wait_ge(self.hot_used[b], c // 2 + 1)
                    v.tensor_tensor(self.hot_place[b].rearrange("p (q m) -> p q m", m=P),
                                    self.place_no.rearrange("p (o m) -> p o m", o=1).to_broadcast([P, PAIRS, P]),
                                    over(self.place_of[:, q], P), ALU.is_equal)
                    step(v.tensor_tensor(tiles_[:, :, 1, :],
                                         tile_no[:, :].rearrange("p (o g) -> p o g", o=1)
                                         .to_broadcast([P, PAIRS, G]),
                                         over(self.tile_of[:, q], G), ALU.is_equal))
                    step(v.tensor_tensor(tiles_[:, :, 0, :], tiles_[:, :, 1, :], over(ids, G), ALU.mult))
                    v.tensor_tensor(tiles_[:, :, 1, :], tiles_[:, :, 1, :], over(wt[:, q], G), ALU.mult
                                    ).then_inc(self.hot_ready[b], 1)
                b3 = self.below.rearrange("p (g e) -> p g e", e=E)[0:1]
                step(v.tensor_tensor(b3, self.end[0:1].rearrange("p (o e) -> p o e", o=1)
                                     .to_broadcast([1, SLOT_TILES, E]),
                                     tile_no[0:1].rearrange("p (g o) -> p g o", o=1).to_broadcast([1, SLOT_TILES, E]),
                                     ALU.is_le))
                step(v.tensor_reduce(self.tile_e[0:1], b3, AXX, ALU.add))
                step(v.tensor_scalar(self.tile_e[0:1], self.tile_e[0:1], float(E - 1), None, ALU.min))
                v.tensor_copy(expert_of[:, :], self.tile_e[0:1]).then_inc(self.tiles_known, 1)
                for k in range(2):
                    v.wait_ge(self.hot_used[k], 3)
                step(v.tensor_scalar(self.spare, bank[5][:, 0:G], 0.0, spare_row[:, :],
                                     ALU.is_equal, ALU.mult))
                v.scalar_tensor_tensor(out=slot_row[:, :], in0=bank[5][:, 0:G], scalar=1.0,
                                       in1=self.spare, op0=ALU.subtract, op1=ALU.add)
                v.tensor_copy(slot_w[:, :], bank[5][:, G:2 * G])

            def route_scalar(self, a):
                layer_norm_sqrt(a, self)
                with a.Fori(0, PAIRS) as i:
                    for s in range(2):
                        a.wait_ge(self.tp_ready[s], i + 2)
                        a.copy(self.xt[s], bank[s][:, 0:D]).then_inc(self.xt_ready[s], 1)
                if self.second_norm:
                    a.wait_ge(self.var_ready, 2)
                    a.activation(self.scale_x, self.scale_x, ACT.Sqrt).then_inc(self.sd_ready, 1)
                    a.wait_ge(self.x_spilled, 16)
                a.wait_ge(self.scales_ready, 1)
                for half in range(2):
                    with a.Fori(half * PAIRS, (half + 1) * PAIRS) as t:
                        xv = X[:, at(t * D, D)]
                        a.activation(xv, xv, ACT.Identity, scale=self.scale_x[:, at(t, 1)],
                                     bias=self.shift_x[:, at(t, 1)]).then_inc(self.x_scaled, 1)
                    if half == 0:
                        a.wait_ge(self.picked, 3)
                        a.activation(self.posx, self.posx, ACT.Exp).then_inc(self.exps, 1)
                        a.activation(self.e2, self.e2, ACT.Exp).then_inc(self.exps, 1)
                if self.second_norm:
                    self.fold_scalar(a)

            def route_tensor(self, pe):
                pe.wait_ge(self.loaded, 32)

                def turn(i, s):
                    pe.wait_ge(self.xn_ready[s], i + 2)
                    pe.wait_ge(self.xt_ready[s], i + 1)
                    for k in range(KC):
                        last = pe.transpose(bank[s][:, k * P:(k + 1) * P], self.xn[s][:, k * P:(k + 1) * P],
                                            ident[:, :])
                    last.then_inc(self.tp_ready[s], 1)

                def logits_of(i, s):
                    pe.wait_ge(self.xt_ready[s], i + 2)
                    for k in range(KC):
                        last = pe.matmul(bank[2][:, at((2 * i + s) * E, E)], self.xt[s][:, k * P:(k + 1) * P],
                                         self.gate[:, k * E:(k + 1) * E], start=(k == 0), stop=(k == KC - 1))
                    last.then_inc(self.lg_done, 1)

                turn(0, 0)
                with pe.Fori(0, PAIRS - 1) as i:
                    for s in range(2):
                        turn(i + s, 1 - s)
                        logits_of(i, s)
                turn(PAIRS - 1, 1)
                for s in range(2):
                    logits_of(PAIRS - 1, s)
                if self.second_norm:
                    self.fold_tensor(pe, 0, 1)
                pe.wait_ge(self.picked, 3)
                pe.matmul(bank[3][:, 0:T * E], earlier[:, :], self.routed, start=True, stop=True)
                pe.matmul(bank[4][:, 0:T * E], ones[:, :], self.routed, start=True, stop=True
                          ).then_inc(self.cnt_done, 1)
                if self.second_norm:
                    self.fold_tensor(pe, 1, 3)
                pe.matmul(bank[5][:, 0:2 * SLOT_TILES], zeros[:, 0:P], zeros[:, 0:2 * SLOT_TILES],
                          start=True, stop=True)
                for c in range(4):
                    pe.wait_ge(self.hot_ready[c % 2], c // 2 + 1)
                    for q in range(PAIRS):
                        last = pe.matmul(bank[5][:, 0:2 * SLOT_TILES],
                                         self.hot_place[c % 2][:, q * P:(q + 1) * P],
                                         self.hot_tile[c % 2][:, q * 2 * SLOT_TILES:(q + 1) * 2 * SLOT_TILES],
                                         start=False, stop=False, skip_group_check=True)
                    last.then_inc(self.hot_used[c % 2], 1)
                if self.second_norm:
                    self.fold_tensor(pe, 3, E)

            def route_gpsimd(self, pool):
                pool.iota(self.place_no, [[1, P]], base=0, channel_multiplier=0,
                          allow_small_or_imprecise_dtypes=True).then_inc(self.places_ready, 1)
                if self.second_norm:
                    pool.memset(self.one_row[0:1, :], 1.0).then_inc(self.lnb_ready, 1)
                    pool.wait_ge(self.lng_loaded, 48)
                    for c in range(E * KC):
                        pool.tensor_copy(self.lnb[:, c * P:(c + 1) * P], self.ln_b[:, c:c + 1].to_broadcast([P, P])
                                         ).then_inc(self.lnb_ready, 1)

            def tiles_sync(self, sp, b1m, b2m):
                if not self.second_norm:
                    sp.dma_start(self.b1, b1m.partition_broadcast(P)).then_inc(self.b_loaded, 16)
                sp.dma_start(self.b2, b2m.partition_broadcast(P)).then_inc(self.b_loaded, 16)

            def tiles_gpsimd(self, pool, total):
                def gather(g):
                    pool.indirect_dma_start(self.rx[g % 4], None, xs[:, :],
                                            bass.IndirectOffsetOnAxis(ap=slot_row[:, g:g + 1], axis=0)
                                            ).then_inc(self.rx_loaded[g % 4], 16)
                for g in range(4):
                    gather(g)
                for g in range(RUN_TILES):
                    if g + 4 < SLOT_TILES:
                        pool.wait_ge(self.tx_ready[g % 2], g // 2 + 2)
                        gather(g + 4)
                    pool.wait_ge(self.ry_ready[g % 2], g // 2 + 2)
                    if g > 0:
                        pool.wait_ge(self.added, 16 * g)
                        pool.sem_inc(self.ry_free[(g - 1) % 2], 1)
                    pool.indirect_dma_start(total[:, :],
                                            bass.IndirectOffsetOnAxis(ap=slot_row[:, g:g + 1], axis=0),
                                            self.ry[g % 2], None, compute_op=ALU.add).then_inc(self.added, 16)
                pool.wait_ge(self.added, 16 * RUN_TILES)

            def tiles_tensor(self, pe):
                HID, HC = self.HID, self.HC

                def hidden(e, s):
                    for b in range(self.HB):
                        for k in range(KC):
                            last = pe.matmul(bank[b][:, :], self.rxt[s][:, k * P:(k + 1) * P],
                                             self.W1[:, at(e * (KC * HID) + k * HID + b * 512, 512)],
                                             start=(k == 0), stop=(k == KC - 1))
                    last.then_inc(self.h_ready[s], 1)

                def turn_x(q):
                    for k in range(KC):
                        last = pe.transpose(bank[4][:, k * P:(k + 1) * P], self.rx[q][:, k * P:(k + 1) * P],
                                            ident[:, :])
                    last.then_inc(self.tx_ready[q % 2], 1)

                pe.wait_ge(self.w_loaded, 16 * 4)
                pe.wait_ge(self.rx_loaded[0], 16)
                turn_x(0)
                pe.wait_ge(self.rx_loaded[1], 16)
                pe.wait_ge(self.xgt_ready[0], 1)
                turn_x(1)
                e0 = pe.value_load(expert_of[0:1, 0:1], min_val=0, max_val=E - 1)
                hidden(e0, 0)
                pe.wait_ge(self.w2_loaded, 16 * 8)
                with pe.Fori(0, RUN_TILES // 4) as j:
                    for q in range(4):
                        i, s = 2 * j + q // 2, q % 2
                        o = 1 - s
                        g = 4 * j + q
                        pe.wait_ge(self.hid_ready, g + 1)
                        pe.wait_ge(self.ht_ready[o], i + 1 + s)
                        for c in range(HC):
                            last = pe.transpose(bank[2 + c // 4][:, c % 4 * P:(c % 4 + 1) * P],
                                                self.hid[:, c * P:(c + 1) * P], ident[:, :])
                        last.then_inc(self.th_ready[s], 1)
                        pe.wait_ge(self.rx_loaded[(q + 2) % 4], 16 * (j + 1 + (q >= 2)))
                        pe.wait_ge(self.xgt_ready[o], i + 1 + s)
                        turn_x((q + 2) % 4)
                        e = pe.value_load(expert_of[0:1, at(g + 1, 1)], min_val=0, max_val=E - 1)
                        hidden(e, o)
                        e = pe.value_load(expert_of[0:1, at(g, 1)], min_val=0, max_val=E - 1)
                        pe.wait_ge(self.ht_ready[s], i + 2)
                        pe.wait_ge(self.ry_ready[s], i + 1)
                        for c in range(HC):
                            last = pe.matmul(bank[5 + s][:, 0:D], self.ht[s][:, c * P:(c + 1) * P],
                                             self.W2[:, at(e * (HC * D) + c * D, D)],
                                             start=(c == 0), stop=(c == HC - 1))
                        last.then_inc(self.y_ready[s], 1)

            def tiles_scalar(self, a):
                for s in range(2):
                    a.wait_ge(self.tx_ready[s], 2)
                    a.copy(self.rxt[s], bank[4][:, 0:D]).then_inc(self.xgt_ready[s], 1)
                with a.Fori(0, RUN_TILES // 2) as i:
                    for s in range(2):
                        a.wait_ge(self.th_ready[s], i + 2)
                        a.wait_ge(self.y_ready[s], i + 1)
                        for b in range(self.HB):
                            last = a.activation(self.ht[s][:, b * 512:(b + 1) * 512], bank[2 + b][:, :], ACT.Gelu)
                        last.then_inc(self.ht_ready[s], 1)
                        a.wait_ge(self.tx_ready[s], i + 3)
                        a.wait_ge(self.h_ready[s], i + 2)
                        a.copy(self.rxt[s], bank[4][:, 0:D]).then_inc(self.xgt_ready[s], 1)

            def tiles_vector(self, v):
                HID = self.HID

                def add_bias(e, s, use):
                    v.wait_ge(self.h_ready[s], use + 2)
                    for b in range(self.HB):
                        last = v.tensor_tensor(self.hid[:, b * 512:(b + 1) * 512], bank[b][:, :],
                                               self.b1[:, at(e * HID + b * 512, 512)], ALU.add)
                    last.then_inc(self.hid_ready, 1)

                v.wait_ge(self.b_loaded, 16 if self.second_norm else 32)
                e0 = v.value_load(expert_of[0:1, 0:1], min_val=0, max_val=E - 1)
                add_bias(e0, 0, 0)
                with v.Fori(0, RUN_TILES // 2) as i:
                    for s in range(2):
                        o = 1 - s
                        g = 2 * i + s
                        e = v.value_load(expert_of[0:1, at(g + 1, 1)], min_val=0, max_val=E - 1)
                        v.wait_ge(self.th_ready[s], i + 2)
                        add_bias(e, o, i + s)
                        e = v.value_load(expert_of[0:1, at(g, 1)], min_val=0, max_val=E - 1)
                        v.wait_ge(self.y_ready[s], i + 2)
                        v.wait_ge(self.ry_free[s], i + 1)
                        v.tensor_tensor(self.ysum[s], bank[5 + s][:, 0:D], self.b2[:, at(e * D, D)], ALU.add
                                        ).then_inc(self.ysum_ready, 1)
                        v.wait_ge(self.ysum_ready, g + 1)
                        v.tensor_scalar(self.ry[s], self.ysum[s], slot_w[:, at(g, 1)], None, ALU.mult
                                        ).then_inc(self.ry_ready[s], 1)

            def fold_bank(self, e, b):
                return bank[(6, 0)[e % 2] + b][:, :]

            def fold_tensor(self, pe, first, last):
                HID = self.HID
                pe.wait_ge(self.w_loaded, 16 * 4)
                pe.wait_ge(self.lnb_ready, E * KC + 1)
                for e in range(first, last):
                    if e >= 2:
                        pe.wait_ge(self.fold_used, e - 1)
                    for b in range(self.HB):
                        to = self.fold_bank(e, b)
                        pe.matmul(to, self.one_row[0:1, :], self.b1[0:1, at(e * HID + b * 512, 512)],
                                  start=True, stop=False)
                        for k in range(KC):
                            done = pe.matmul(to, self.lnb[:, e * D + k * P:e * D + (k + 1) * P],
                                             self.W1[:, at(e * (KC * HID) + k * HID + b * 512, 512)],
                                             start=False, stop=(k == KC - 1))
                    done.then_inc(self.fold_mm, 1)

            def fold_scalar(self, a):
                HID = self.HID
                with a.Fori(0, E // 2) as i:
                    for s in range(2):
                        e = 2 * i + s
                        a.wait_ge(self.fold_mm, e + 1)
                        for b in range(self.HB):
                            last = a.copy(self.b1[:, at(e * HID + b * 512, 512)], self.fold_bank(s, b))
                        last.then_inc(self.fold_used, 1)
                        for k in range(KC):
                            wv = self.W1[:, at(e * (KC * HID) + k * HID, HID)]
                            a.activation(wv, wv, ACT.Identity, scale=self.ln_g[:, at(e * KC + k, 1)])

            def back_sync(self, sp):
                sp.dma_start(X[:, :].rearrange("p (t d) -> p t d", d=D), xd[0:NP, :].rearrange("(t p) d -> p t d", p=P)
                             ).then_inc(self.x_back, 16)
                sp.wait_ge(self.x_back, 16)

        def layer_norm_stats(v, sems, nth=1):
            with v.Fori(0, 2) as half:
                for q in range(PAIRS):
                    t = half * PAIRS + q
                    v.bn_stats(stats[:, at(t * 6, 6)], X[:, at(t * D, D)]).then_inc(sems.stat, 1)
            v.wait_ge(sems.stat, T * nth)
            st = stats[:, :].rearrange("p (t k) -> p t k", k=6)
            half_sum, half_diff, m2 = mv[:, 0:T], mv[:, T:2 * T], mv[:, 2 * T:3 * T]
            v.tensor_tensor(half_sum, st[:, :, 1], st[:, :, 4], ALU.add).then_inc(sems.aggr, 1)
            v.tensor_tensor(half_diff, st[:, :, 1], st[:, :, 4], ALU.subtract).then_inc(sems.aggr, 1)
            v.tensor_tensor(m2, st[:, :, 2], st[:, :, 5], ALU.add).then_inc(sems.aggr, 1)
            v.wait_ge(sems.aggr, 6 * nth - 3)
            v.tensor_scalar(half_sum, half_sum, 0.5, None, ALU.mult).then_inc(sems.aggr, 1)
            v.scalar_tensor_tensor(out=half_diff, in0=half_diff, scalar=0.25, in1=half_diff, op0=ALU.mult,
                                   op1=ALU.mult).then_inc(sems.aggr, 1)
            v.wait_ge(sems.aggr, 6 * nth - 1)
            v.scalar_tensor_tensor(out=m2, in0=m2, scalar=1.0 / D, in1=half_diff, op0=ALU.mult, op1=ALU.add
                                   ).then_inc(sems.aggr, 1)
            v.wait_ge(sems.aggr, 6 * nth)
            v.tensor_scalar(rstd[:, :], m2, EPS, None, ALU.add).then_inc(sems.var_ready, 1)
            v.wait_ge(sems.sd_ready, nth)
            v.reciprocal(rstd[:, :], rstd[:, :]).then_inc(sems.rstd_ready, 1)
            v.wait_ge(sems.rstd_ready, nth)

        def layer_norm_sqrt(a, sems, nth=1):
            a.wait_ge(sems.var_ready, nth)
            a.activation(rstd[:, :], rstd[:, :], ACT.Sqrt).then_inc(sems.sd_ready, 1)

        hand_over()
        A0 = Attention(L0, "a0_")
        a0_sems, a0_ones = hand_over()

        def give_ones(eng, sems):
            for free in sems:
                eng.sem_inc(free, 1)

        with nc.Block() as block:
            @block.sync
            def _(sp):
                loads_sync(sp)
                give_ones(sp, a0_ones[0::2])

            @block.tensor
            def _(pe):
                give_ones(pe, a0_ones[1::2])

            @block.gpsimd
            def _(pool):
                constants_gpsimd(pool)

        with nc.Block() as block:
            @block.sync
            def _(sp):
                A0.values_sync(sp)
                A0.rows_sync(sp)

            @block.gpsimd
            def _(pool):
                mask_loads_gpsimd(pool)
                A0.bins_gpsimd(pool)

            @block.vector
            def _(v):
                v.wait_ge(x_loaded, 32)
                A0.values_vector(v)
                A0.bins_vector(v)
                A0.count_vector(v)
                A0.rows_vector(v)

            @block.scalar
            def _(a):
                A0.values_scalar(a)
                A0.count_scalar(a)
                A0.rows_scalar(a)

            @block.tensor
            def _(pe):
                A0.values_tensor(pe)
                A0.count_tensor(pe)
                A0.rows_tensor(pe)

        X0 = Experts(512, "x0_", V_AT, 38016, False)
        x0_sems, x0_ones = hand_over()

        with nc.Block() as block:
            @block.sync
            def _(sp):
                A0.attend_sync(sp)
                give_ones(sp, x0_ones)
                for t in (xs, xd, out):
                    sp.dma_start(t[NP:NP + P, :], zeros[:, :].bitcast(F32)).then_inc(spare_clean, 16)
                A0.gelu_sync(sp)
                sp.wait_ge(spare_clean, 48)

            @block.vector
            def _(v):
                A0.single_vector(v)
                A0.gelu_vector(v)

            @block.scalar
            def _(a):
                A0.single_scalar(a)
                A0.gelu_scalar(a)

            @block.tensor
            def _(pe):
                A0.single_tensor(pe)

        nc.clear_and_free_semaphores(a0_sems)

        def experts_blocks(X_, total, next_ones, gate_w, gate_b, w1m, b1m, w2m, b2m, ln=None):
            with nc.Block() as block:
                @block.sync
                def _(sp):
                    X_.route_sync(sp, gate_w, gate_b, w1m, w2m, total, ln)

                @block.gpsimd
                def _(pool):
                    X_.route_gpsimd(pool)

                @block.vector
                def _(v):
                    X_.route_vector(v)

                @block.scalar
                def _(a):
                    X_.route_scalar(a)

                @block.tensor
                def _(pe):
                    X_.route_tensor(pe)

            with nc.Block() as block:
                @block.sync
                def _(sp):
                    give_ones(sp, next_ones)
                    X_.tiles_sync(sp, b1m, b2m)

                @block.gpsimd
                def _(pool):
                    X_.tiles_gpsimd(pool, total)

                @block.vector
                def _(v):
                    X_.tiles_vector(v)

                @block.scalar
                def _(a):
                    X_.tiles_scalar(a)

                @block.tensor
                def _(pe):
                    X_.tiles_tensor(pe)

        A1 = Attention(L1, "a1_")
        a1_sems, a1_ones = hand_over()
        a1_sems = [s for s in a1_sems if s not in A1.before_attend]
        experts_blocks(X0, xd, a1_ones, gate0, gate_b0, m0w1, m0b1, m0w2, m0b2)

        with nc.Block() as block:
            @block.sync
            def _(sp):
                X0.back_sync(sp)

            @block.vector
            def _(v):
                m32 = words(MASK_AT, MASK_WORDS).bitcast(U32)
                v.tensor_scalar(m32, m32, 3, None, ALU.logical_shift_left)

        nc.clear_and_free_semaphores(x0_sems)
        nc.all_engine_barrier()
        Q1 = Signed(A1, "q1_")
        q1_sems, q1_ones = hand_over()
        with nc.Block() as block:
            @block.sync
            def _(sp):
                give_ones(sp, q1_ones)
                A1.values_sync(sp)
                A1.rows_sync(sp)

            @block.gpsimd
            def _(pool):
                A1.bins_gpsimd(pool)

            @block.vector
            def _(v):
                A1.values_vector(v)
                A1.bins_vector(v)
                A1.count_vector(v)
                A1.rows_vector(v)

            @block.scalar
            def _(a):
                A1.values_scalar(a)
                A1.count_scalar(a)
                A1.rows_scalar(a)

            @block.tensor
            def _(pe):
                A1.values_tensor(pe)
                A1.count_tensor(pe)
                A1.rows_tensor(pe)

        nc.clear_and_free_semaphores(A1.before_attend)
        nc.all_engine_barrier()
        X1 = Experts(1024, "x1_", 0, 40960, True)
        x1_sems, x1_ones = hand_over()

        with nc.Block() as block:
            @block.sync
            def _(sp):
                with sp.If(sp.value_load(is_far[0:1, 0:1], min_val=0, max_val=1) > 0):
                    A1.attend_sync(sp)
                with sp.Else():
                    Q1.row_sync(sp)
                give_ones(sp, x1_ones)

            @block.gpsimd
            def _(pool):
                with pool.If(pool.value_load(is_far[0:1, 0:1], min_val=0, max_val=1) < 1):
                    Q1.scale_gpsimd(pool)

            @block.vector
            def _(v):
                with v.If(v.value_load(is_far[0:1, 0:1], min_val=0, max_val=1) > 0):
                    A1.attend_vector(v)
                with v.Else():
                    Q1.split_vector(v)

            @block.scalar
            def _(a):
                with a.If(a.value_load(is_far[0:1, 0:1], min_val=0, max_val=1) > 0):
                    A1.attend_scalar(a)
                with a.Else():
                    Q1.sign_scalar(a)

            @block.tensor
            def _(pe):
                with pe.If(pe.value_load(is_far[0:1, 0:1], min_val=0, max_val=1) > 0):
                    A1.attend_tensor(pe)
                with pe.Else():
                    Q1.products_tensor(pe)

        nc.clear_and_free_semaphores(a1_sems + q1_sems)
        experts_blocks(X1, out, [], gate1, gate_b1, m1w1, m1b1, m1w2, m1b2, (ln_g1, ln_b1, m1b1))


def kernel(x, adj, L0_gnn_W, L0_gnn_r, L0_ffn_gate_w, L0_ffn_gate_b, L0_ffn_W1, L0_ffn_b1, L0_ffn_W2, L0_ffn_b2,
           L1_gnn_weight, L1_gnn_weight_u, L1_gnn_weight_v, L1_gnn_bias, L1_gnn_proj_w, L1_gnn_proj_b,
           L1_ffn_Wr, L1_ffn_br, L1_ffn_ln_g, L1_ffn_ln_b, L1_ffn_W1, L1_ffn_b1, L1_ffn_W2, L1_ffn_b2):
    import numpy as np
    import concourse.bacc as bacc
    from concourse.bass_utils import run_bass_kernel_spmd as run

    x = np.asarray(x)
    xp = np.zeros((NP, D), x.dtype)
    xp[:NODES] = x
    adjT = np.zeros((NP, NP), np.int32)
    adjT[:NODES, :NODES] = np.asarray(adj).T
    for n in range(NODES, NP):
        adjT[n, n] = 1
    w0 = np.asarray(L0_gnn_W)
    r0 = np.asarray(L0_gnn_r).reshape(2, D)
    w1 = np.asarray(L1_gnn_weight)
    uv = np.zeros((D, 8), w1.dtype)
    for h in range(4):
        uv[h * 64:(h + 1) * 64, h] = np.asarray(L1_gnn_weight_u)[h, :, 0]
        uv[h * 64:(h + 1) * 64, 4 + h] = np.asarray(L1_gnn_weight_v)[h, :, 0]
    arrays = {
        "x_in": xp, "adjT": adjT, "w0T": w0.T, "w0": w0, "r0": r0[::-1].T,
        "w1": w1, "w1T": w1.T, "uv1": uv, "proj_wT": np.asarray(L1_gnn_proj_w).T,
        "bias1": np.asarray(L1_gnn_bias).reshape(D), "proj_b1": np.asarray(L1_gnn_proj_b).reshape(D),
    }

    def up(w):
        w = np.asarray(w)
        return w.reshape(E, KC, P, -1).transpose(2, 0, 1, 3).reshape(P, -1)

    def down(w):
        w = np.asarray(w)
        return w.reshape(E, -1, P, D).transpose(2, 0, 1, 3).reshape(P, -1)

    def cols(w):
        return np.asarray(w).reshape(E, KC, P).transpose(2, 0, 1).reshape(P, -1)

    arrays.update({
        "gate0": np.asarray(L0_ffn_gate_w), "gate_b0": np.asarray(L0_ffn_gate_b),
        "m0w1": up(L0_ffn_W1), "m0b1": np.asarray(L0_ffn_b1).reshape(-1),
        "m0w2": down(L0_ffn_W2), "m0b2": np.asarray(L0_ffn_b2).reshape(-1),
        "gate1": np.asarray(L1_ffn_Wr), "gate_b1": np.asarray(L1_ffn_br),
        "ln_g1": cols(L1_ffn_ln_g), "ln_b1": cols(L1_ffn_ln_b),
        "m1w1": up(L1_ffn_W1), "m1b1": np.asarray(L1_ffn_b1).reshape(-1),
        "m1w2": down(L1_ffn_W2), "m1b2": np.asarray(L1_ffn_b2).reshape(-1),
    })
    arrays = {k: np.ascontiguousarray(a) for k, a in arrays.items()}
    nc = bacc.Bacc("TRN2", target_bir_lowering=False, num_devices=1)
    args = {k: nc.dram_tensor(k, a.shape, mybir.dt.from_np(a.dtype), kind="ExternalInput").ap()
            for k, a in arrays.items()}
    out = nc.dram_tensor("out", (NP + P, D), F32, kind="ExternalOutput").ap()
    qd = nc.dram_tensor("qd", (3 * 4 * T, P), F32, kind="Internal").ap()
    xd = nc.dram_tensor("xd", (NP + P, D), F32, kind="Internal").ap()
    xs = nc.dram_tensor("xs", (NP + P, D), F32, kind="Internal").ap()
    program(nc, out=out, qd=qd, xd=xd, xs=xs, **args)
    r = run(nc, [arrays], core_ids=[0])
    return r.results[0]["out"][:NODES]
```
